# Optimizing a Trainium2 kernel written in Bass

```python
import numpy as np
import jax
import jax.numpy as jnp

def _softmax(x, axis=-1):
    return jax.nn.softmax(x, axis=axis)

def _gelu(x):
    return jax.nn.gelu(x, approximate=True)

def _silu(x):
    return jax.nn.silu(x)

def _sigmoid(x):
    return jax.nn.sigmoid(x)

def _layernorm(x, axis=-1, eps=1e-05):
    m = jnp.mean(x, axis=axis, keepdims=True)
    v = jnp.var(x, axis=axis, keepdims=True)
    return (x - m) / jnp.sqrt(v + eps)

def _scatter_add(tgt, idx, src, axis=0):
    return tgt.at[idx].add(src)

def _segment_sum(src, seg, n):
    return jax.ops.segment_sum(src, seg, n)
kernel_name = 'mk_gnn_ffn_d2_gnn_r32_9f5fcc'

def setup_inputs(seed: int=0):
    np.random.seed(seed)
    _w = jnp.asarray

    def _rec_inputs():
        import jax
        import jax.numpy as jnp
        _gk = jax.random.key(seed)
        x = -0.0003713 + 1 * jax.random.normal(jax.random.fold_in(_gk, 1), (3125, 256), jnp.float32)
        src = jax.random.randint(jax.random.fold_in(_gk, 2), (50000,), 0, 3125, jnp.int32)
        dst = jax.random.randint(jax.random.fold_in(_gk, 3), (50000,), 0, 3125, jnp.int32)
        _o = jnp.argsort(dst, stable=True)
        src = src[_o]
        dst = dst[_o]
        edge_type_8 = jax.random.randint(jax.random.fold_in(_gk, 13), (50000,), 0, 8, jnp.int32)
        edge_weight = jax.random.uniform(jax.random.fold_in(_gk, 14), (50000,), jnp.float32, 0.0, 1)
        return (x, src, dst, edge_type_8, edge_weight)
    x, src, dst, edge_type_8, edge_weight = _rec_inputs()

    def _L0_gnn_setup():
        import jax, jax.numpy as jnp
        import numpy as np
        N, IN_CH, HEADS, OUT_CH, E = (50000, 256, 4, 64, 25000)
        key = jax.random.key(seed)
        k1, k2, k3, k4, k5 = jax.random.split(key, 5)
        x = jax.random.normal(k1, (N, IN_CH), dtype=jnp.float32)
        edge_index = jax.random.randint(k2, (2, E), 0, N, dtype=jnp.int64)
        bw = float(np.sqrt(6.0 / (IN_CH + HEADS * OUT_CH)))
        ba = float(np.sqrt(6.0 / (HEADS + OUT_CH)))
        weight = jax.random.uniform(k3, (IN_CH, HEADS * OUT_CH), jnp.float32, -bw, bw)
        attn_l = jax.random.uniform(k4, (HEADS, OUT_CH), jnp.float32, -ba, ba)
        attn_r = jax.random.uniform(k5, (HEADS, OUT_CH), jnp.float32, -ba, ba)
        return {'x': x, 'edge_index': edge_index, 'weight': weight, 'attn_l': attn_l, 'attn_r': attn_r}
    _L0_gnn_all = _L0_gnn_setup()
    _L0_gnn_in = {k: v for k, v in _L0_gnn_all.items() if k in ('weight', 'attn_l', 'attn_r')}
    del _L0_gnn_all

    def _L0_ffn_setup():
        import jax, jax.numpy as jnp
        import numpy as np
        B, N, D = (16, 128, 256)
        NUM_EXPERTS, TOP_K, HEADS = (4, 2, 4)
        N_EDGES = 32768
        LN_EPS = 1e-05

        def _layernorm(x, g, b):
            mu = x.mean(-1, keepdims=True)
            var = ((x - mu) ** 2).mean(-1, keepdims=True)
            return (x - mu) * jax.lax.rsqrt(var + LN_EPS) * g + b

        def _forward(x, edge_index, W_gat, att_src, att_dst, b_gat, ln_gamma, ln_beta, W1, b1, W2, b2):
            Bc, Nc, Dc = x.shape
            M = Bc * Nc
            x_flat = x.reshape(M, Dc)
            h = (x_flat @ W_gat).reshape(M, HEADS, NUM_EXPERTS)
            loops = jnp.arange(M, dtype=edge_index.dtype)
            src = jnp.concatenate([edge_index[0], loops])
            dst = jnp.concatenate([edge_index[1], loops])
            a_src = (h * att_src).sum(-1)
            a_dst = (h * att_dst).sum(-1)
            e = jax.nn.leaky_relu(a_src[src] + a_dst[dst], negative_slope=0.2)
            e_max = jax.ops.segment_max(e, dst, num_segments=M)
            ee = jnp.exp(e - e_max[dst])
            denom = jax.ops.segment_sum(ee, dst, num_segments=M)
            alpha = ee / (denom[dst] + 1e-16)
            msg = h[src] * alpha[:, :, None]
            agg = jax.ops.segment_sum(msg, dst, num_segments=M).reshape(M, HEADS * NUM_EXPERTS) + b_gat
            scores = _layernorm(agg, ln_gamma, ln_beta).reshape(M, HEADS, NUM_EXPERTS).mean(1)
            scores = scores.reshape(Bc, Nc, NUM_EXPERTS)
            topk_s, topk_i = jax.lax.top_k(scores, TOP_K)
            w = jax.nn.softmax(topk_s, axis=-1)
            out = jnp.zeros_like(x)
            for ei in range(NUM_EXPERTS):
                g = jnp.where(topk_i == ei, w, 0.0).sum(-1)
                hh = jax.nn.gelu(x @ W1[ei] + b1[ei], approximate=False)
                out = out + g[..., None] * (hh @ W2[ei] + b2[ei])
            return out
        key = jax.random.key(seed)
        ks = jax.random.split(key, 8)
        s = 0.05
        return {'x': jax.random.normal(ks[0], (B, N, D), jnp.float32), 'W_gat': jax.random.normal(ks[1], (D, HEADS * NUM_EXPERTS), jnp.float32) * s, 'att_src': jax.random.normal(ks[2], (HEADS, NUM_EXPERTS), jnp.float32) * s, 'att_dst': jax.random.normal(ks[3], (HEADS, NUM_EXPERTS), jnp.float32) * s, 'b_gat': jnp.zeros((HEADS * NUM_EXPERTS,), jnp.float32), 'ln_gamma': jnp.ones((HEADS * NUM_EXPERTS,), jnp.float32), 'ln_beta': jnp.zeros((HEADS * NUM_EXPERTS,), jnp.float32), 'W1': jax.random.normal(ks[4], (NUM_EXPERTS, D, 2 * D), jnp.float32) * s, 'b1': jnp.zeros((NUM_EXPERTS, 2 * D), jnp.float32), 'W2': jax.random.normal(ks[5], (NUM_EXPERTS, 2 * D, D), jnp.float32) * s, 'b2': jnp.zeros((NUM_EXPERTS, D), jnp.float32), 'edge_index': jax.random.randint(ks[6], (2, N_EDGES), 0, B * N, jnp.int32)}
    _L0_ffn_all = _L0_ffn_setup()
    _L0_ffn_in = {k: v for k, v in _L0_ffn_all.items() if k in ('W_gat', 'att_src', 'att_dst', 'b_gat', 'ln_gamma', 'ln_beta', 'W1', 'b1', 'W2', 'b2', 'edge_index')}
    del _L0_ffn_all

    def _L1_gnn_setup():
        import jax, jax.numpy as jnp
        import numpy as np
        N_NODES = 1250
        N_EDGES = 20000
        IN_FEAT = 256
        OUT_FEAT = 256
        NUM_RELS = 8
        key = jax.random.key(seed)
        k = jax.random.split(key, 6)
        h = jax.random.normal(k[0], (N_NODES, IN_FEAT), dtype=jnp.float32)
        norm = jax.random.uniform(k[1], (N_EDGES,), dtype=jnp.float32)
        gain = float(np.sqrt(2.0))
        bound = gain * float(np.sqrt(6.0 / (IN_FEAT + OUT_FEAT)))
        weight = jax.random.uniform(k[2], (NUM_RELS, IN_FEAT, OUT_FEAT), dtype=jnp.float32, minval=-bound, maxval=bound)
        edge_src = jax.random.randint(k[3], (N_EDGES,), 0, N_NODES)
        edge_dst = jax.random.randint(k[4], (N_EDGES,), 0, N_NODES)
        edge_type = jax.random.randint(k[5], (N_EDGES,), 0, NUM_RELS)
        return {'h': h, 'norm': norm, 'weight': weight, 'edge_src': edge_src, 'edge_dst': edge_dst, 'edge_type': edge_type}
    _L1_gnn_all = _L1_gnn_setup()
    _L1_gnn_in = {k: v for k, v in _L1_gnn_all.items() if k in ('weight',)}
    del _L1_gnn_all

    def _L1_ffn_setup():
        import jax, jax.numpy as jnp
        import numpy as np
        TOP_K = 2
        key = jax.random.key(seed)
        ks = jax.random.split(key, 4)
        B, L, D, H, E = (8, 128, 256, 1024, 8)
        s = 0.02
        return {'x': jax.random.normal(ks[0], (B, L, D), jnp.float32), 'Wg': jax.random.normal(ks[1], (D, E), jnp.float32) * s, 'bg': jnp.zeros((E,), jnp.float32), 'W1': jax.random.normal(ks[2], (E, D, H), jnp.float32) * s, 'b1': jnp.zeros((E, H), jnp.float32), 'W2': jax.random.normal(ks[3], (E, H, D), jnp.float32) * s, 'b2': jnp.zeros((E, D), jnp.float32)}
    _L1_ffn_all = _L1_ffn_setup()
    _L1_ffn_in = {k: v for k, v in _L1_ffn_all.items() if k in ('Wg', 'bg', 'W1', 'b1', 'W2', 'b2')}
    del _L1_ffn_all
    return {'x': x, 'src': src, 'dst': dst, 'edge_type_8': edge_type_8, 'edge_weight': edge_weight, 'L0_gnn_weight': _L0_gnn_in['weight'], 'L0_gnn_attn_l': _L0_gnn_in['attn_l'], 'L0_gnn_attn_r': _L0_gnn_in['attn_r'], 'L0_ffn_W_gat': _L0_ffn_in['W_gat'], 'L0_ffn_att_src': _L0_ffn_in['att_src'], 'L0_ffn_att_dst': _L0_ffn_in['att_dst'], 'L0_ffn_b_gat': _L0_ffn_in['b_gat'], 'L0_ffn_ln_gamma': _L0_ffn_in['ln_gamma'], 'L0_ffn_ln_beta': _L0_ffn_in['ln_beta'], 'L0_ffn_W1': _L0_ffn_in['W1'], 'L0_ffn_b1': _L0_ffn_in['b1'], 'L0_ffn_W2': _L0_ffn_in['W2'], 'L0_ffn_b2': _L0_ffn_in['b2'], 'L0_ffn_edge_index': _L0_ffn_in['edge_index'], 'L1_gnn_weight': _L1_gnn_in['weight'], 'L1_ffn_Wg': _L1_ffn_in['Wg'], 'L1_ffn_bg': _L1_ffn_in['bg'], 'L1_ffn_W1': _L1_ffn_in['W1'], 'L1_ffn_b1': _L1_ffn_in['b1'], 'L1_ffn_W2': _L1_ffn_in['W2'], 'L1_ffn_b2': _L1_ffn_in['b2']}

def reference(x, src, dst, edge_type_8, edge_weight, L0_gnn_weight, L0_gnn_attn_l, L0_gnn_attn_r, L0_ffn_W_gat, L0_ffn_att_src, L0_ffn_att_dst, L0_ffn_b_gat, L0_ffn_ln_gamma, L0_ffn_ln_beta, L0_ffn_W1, L0_ffn_b1, L0_ffn_W2, L0_ffn_b2, L0_ffn_edge_index, L1_gnn_weight, L1_ffn_Wg, L1_ffn_bg, L1_ffn_W1, L1_ffn_b1, L1_ffn_W2, L1_ffn_b2):
    import jax
    import jax.numpy as jnp

    def _L0_gnn_ref(x, edge_index, weight, attn_l, attn_r):
        import jax, jax.numpy as jnp
        import numpy as np
        N, IN_CH, HEADS, OUT_CH, E = (50000, 256, 4, 64, 25000)
        heads, out_ch = attn_l.shape
        n = x.shape[0]
        xt = jnp.matmul(x, weight).reshape(-1, heads, out_ch)
        row, col = (edge_index[0], edge_index[1])
        alpha_l = jnp.einsum('ehd,hd->eh', xt[row], attn_l)
        alpha_r = jnp.einsum('ehd,hd->eh', xt[col], attn_r)
        alpha = jax.nn.softmax(jax.nn.leaky_relu(alpha_l + alpha_r, 0.01), axis=1)
        tmp = jnp.einsum('nh,nhd->nd', alpha[:n], xt[col[:n]])
        out = jnp.broadcast_to(tmp[:, None, :], (n, heads, out_ch))
        return out.reshape(n, heads * out_ch)

    def _L0_ffn_ref(x, W_gat, att_src, att_dst, b_gat, ln_gamma, ln_beta, W1, b1, W2, b2, edge_index):
        import jax, jax.numpy as jnp
        import numpy as np
        B, N, D = (16, 128, 256)
        NUM_EXPERTS, TOP_K, HEADS = (4, 2, 4)
        N_EDGES = 32768
        LN_EPS = 1e-05

        def _layernorm(x, g, b):
            mu = x.mean(-1, keepdims=True)
            var = ((x - mu) ** 2).mean(-1, keepdims=True)
            return (x - mu) * jax.lax.rsqrt(var + LN_EPS) * g + b

        def _forward(x, edge_index, W_gat, att_src, att_dst, b_gat, ln_gamma, ln_beta, W1, b1, W2, b2):
            Bc, Nc, Dc = x.shape
            M = Bc * Nc
            x_flat = x.reshape(M, Dc)
            h = (x_flat @ W_gat).reshape(M, HEADS, NUM_EXPERTS)
            loops = jnp.arange(M, dtype=edge_index.dtype)
            src = jnp.concatenate([edge_index[0], loops])
            dst = jnp.concatenate([edge_index[1], loops])
            a_src = (h * att_src).sum(-1)
            a_dst = (h * att_dst).sum(-1)
            e = jax.nn.leaky_relu(a_src[src] + a_dst[dst], negative_slope=0.2)
            e_max = jax.ops.segment_max(e, dst, num_segments=M)
            ee = jnp.exp(e - e_max[dst])
            denom = jax.ops.segment_sum(ee, dst, num_segments=M)
            alpha = ee / (denom[dst] + 1e-16)
            msg = h[src] * alpha[:, :, None]
            agg = jax.ops.segment_sum(msg, dst, num_segments=M).reshape(M, HEADS * NUM_EXPERTS) + b_gat
            scores = _layernorm(agg, ln_gamma, ln_beta).reshape(M, HEADS, NUM_EXPERTS).mean(1)
            scores = scores.reshape(Bc, Nc, NUM_EXPERTS)
            topk_s, topk_i = jax.lax.top_k(scores, TOP_K)
            w = jax.nn.softmax(topk_s, axis=-1)
            out = jnp.zeros_like(x)
            for ei in range(NUM_EXPERTS):
                g = jnp.where(topk_i == ei, w, 0.0).sum(-1)
                hh = jax.nn.gelu(x @ W1[ei] + b1[ei], approximate=False)
                out = out + g[..., None] * (hh @ W2[ei] + b2[ei])
            return out
        return _forward(x, edge_index, W_gat, att_src, att_dst, b_gat, ln_gamma, ln_beta, W1, b1, W2, b2)

    def _L1_gnn_ref(h, norm, weight, edge_src, edge_dst, edge_type):
        import jax, jax.numpy as jnp
        import numpy as np
        N_NODES = 1250
        N_EDGES = 20000
        IN_FEAT = 256
        OUT_FEAT = 256
        NUM_RELS = 8
        transformed = jnp.einsum('ni,rio->rno', h, weight)
        msg = transformed[edge_type, edge_src] * norm[:, None]
        agg = jax.ops.segment_sum(msg, edge_dst, num_segments=h.shape[0])
        return jax.nn.relu(agg)

    def _L1_ffn_ref(x, Wg, bg, W1, b1, W2, b2):
        import jax, jax.numpy as jnp
        import numpy as np
        TOP_K = 2
        B, L, D = x.shape
        E = W1.shape[0]
        xf = x.reshape(-1, D)
        gate_logits = xf @ Wg + bg
        top_w, top_i = jax.lax.top_k(gate_logits, TOP_K)
        top_w = jax.nn.softmax(top_w, axis=-1)
        w_dense = jnp.sum(jax.nn.one_hot(top_i, E, dtype=xf.dtype) * top_w[..., None], axis=1)
        out = jnp.zeros_like(xf)
        for e in range(E):
            h = jax.nn.gelu(xf @ W1[e] + b1[e], approximate=False)
            out = out + w_dense[:, e:e + 1] * (h @ W2[e] + b2[e])
        return out.reshape(B, L, D)
    edge_index = jnp.stack([src, dst])
    x = x + _L0_gnn_ref(_layernorm(x, axis=-1), edge_index, L0_gnn_weight, L0_gnn_attn_l, L0_gnn_attn_r)
    x = x + _L0_ffn_ref(_layernorm(x, axis=-1)[None], L0_ffn_W_gat, L0_ffn_att_src, L0_ffn_att_dst, L0_ffn_b_gat, L0_ffn_ln_gamma, L0_ffn_ln_beta, L0_ffn_W1, L0_ffn_b1, L0_ffn_W2, L0_ffn_b2, L0_ffn_edge_index)[0]
    x = x + _L1_gnn_ref(_layernorm(x, axis=-1), edge_weight, L1_gnn_weight, src, dst, edge_type_8)
    x = x + _L1_ffn_ref(_layernorm(x, axis=-1)[None], L1_ffn_Wg, L1_ffn_bg, L1_ffn_W1, L1_ffn_b1, L1_ffn_W2, L1_ffn_b2)[0]
    return x

_drawn_inputs = setup_inputs


def setup_inputs(seed=0):
    import zlib

    import numpy as np

    out = dict(_drawn_inputs(seed))
    spreads = {'L0_ffn_b_gat': (0.0, 0.1),
     'L0_ffn_ln_gamma': (1.0, 0.2),
     'L0_ffn_ln_beta': (0.0, 0.1),
     'L0_ffn_b1': (0.0, 0.1),
     'L0_ffn_b2': (0.0, 0.1),
     'L1_ffn_bg': (0.0, 0.348),
     'L1_ffn_b1': (0.0, 0.8),
     'L1_ffn_b2': (0.0, 0.297)}
    factors = {}
    for name, (base, spread) in spreads.items():
        noise = np.random.default_rng([zlib.crc32(name.encode()), seed]).standard_normal(out[name].shape)
        drawn = base * np.exp(spread * noise) if base else spread * noise
        out[name] = jnp.asarray(drawn.astype(out[name].dtype))
    for name, factor in factors.items():
        out[name] = (out[name] * factor).astype(out[name].dtype)
    return out
```

```python
from contextlib import ExitStack

import concourse.bass as bass
from concourse import mybir

F32 = mybir.dt.float32
BF16 = mybir.dt.bfloat16
I32 = mybir.dt.int32
ALU = mybir.AluOpType
ACT = mybir.ActivationFunctionType
AX = mybir.AxisListType
RMAX = bass.bass_isa.ReduceOp.max

P = 128
ROW, BLOCK_BITS, LANE_MASK = 4, 7, 127
BIG_TILES = 5


class Chain:

    def __init__(self, eng, sem):
        self.eng, self.sem, self.n = eng, sem, 0

    def __call__(self, ins):
        ins.then_inc(self.sem, 1)
        self.n = self.n + 1
        self.eng.wait_ge(self.sem, self.n)


def graph_layers(nc, x, src, dst, etype, eweight, w_gat, attn_l, attn_r, w_score, att_src, att_dst, b_gat, ln_gamma,
                 ln_beta, moe0_w1, moe0_b1, moe0_w2, moe0_b2, edges0, w_rel, w_gate, b_gate, moe1_w1, moe1_b1,
                 moe1_w2, moe1_b2, out):
    N, D = x.shape
    KT = D // P
    NB = -(-N // P)
    NT = NB + NB % 2
    FULL, REST = N // P, N % P
    HEADS = attn_l.shape[0]
    HD = D // HEADS
    SH, E0 = att_src.shape
    SC = SH * E0
    R = w_rel.shape[0]
    E1 = w_gate.shape[1]
    F0, F1 = moe0_w1.shape[2] // P, moe1_w1.shape[2] // P
    EB, EC = edges0.shape[1], src.shape[0]
    CB = EB // P
    CC = -(-EC // P // 4) * 4 + 0
    CC = CC if CC * P >= EC else CC + 4
    TB = -(-((CB * P + NB * (P - 1)) // P) // 4) * 4
    TC = -(-((CC * P + NB * (P - 1)) // P) // 4) * 4
    GROUPS = NB // BIG_TILES
    GT = BIG_TILES * P
    HALF = GT // 2
    assert D == 2 * P and NB % BIG_TILES == 0 and CB * P == EB and CB % 4 == 0

    tab_val = nc.dram_tensor("tab_val", (NT * P, D + HEADS), F32, kind="Internal").ap()
    tab_left = nc.dram_tensor("tab_left", (NT * P, HEADS), F32, kind="Internal").ap()
    tab_src = nc.dram_tensor("tab_src", (NT * P, SC + SH), F32, kind="Internal").ap()
    tab_dst = nc.dram_tensor("tab_dst", (NT * P, 2 * SH), F32, kind="Internal").ap()
    tab_rel = nc.dram_tensor("tab_rel", (NT * P * R, D), F32, kind="Internal").ap()
    rec_b = nc.dram_tensor("rec_b", (P * TB, ROW), F32, kind="Internal").ap()
    rec_c = nc.dram_tensor("rec_c", (P * TC, ROW), F32, kind="Internal").ap()

    with ExitStack() as ctx:
        def sb(name, shape, dt=F32):
            return ctx.enter_context(nc.sbuf_tensor(name, shape, dt))

        def sem(name):
            return ctx.enter_context(nc.semaphore(name))

        ps = [ctx.enter_context(nc.psum_tensor(f"bank{i}", [P, 512], F32)) for i in range(8)]

        X = sb("X", [P, NT, D])
        ident = sb("ident", [P, P])
        iota_row = sb("iota_row", [P, P])
        before = sb("before", [P, P], BF16)
        ones_b = sb("ones_b", [P, P], BF16)
        ones_f = sb("ones_f", [P, P])
        iota_blk = sb("iota_blk", [P, NB])
        iota_tile = sb("iota_tile", [1, TC])
        lower0 = sb("lower0", [P, E0, E0])
        lower1 = sb("lower1", [P, E1, E1])
        xn = sb("xn", [P, 2, D])
        xTs = sb("xTs", [P, 2, KT, P])
        rows = sb("rows", [P, 2, D + 2 * HEADS])
        stats = sb("stats", [P, NT, 6])
        mean = sb("mean", [P, NT])
        var = sb("var", [P, NT])
        tmpn = sb("tmpn", [P, NT])
        rstd = sb("rstd", [P, NT])
        sorted_b = sb("sorted_b", [P, TB, ROW])
        sorted_c = sb("sorted_c", [P, TC, ROW])
        tile_blk_b = sb("tile_blk_b", [1, TB], I32)
        tile_blk_c = sb("tile_blk_c", [1, TC], I32)
        pick = sb("pick", [P, 4, 2], I32)
        got = sb("got", [P, 4, D + HEADS])
        got_left = sb("got_left", [P, 4, HEADS])
        hot = sb("hot", [P, 2, P])
        diag = sb("diag", [P, 2, SH, P])
        small = sb("small", [P, 2, 16])
        ecol = sb("ecol", [P, NT], I32)
        erow = sb("erow", [P, NT], I32)
        al_b = sb("al_b", [P, D])
        ar_b = sb("ar_b", [P, D])
        prod = sb("prod", [P, D])
        asrc_b = sb("asrc_b", [P, SC])
        adst_b = sb("adst_b", [P, SC])
        bg_b = sb("bg_b", [P, SC])
        gamma_b = sb("gamma_b", [P, SC])
        beta_b = sb("beta_b", [P, SC])
        bgate_b = sb("bgate_b", [P, E1])
        wg_sb = sb("wg_sb", [P, KT, D])
        ws_sb = sb("ws_sb", [P, KT, SC])
        wgate_sb = sb("wgate_sb", [P, KT, E1])
        b1_0 = sb("b1_0", [P, E0, F0])
        b1_1 = sb("b1_1", [P, E1, F1])
        b2_0 = sb("b2_0", [1, E0, D])
        b2_1 = sb("b2_1", [1, E1, D])
        nodes = sb("nodes", [P, NT, SC + SH])
        adm = sb("adm", [P, NT, 2 * SH])
        gates = sb("gates", [P, NT, E1])
        gx = sb("gx", [P, NT, E1])
        gy = sb("gy", [P, NT])
        eps = sb("eps", [P, 1])
        low = sb("low", [P, SH])
        nlow = sb("nlow", [P, SH])

        rec_slot = sb("rec_slot", [P, 4, ROW])
        bf2 = sb("bf2", [1, TC])
        small2 = sb("small2", [P, NT, SH])
        ARENA = 23296
        arena = sb("arena", [P, ARENA])

        def part(at, *dims, dt=F32):
            n = 1
            for d in dims:
                n *= d
            words = n if dt != BF16 else n // 2
            assert at + words <= ARENA, (at, words)
            v = arena[:, at:at + words]
            if dt != F32:
                v = v.bitcast(dt)
            if len(dims) == 2:
                v = v.rearrange("p (a b) -> p a b", b=dims[1])
            if len(dims) == 3:
                v = v.rearrange("p (a b c) -> p a b c", b=dims[1], c=dims[2])
            return v

        def bucket_parts(C):
            at = 0
            ohv = part(at, NB, C, dt=BF16); at += NB * C // 2
            cnt = part(at, NB, C); at += NB * C
            pk = part(at, C, ROW); at += C * ROW
            di = part(at, C, dt=I32); at += C
            si = part(at, C, dt=I32); at += C
            ti = part(at, C, dt=I32); at += C
            addr = part(at, C, dt=I32); at += C
            chunk = part(at, 2, 512); at += 1024
            bf = part(at, C); at += C
            wi = part(at, C); at += C
            return ohv, cnt, pk, di, si, ti, addr, chunk, bf, wi

        bcnt = sb("bcnt", [P, NB])
        bnum = sb("bnum", [P, NB])
        bint = sb("bint", [P, NB], I32)
        bnt = sb("bnt", [P, NB])
        bend = sb("bend", [P, NB])
        badj = sb("badj", [P, NB])
        bz = sb("bz", [P, 512])
        carry = sb("carry", [P, 1])
        XT = part(0, KT, NT * P)
        R0 = KT * NT * P
        edge1 = part(R0, TB, SC + SH)
        edge2 = part(R0 + TB * (SC + SH), TB, 2 * SH)
        agg_b = part(R0 + TB * (SC + 3 * SH), NT, SC + SH)
        agg_c = part(R0, NT, D)
        wrel = part(R0 + NT * D, KT, R * D)
        rel_out = [part(R0 + NT * D + KT * R * D + q * 1024, 2, 512) for q in range(4)]
        w1v, w2v = {}, {}
        for m, F in ((0, F0), (1, F1)):
            half = KT * F * P
            w1v[m] = [part(R0 + u * 2 * half, KT, F * P) for u in range(2)]
            w2v[m] = [part(R0 + u * 2 * half + half, F, D) for u in range(2)]
        R1 = R0 + 4 * KT * F1 * P
        hT = part(R1, F1, GT)
        pairs = part(R1 + F1 * GT, NT, E1 * E1)
        pairs2 = part(R1 + F1 * GT + NT * E1 * E1, NT, E1 * E1)

        block = ctx.enter_context(nc.Block())

        S = {}

        def s(name):
            if name not in S:
                S[name] = sem(name)
            return S[name]

        ASKS = {n: i + 1 for i, n in enumerate(("std_val", "std_score", "self_exp", "edge_exp", "std_agg", "top_exp0",
                                                "std_rel", "std_gate", "top_exp1"))}
        NBUCK = {"b": (CB, TB, 400), "c": (CC, TC, 490)}
        for C, _, w in NBUCK.values():
            assert (NB * C) % (2 * w) == 0, (NB * C, w)
        parts = {k: bucket_parts(NBUCK[k][0]) for k in NBUCK}
        rec = {"b": rec_b, "c": rec_c}
        srt = {"b": sorted_b, "c": sorted_c}
        LN_STAGES = ("val", "score", "rel", "gate")
        WIDTH = {"val": D, "score": SC, "rel": R * D, "gate": E1}

        @block.sync
        def _(sp):
            sp.wait_ge(s("x_zeroed"), 1)
            sp.dma_start(X[:, 0:FULL, :], x[0:FULL * P, :].rearrange("(t p) d -> p t d", p=P)).then_inc(s("x_in"), 16)
            sp.dma_start(X[0:REST, FULL, :], x[FULL * P:N, :]).then_inc(s("x_in"), 16)
            sp.dma_start(ecol[:, 0:FULL], dst[0:FULL * P].rearrange("(t p) -> p t", p=P), allow_slow_non_contiguous=True).then_inc(s("x_in"), 16)
            sp.dma_start(ecol[0:REST, FULL:FULL + 1], dst[FULL * P:N].rearrange("(p o) -> p o", o=1), allow_slow_non_contiguous=True).then_inc(s("x_in"), 16)
            sp.dma_start(erow[:, 0:FULL], src[0:FULL * P].rearrange("(t p) -> p t", p=P), allow_slow_non_contiguous=True).then_inc(s("x_in"), 16)
            sp.dma_start(erow[0:REST, FULL:FULL + 1], src[FULL * P:N].rearrange("(p o) -> p o", o=1), allow_slow_non_contiguous=True).then_inc(s("x_in"), 16)
            flat = lambda a: a.rearrange("a b -> (a b)")
            loads = [
                (al_b[:], flat(attn_l).partition_broadcast(P)), (ar_b[:], flat(attn_r).partition_broadcast(P)),
                (asrc_b[:], flat(att_src).partition_broadcast(P)), (adst_b[:], flat(att_dst).partition_broadcast(P)),
                (bg_b[:], b_gat.partition_broadcast(P)), (gamma_b[:], ln_gamma.partition_broadcast(P)),
                (beta_b[:], ln_beta.partition_broadcast(P)), (bgate_b[:], b_gate.partition_broadcast(P)),
                (wg_sb[:], w_gat.rearrange("(k p) n -> p k n", p=P)),
                (ws_sb[:], w_score.rearrange("(k p) n -> p k n", p=P)),
                (wgate_sb[:], w_gate.rearrange("(k p) n -> p k n", p=P)),
                (b2_0[:], moe0_b2.rearrange("(o e) d -> o e d", o=1)), (b2_1[:], moe1_b2.rearrange("(o e) d -> o e d", o=1)),
            ] + [(b1_0[:, e, :], moe0_b1[e].rearrange("(f p) -> p f", p=P)) for e in range(E0)] \
              + [(b1_1[:, e, :], moe1_b1[e].rearrange("(f p) -> p f", p=P)) for e in range(E1)]
            for o, i in loads:
                sp.dma_start(o, i, allow_slow_non_contiguous=True).then_inc(s("params_in"), 16)
            S["n_params"] = 16 * len(loads)
            for k in "bc":
                C, T, _ = NBUCK[k]
                ohv, cnt, pk, di, si, ti, addr, chunk, bf, wi = parts[k]
                sp.wait_ge(s(f"edges_zeroed_{k}"), 1)
                sp.dma_start(rec[k].rearrange("(p t) r -> p t r", p=P), srt[k][:]).then_inc(s(f"pad_out_{k}"), 16)
                if k == "b":
                    sp.dma_start(si, edges0[0].rearrange("(p c) -> p c", p=P)).then_inc(s("edges_in_b"), 16)
                    sp.dma_start(di, edges0[1].rearrange("(p c) -> p c", p=P)).then_inc(s("edges_in_b"), 16)
                else:
                    full, rest = EC // C, EC % C
                    for o, i in ((si, src), (di, dst), (ti, etype), (wi, eweight)):
                        sp.dma_start(o[0:full, :], i[0:full * C].rearrange("(p c) -> p c", c=C)).then_inc(s("edges_in_c"), 16)
                        sp.dma_start(o[full:full + 1, 0:rest], i[full * C:EC].rearrange("(o c) -> o c", o=1)).then_inc(s("edges_in_c"), 16)
                for q in range(4):
                    sp.wait_ge(s(f"scattered_{k}{q}"), 16 * (C // 4))
                sp.wait_ge(s(f"pad_out_{k}"), 16)
                sp.dma_start(srt[k][:], rec[k].rearrange("(p t) r -> p t r", p=P)).then_inc(s(f"sorted_in_{k}"), 16)

            def store_val(i, first):
                for u in range(2):
                    t = i * 2 + u
                    sp.wait_ge(s("val_row_ready"), t + 1)
                    sp.dma_start(tab_val[bass.ds(t * P, P), :], rows[:, u, 0:D + HEADS]).then_inc(s(f"val_out{u}"), 16)
                    sp.dma_start(tab_left[bass.ds(t * P, P), :], rows[:, u, D + HEADS:D + 2 * HEADS]).then_inc(s(f"val_out{u}"), 16)
            store_val(0, True)
            with sp.Fori(1, NT // 2) as i:
                store_val(i, False)
            sp.wait_ge(s("nodes_ready"), 1)
            sp.dma_start(tab_src.rearrange("(t p) r -> p t r", p=P), nodes[:]).then_inc(s("src_out"), 16)
            sp.wait_ge(s("maxima_ready"), 1)
            sp.dma_start(tab_dst.rearrange("(t p) r -> p t r", p=P), adm[:]).then_inc(s("dst_out"), 16)
            def load_experts(m, E, w1, w2):
                for e in range(E):
                    u = e % 2
                    if e == 0:
                        sp.wait_ge(s(f"moe_room{m}"), 1)
                    if e >= 2:
                        sp.wait_ge(s(f"expert_done{m}"), e - 1)
                    sp.dma_start(w1v[m][u], w1[e].rearrange("(k p) f -> p k f", p=P)).then_inc(s(f"w_in{m}{u}"), 16)
                    sp.dma_start(w2v[m][u], w2[e].rearrange("(f p) d -> p f d", p=P)).then_inc(s(f"w_in{m}{u}"), 16)
            load_experts(0, E0, moe0_w1, moe0_w2)
            sp.wait_ge(s("rel_room"), 1)
            sp.dma_start(wrel.rearrange("p k (r n) -> p k r n", r=R)[:, 0], w_rel[:, 0:P, :].rearrange("r p n -> p r n")).then_inc(s("wrel_in"), 16)
            sp.dma_start(wrel.rearrange("p k (r n) -> p k r n", r=R)[:, 1], w_rel[:, P:2 * P, :].rearrange("r p n -> p r n")).then_inc(s("wrel_in"), 16)
            tr = tab_rel.rearrange("(n r) d -> n (r d)", r=R)

            def store_rel(i, first):
                for u in range(2):
                    t = i * 2 + u
                    for q in range(4):
                        sp.wait_ge(s(f"rel_ready{q % 2}"), t * 2 + q // 2 + 1)
                        sp.dma_start(tr[bass.ds(t * P, P), q * 512:(q + 1) * 512], rel_out[q][:, u, :]).then_inc(s(f"rel_out{u}{q}"), 16)
            store_rel(0, True)
            with sp.Fori(1, NT // 2) as i:
                store_rel(i, False)
            load_experts(1, E1, moe1_w1, moe1_w2)
            sp.wait_ge(s("acc_done1"), 1 + NB * E1)
            sp.dma_start(out[0:FULL * P, :].rearrange("(t p) d -> p t d", p=P), X[:, 0:FULL, :]).then_inc(s("result_out"), 16)
            sp.dma_start(out[FULL * P:N, :], X[0:REST, FULL, :]).then_inc(s("result_out"), 16)
            sp.wait_ge(s("result_out"), 32)

        n_params = S.pop("n_params")

        @block.gpsimd
        def _(pool):
            ch = Chain(pool, s("pool_chain"))
            ch(pool.memset(ident[:], 0.0))
            ch(pool.affine_select(out=ident[:], in_=ident[:], compare_op=ALU.not_equal, fill=1.0, base=0,
                                  pattern=[[-1, P]], channel_multiplier=1))
            ch(pool.memset(ones_f[:], 1.0))
            ch(pool.memset(ones_b[:], 1.0))
            ch(pool.affine_select(out=before[:], in_=ones_b[:], compare_op=ALU.is_gt, fill=0.0, base=0,
                                  pattern=[[1, P]], channel_multiplier=-1))
            ch(pool.iota(iota_row[:], [[1, P]], base=0, channel_multiplier=0, allow_small_or_imprecise_dtypes=True))
            ch(pool.iota(iota_blk[:], [[1, NB]], base=0, channel_multiplier=0, allow_small_or_imprecise_dtypes=True))
            ch(pool.iota(iota_tile[:], [[1, TC]], base=0, channel_multiplier=0, allow_small_or_imprecise_dtypes=True))
            for low_m, E in ((lower0, E0), (lower1, E1)):
                ch(pool.memset(low_m[:], 1.0))
                ch(pool.affine_select(out=low_m[:], in_=low_m[:], compare_op=ALU.is_gt, fill=0.0, base=0,
                                      pattern=[[1, E], [-1, E]], channel_multiplier=0))
            pool.memset(eps[:], 1e-5).then_inc(s("consts"), 1)

            for k in "bc":
                C, T, _ = NBUCK[k]
                pk = parts[k][2]

                def scatter(i, first):
                    for q in range(4):
                        pool.wait_ge(s(f"place_ready_{k}"), i * 4 + q + 1)
                        pool.sem_inc(s("pool_turn"), 1)
                        pool.indirect_dma_start(rec[k], bass.IndirectOffsetOnAxis(ap=pick[:, q, 0:1], axis=0),
                                                rec_slot[:, q, :], None).then_inc(s(f"scattered_{k}{q}"), 16)
                pool.wait_ge(s(f"pad_out_{k}"), 16)
                scatter(0, True)
                with pool.Fori(1, C // 4) as i:
                    scatter(i, False)

            for u in range(2):
                pool.wait_ge(s(f"val_out{u}"), 32 * (NT // 2))

            def gather_val(i, first):
                for u in range(2):
                    pool.wait_ge(s("val_pick"), i * 2 + u + 1)
                    pool.sem_inc(s("pool_turn"), 1)
                    pool.indirect_dma_start(got[:, u, 0:D + HEADS], None, tab_val,
                                            bass.IndirectOffsetOnAxis(ap=pick[:, u, 0:1], axis=0)).then_inc(s(f"val_got{u}"), 16)
                    pool.indirect_dma_start(got_left[:, u, :], None, tab_left,
                                            bass.IndirectOffsetOnAxis(ap=pick[:, u, 1:2], axis=0)).then_inc(s(f"val_got{u}"), 16)
            gather_val(0, True)
            with pool.Fori(1, NT // 2) as i:
                gather_val(i, False)

            pool.wait_ge(s("low_ready"), 1)
            pool.partition_all_reduce(low[:], nlow[:], P, RMAX).then_inc(s("low_all"), 1)

            def gathers(key, T, table, width):
                def body(i, first):
                    for q in range(4):
                        pool.wait_ge(s(f"{key}_pick"), i * 4 + q + 1)
                        pool.sem_inc(s("pool_turn"), 1)
                        pool.indirect_dma_start(got[:, q, 0:width], None, table,
                                                bass.IndirectOffsetOnAxis(ap=pick[:, q, 0:1], axis=0)).then_inc(s(f"{key}_got{q}"), 16)
                body(0, True)
                with pool.Fori(1, T // 4) as i:
                    body(i, False)
            pool.wait_ge(s("src_out"), 16)
            gathers("src", TB, tab_src, SC + SH)
            pool.wait_ge(s("dst_out"), 16)
            gathers("dst", TB, tab_dst, 2 * SH)
            for u in range(2):
                for q in range(4):
                    pool.wait_ge(s(f"rel_out{u}{q}"), 16 * (NT // 2))
            gathers("rel", TC, tab_rel, D)

        @block.scalar
        def _(act):
            def settle():
                act.sem_inc(s("act_turn"), 1)

            act.wait_ge(s("consts"), 1)
            for k in "bc":
                C, T, _ = NBUCK[k]
                pk, addr = parts[k][2], parts[k][6]
                act.wait_ge(s(f"places_{k}"), 1)

                def place(i, first):
                    for q in range(4):
                        if not first:
                            act.wait_ge(s(f"scattered_{k}{q}"), i * 16)
                            settle()
                        act.copy(rec_slot[:, q, :], pk[:, bass.ds(i * 4 + q, 1), :].rearrange("p a r -> p (a r)")).then_inc(s("rec_slot_set"), 1)
                        act.copy(pick[:, q, 0:1], addr[:, bass.ds(i * 4 + q, 1)]).then_inc(s(f"place_ready_{k}"), 1)
                place(0, True)
                with act.Fori(1, C // 4) as i:
                    place(i, False)

            def std(k):
                act.wait_ge(s("asked"), ASKS[f"std_{k}"])
                act.activation(var[:], var[:], ACT.Sqrt, bias=eps[:, 0:1]).then_inc(s("answered"), 1)

            def transposed(k, keep):
                def body(i, first):
                    for u in range(2):
                        t = i * 2 + u
                        act.wait_ge(s(f"tp_{k}"), t + 1)
                        if not first:
                            act.wait_ge(s("rel_mm" if k == "rel" else f"prod_{k}"), (t - 1) * 4 if k == "rel" else t - 1)
                        settle()
                        v = ps[u][:, 0:D].rearrange("p (k n) -> p k n", k=KT)
                        if keep:
                            act.copy(XT[:, :, bass.ds(t * P, P)], v).then_inc(s("xt_kept"), 1)
                        act.copy(xTs[:, u, :, :], v).then_inc(s(f"xT_{k}"), 1)
                        if k == "val":
                            act.wait_ge(s("prod_val"), t + 1)
                            if not first:
                                act.wait_ge(s(f"val_out{u}"), 32 * i)
                            settle()
                            act.copy(rows[:, u, 0:D], ps[2 + u][:, 0:D]).then_inc(s("val_copied"), 1)
                        if k == "score":
                            act.wait_ge(s("prod_score"), t + 1)
                            settle()
                            act.copy(nodes[:, bass.ds(t, 1), 0:SC].rearrange("p a c -> p (a c)"), ps[2 + u][:, 0:SC]).then_inc(s("score_copied"), 1)
                        if k == "gate":
                            act.wait_ge(s("prod_gate"), t + 1)
                            settle()
                            act.copy(gates[:, bass.ds(t, 1), :].rearrange("p a c -> p (a c)"), ps[2 + u][:, 0:E1]).then_inc(s("gate_copied"), 1)
                        if k == "rel":
                            for q in (0, 2):
                                act.wait_ge(s("rel_mm"), t * 4 + q + 1)
                                if not first:
                                    act.wait_ge(s(f"rel_out{u}{q}"), 16 * i)
                                settle()
                                act.copy(rel_out[q][:, u, :], ps[2 + q][:, :]).then_inc(s("rel_ready0"), 1)
                body(0, True)
                with act.Fori(1, NT // 2) as i:
                    body(i, False)

            std("val")
            transposed("val", False)
            def picks(i, first):
                for u in range(2):
                    t = i * 2 + u
                    if not first:
                        act.wait_ge(s(f"val_got{u}"), 32 * i)
                        settle()
                    act.copy(pick[:, u, 0:1], ecol[:, bass.ds(t, 1)]).then_inc(s("val_col"), 1)
                    act.copy(pick[:, u, 1:2], erow[:, bass.ds(t, 1)]).then_inc(s("val_pick"), 1)
                    act.wait_ge(s("val_z"), t + 1)
                    act.activation(small[:, 0, 4:4 + HEADS], small[:, 0, 0:HEADS], ACT.Exp).then_inc(s("val_e"), 1)
            act.wait_ge(s("scattered_c0"), 16 * (CC // 4))
            for q in range(4):
                act.wait_ge(s(f"scattered_c{q}"), 16 * (CC // 4))
            picks(0, True)
            with act.Fori(1, NT // 2) as i:
                picks(i, False)

            std("score")
            transposed("score", True)

            act.wait_ge(s("sorted_in_b"), 16)
            for u in range(2):
                act.wait_ge(s(f"val_got{u}"), 32 * (NT // 2))

            def src_rows(i, first):
                for q in range(4):
                    if first is True:
                        act.copy(pick[:, q, 0:1], sorted_b[:, q, 0:1]).then_inc(s("src_pick"), 1)
                for q in range(4):
                    j = i * 4 + q
                    u = q % 2
                    act.wait_ge(s(f"src_got{q}"), i * 16 + 16)
                    settle()
                    act.copy(edge1[:, bass.ds(j, 1), :].rearrange("p a c -> p (a c)"), got[:, q, 0:SC + SH]).then_inc(s("src_kept"), 1)
                    act.wait_ge(s("src_shifted"), j + 1)
                    if not (first is True and q < 2):
                        act.wait_ge(s("spread"), j - 1)
                    settle()
                    for h in range(SH):
                        act.activation(diag[:, u, h, :], ident[:], ACT.Copy, scale=small[:, u, h:h + 1]).then_inc(s("diag_ready"), 1)
                    if first != "last":
                        act.copy(pick[:, q, 0:1], sorted_b[:, bass.ds(j + 4, 1), 0]).then_inc(s("src_pick"), 1)
            src_rows(0, True)
            with act.Fori(1, TB // 4 - 1) as i:
                src_rows(i, False)
            src_rows(TB // 4 - 1, "last")

            def dst_rows(i, first):
                for q in range(4):
                    if first is True:
                        act.copy(pick[:, q, 0:1], sorted_b[:, q, 2:3]).then_inc(s("dst_pick"), 1)
                for q in range(4):
                    j = i * 4 + q
                    act.wait_ge(s(f"dst_got{q}"), i * 16 + 16)
                    settle()
                    act.copy(edge2[:, bass.ds(j, 1), :].rearrange("p a c -> p (a c)"), got[:, q, 0:2 * SH]).then_inc(s("dst_kept"), 1)
                    if first != "last":
                        act.copy(pick[:, q, 0:1], sorted_b[:, bass.ds(j + 4, 1), 2]).then_inc(s("dst_pick"), 1)
            dst_rows(0, True)
            with act.Fori(1, TB // 4 - 1) as i:
                dst_rows(i, False)
            dst_rows(TB // 4 - 1, "last")

            act.wait_ge(s("asked"), ASKS["self_exp"])
            act.activation(small2[:], small2[:], ACT.Exp).then_inc(s("answered"), 1)
            act.wait_ge(s("asked"), ASKS["edge_exp"])
            act.activation(edge2[:, :, 0:SH], edge2[:, :, 0:SH], ACT.Exp).then_inc(s("answered"), 1)
            act.wait_ge(s("asked"), ASKS["std_agg"])
            act.activation(gy[:], gy[:], ACT.Sqrt, bias=eps[:, 0:1]).then_inc(s("answered"), 1)
            act.wait_ge(s("asked"), ASKS["top_exp0"])
            act.activation(gates[:, :, 0:E0], gates[:, :, 0:E0], ACT.Exp).then_inc(s("answered"), 1)

            def hidden(m, E, FC, b1):
                act.sem_inc(s(f"h_room{m}"), 4)
                with act.Fori(0, E) as e:
                    with act.Fori(0, GROUPS) as g:
                        for f in range(FC):
                            for half in range(2):
                                n = ((e * GROUPS + g) * FC + f) * 2 + half
                                act.wait_ge(s(f"mm1_{m}"), n + 1)
                                if f == 0 and half == 0:
                                    act.wait_ge(s(f"group_done{m}"), e * GROUPS + g + 1)
                                settle()
                                act.activation(hT[:, f, half * HALF:(half + 1) * HALF], ps[(f * 2 + half) % 4][:, 0:HALF],
                                               ACT.Gelu, bias=b1[:, bass.ds(e, 1), f]).then_inc(s(f"h_room{m}"), 1)
            hidden(0, E0, F0, b1_0)
            std("rel")
            transposed("rel", False)

            act.wait_ge(s("sorted_in_c"), 16)
            def rel_picks(i, first):
                for q in range(4):
                    j = i * 4 + q
                    if not first:
                        act.wait_ge(s(f"rel_got{q}"), 16 * i)
                        act.wait_ge(s("rel_spread"), j - 3)
                        settle()
                    act.copy(pick[:, q, 0:1], sorted_c[:, bass.ds(j, 1), 0]).then_inc(s("rel_pick"), 1)
            rel_picks(0, True)
            with act.Fori(1, TC // 4) as i:
                rel_picks(i, False)
            std("gate")
            transposed("gate", True)
            act.wait_ge(s("asked"), ASKS["top_exp1"])
            act.activation(gates[:, :, 0:E1], gates[:, :, 0:E1], ACT.Exp).then_inc(s("answered"), 1)
            hidden(1, E1, F1, b1_1)

        @block.tensor
        def _(pe):
            pe.wait_ge(s("consts"), 1)
            for k in "bc":
                C, T, w = NBUCK[k]
                ohv = parts[k][0].rearrange("p b c -> p (b c)")
                pe.wait_ge(s(f"counted_{k}"), 1)
                pe.matmul(ps[4][:, 0:NB], ones_f[:], bcnt[:], start=True, stop=True).then_inc(s(f"totals_{k}"), 1)

                def counts(i, first):
                    for u in range(2):
                        n = i * 2 + u
                        if not first:
                            pe.wait_ge(s(f"chunk_used_{k}"), n - 1)
                        o = ohv[:, bass.ds(n * w, w)]
                        pe.matmul(ps[u][:, 0:w], ones_b[:], o, start=True, stop=True)
                        pe.matmul(ps[2 + u][:, 0:w], before[:], o, start=True, stop=True).then_inc(s(f"chunk_{k}"), 1)
                counts(0, True)
                with pe.Fori(1, NB * C // w // 2) as i:
                    counts(i, False)

            def tiles(k, weights):
                W = WIDTH[k]

                def body(i, first):
                    for u in range(2):
                        t = i * 2 + u
                        pe.wait_ge(s(f"xn_{k}"), t + 1)
                        if not first:
                            pe.wait_ge(s(f"xT_{k}"), t - 1)
                        pe.transpose(ps[u][:, 0:P], xn[:, u, 0:P], ident[:])
                        pe.transpose(ps[u][:, P:2 * P], xn[:, u, P:2 * P], ident[:]).then_inc(s(f"tp_{k}"), 1)
                        pe.wait_ge(s(f"xT_{k}"), t + 1)
                        if k == "rel":
                            for q in range(4):
                                if not (first and u == 0):
                                    pe.wait_ge(s(f"rel_ready{q % 2}"), (t - 1) * 2 + q // 2 + 1)
                                for kt in range(KT):
                                    mm = pe.matmul(ps[2 + q][:, :], xTs[:, u, kt, :], wrel[:, kt, q * 512:(q + 1) * 512],
                                                   start=(kt == 0), stop=(kt == KT - 1))
                                mm.then_inc(s("rel_mm"), 1)
                            pe.sem_inc(s("pe_turn"), 1)
                        else:
                            if not first:
                                pe.wait_ge(s({"val": "val_copied", "score": "score_copied", "gate": "gate_copied"}[k]), t - 1)
                            for kt in range(KT):
                                mm = pe.matmul(ps[2 + u][:, 0:W], xTs[:, u, kt, :], weights[:, kt, :],
                                               start=(kt == 0), stop=(kt == KT - 1))
                            mm.then_inc(s(f"prod_{k}"), 1)
                body(0, True)
                with pe.Fori(1, NT // 2) as i:
                    body(i, False)

            pe.wait_ge(s("params_in"), n_params)
            for k in "bc":
                pe.wait_ge(s(f"places_{k}"), 1)
            tiles("val", wg_sb)
            tiles("score", ws_sb)

            def spread(i, first):
                for q in range(4):
                    j = i * 4 + q
                    u = q % 2
                    pe.wait_ge(s("hot_b"), j + 1)
                    pe.wait_ge(s("diag_ready"), SH * j + SH)
                    if not (first and q < 2):
                        pe.wait_ge(s("spread_used"), j - 1)
                    pe.matmul(ps[u][:, :], hot[:, u, :], diag[:, u, :, :].rearrange("p h e -> p (h e)"), start=True, stop=True).then_inc(s("spread"), 1)
            spread(0, True)
            with pe.Fori(1, TB // 4) as i:
                spread(i, False)

            def sums(key, T, rhs, W):
                def body(i, first):
                    for q in range(4):
                        j = i * 4 + q
                        u = q % 2
                        pe.wait_ge(s(f"hot_{key}"), j + 1)
                        if not (first and q < 2):
                            pe.wait_ge(s(f"{key}_added"), j - 1)
                        if key == "rel":
                            pe.wait_ge(s(f"rel_got{q}"), 16 * i + 16)
                        pe.matmul(ps[u][:, 0:W], hot[:, u, :], rhs(j, q), start=True, stop=True).then_inc(s(f"{key}_spread"), 1)
                body(0, True)
                with pe.Fori(1, T // 4) as i:
                    body(i, False)
            pe.wait_ge(s("messages"), 1)
            sums("msg", TB, lambda j, q: edge1[:, bass.ds(j, 1), :].rearrange("p a c -> p (a c)"), SC + SH)

            def experts(m, E, FC, b2):
                pe.wait_ge(s(f"gates_ready{m}"), 1)
                with pe.Fori(0, E // 2) as ep:
                    for u in range(2):
                        e = ep * 2 + u
                        pe.wait_ge(s(f"w_in{m}{u}"), ep * 32 + 32)
                        pe.sem_inc(s("pe_turn"), 1)
                        with pe.Fori(0, GROUPS) as g:
                            ge = e * GROUPS + g
                            for f in range(FC):
                                for half in range(2):
                                    pe.wait_ge(s(f"h_room{m}"), (ge * FC + f) * 2 + half + 1)
                                    for kt in range(KT):
                                        mm = pe.matmul(ps[(f * 2 + half) % 4][:, 0:HALF], w1v[m][u][:, kt, f * P:(f + 1) * P],
                                                       XT[:, kt, bass.ds(g * GT + half * HALF, HALF)],
                                                       start=(kt == 0), stop=(kt == KT - 1))
                                    mm.then_inc(s(f"mm1_{m}"), 1)
                            pe.wait_ge(s(f"h_room{m}"), (ge + 1) * FC * 2 + 4)
                            for a in range(BIG_TILES):
                                pe.wait_ge(s(f"y_room{m}"), ge * BIG_TILES + a + (BIG_TILES if a == 0 else 2 if a == 4 else 1))
                                pe.sem_inc(s("pe_turn"), 1)
                                y = ps[4 + a % 4][:, 0:D]
                                pe.matmul(y, ones_f[0:1, :], b2[0:1, bass.ds(e, 1), :].rearrange("p a c -> p (a c)"), start=True, stop=False)
                                for f in range(FC):
                                    mm = pe.matmul(y, hT[:, f, a * P:(a + 1) * P], w2v[m][u][:, f, :], start=False, stop=(f == FC - 1))
                                mm.then_inc(s(f"mm2_{m}"), 1)
                            pe.wait_ge(s(f"mm2_{m}"), (ge + 1) * BIG_TILES)
                            pe.sem_inc(s(f"group_done{m}"), 1)
                        pe.sem_inc(s(f"expert_done{m}"), 1)
            pe.sem_inc(s("group_done0"), 1)
            pe.sem_inc(s("group_done1"), 1)
            experts(0, E0, F0, b2_0)
            pe.wait_ge(s("wrel_in"), 32)
            tiles("rel", None)
            sums("rel", TC, lambda j, q: got[:, q, 0:D], D)
            tiles("gate", wgate_sb)
            experts(1, E1, F1, b2_1)

        @block.vector
        def _(dve):
            ch = Chain(dve, s("dve_chain"))
            tt, tsc, red = dve.tensor_tensor, dve.tensor_scalar, dve.tensor_reduce

            ch(dve.memset(X[:, FULL:NT, :], 0.0))
            ch(dve.memset(ecol[:], 0))
            ch(dve.memset(erow[:], 0))
            dve.sem_inc(s("x_zeroed"), 1)
            ch(dve.memset(bz[:], 0.0))
            dve.wait_ge(s("consts"), 1)
            for k in "bc":
                C, T, w = NBUCK[k]
                ohv, cnt, pk, di, si, ti, addr, chunk, bf, wi = parts[k]
                if k == "c":
                    for q in range(4):
                        dve.wait_ge(s(f"scattered_b{q}"), 16 * (CB // 4))
                    for a in (di, si, ti):
                        ch(dve.memset(a, 0))
                    ch(dve.memset(wi, 0.0))
                ch(dve.memset(srt[k][:], 0.0))
                ch(dve.memset(srt[k][:, :, 1:2], -1.0))
                dve.sem_inc(s(f"edges_zeroed_{k}"), 1)
                dve.wait_ge(s(f"edges_in_{k}"), 32 if k == "b" else 128)
                ch(dve.memset(pk, 0.0))
                ch(tsc(addr, di, LANE_MASK, None, ALU.bitwise_and))
                ch(dve.tensor_copy(pk[:, :, 1], addr))
                ch(tsc(addr, di, BLOCK_BITS, None, ALU.arith_shift_right))
                ch(dve.tensor_copy(bf, addr))
                if k == "b":
                    ch(dve.tensor_copy(pk[:, :, 0], si))
                    ch(dve.tensor_copy(pk[:, :, 2], di))
                else:
                    ch(dve.scalar_tensor_tensor(out=pk[:, :, 0], in0=si, scalar=float(R), in1=ti, op0=ALU.mult, op1=ALU.add))
                    ch(dve.tensor_copy(pk[:, :, 2], wi))
                ch(tt(ohv, bf.unsqueeze(1).to_broadcast([P, NB, C]), iota_blk[:].unsqueeze(2).to_broadcast([P, NB, C]), ALU.is_equal))
                red(bcnt[:], ohv, AX.X, ALU.add).then_inc(s(f"counted_{k}"), 1)
                dve.wait_ge(s(f"totals_{k}"), 1)
                ch(dve.tensor_copy(bnum[:], ps[4][:, 0:NB]))
                ch(tsc(bint[:], bnum[:], float(P - 1), None, ALU.add))
                ch(tsc(bint[:], bint[:], BLOCK_BITS, None, ALU.arith_shift_right))
                ch(dve.tensor_copy(bnt[:], bint[:]))
                ch(dve.tensor_tensor_scan(bend[:], bnt[:], bz[:, 0:NB], 0.0, ALU.add, ALU.add))
                ch(dve.tensor_tensor_scan(badj[:], bnum[:], bz[:, 0:NB], 0.0, ALU.add, ALU.add))
                ch(tt(badj[:], bnum[:], badj[:], ALU.subtract))
                ch(tt(bnt[:], bend[:], bnt[:], ALU.subtract))
                ch(dve.scalar_tensor_tensor(out=badj[:], in0=bnt[:], scalar=float(P), in1=badj[:], op0=ALU.mult, op1=ALU.add))
                ch(dve.memset(carry[:], 0.0))
                base = ch.n

                def places(i, first):
                    for u in range(2):
                        n = i * 2 + u
                        v = chunk[:, u, 0:w]
                        dve.wait_ge(s(f"chunk_{k}"), n + 1)
                        dve.wait_ge(s("dve_chain"), n * 4 + base)
                        dve.tensor_tensor_scan(v, ps[u][:, 0:w], bz[:, 0:w], carry[:, 0:1], ALU.add, ALU.add).then_inc(s("dve_chain"), 1)
                        dve.wait_ge(s("dve_chain"), n * 4 + base + 1)
                        dve.tensor_copy(carry[:], v[:, w - 1:w]).then_inc(s("dve_chain"), 1)
                        dve.wait_ge(s("dve_chain"), n * 4 + base + 2)
                        tt(v, v, ps[u][:, 0:w], ALU.subtract).then_inc(s("dve_chain"), 1)
                        dve.wait_ge(s("dve_chain"), n * 4 + base + 3)
                        tt(cnt.rearrange("p b c -> p (b c)")[:, bass.ds(n * w, w)], v, ps[2 + u][:, 0:w], ALU.add).then_inc(s("dve_chain"), 1)
                        dve.wait_ge(s("dve_chain"), n * 4 + base + 4)
                        dve.sem_inc(s(f"chunk_used_{k}"), 1)
                places(0, True)
                with dve.Fori(1, NB * C // w // 2) as i:
                    places(i, False)
                ch.n = base + NB * C // w * 4
                ch(tt(cnt, cnt, badj[:].unsqueeze(2).to_broadcast([P, NB, C]), ALU.add))
                ch(tt(cnt, cnt, ohv, ALU.mult))
                ch(red(bf, cnt.rearrange("p b c -> p c b"), AX.X, ALU.add))
                ch(dve.tensor_copy(di, bf))
                ch(tsc(si, di, BLOCK_BITS, None, ALU.arith_shift_right))
                ch(tsc(di, di, LANE_MASK, None, ALU.bitwise_and))
                dve.scalar_tensor_tensor(out=addr, in0=di, scalar=float(T), in1=si, op0=ALU.mult, op1=ALU.add).then_inc(s(f"places_{k}"), 1)
                tb = cnt.rearrange("p b c -> p (b c)")[0:1, 0:T * 8].rearrange("p (t b) -> p t b", b=8)
                blk_i = tile_blk_b if k == "b" else tile_blk_c
                blk_f = bf2[0:1, 0:T]
                ch(dve.memset(blk_f, 0.0))
                for b in range(NB):
                    ch(dve.scalar_tensor_tensor(out=blk_f, in0=iota_tile[0:1, 0:T], scalar=bend[0:1, b:b + 1], in1=blk_f,
                                                op0=ALU.is_ge, op1=ALU.add))
                ch(tsc(blk_i[:], blk_f, float(NB - 1), None, ALU.min))

            def layer_norm(k):
                def st(i, first):
                    for u in range(2):
                        dve.bn_stats(stats[:, bass.ds(i * 2 + u, 1), :].rearrange("p a c -> p (a c)"),
                                     X[:, bass.ds(i * 2 + u, 1), :].rearrange("p a c -> p (a c)")).then_inc(s("stats_done"), 1)
                S["ln"] = S.get("ln", 0) + NT
                with dve.Fori(0, NT // 2) as i:
                    st(i, False)
                dve.wait_ge(s("stats_done"), S["ln"])
                me, mo, ve, vo = (stats[:, :, c] for c in (1, 4, 2, 5))
                ch(tt(mean[:], me, mo, ALU.add))
                ch(tsc(mean[:], mean[:], 0.5, None, ALU.mult))
                ch(tt(tmpn[:], me, mo, ALU.subtract))
                ch(tt(tmpn[:], tmpn[:], tmpn[:], ALU.mult))
                ch(tt(var[:], ve, vo, ALU.add))
                ch(tsc(var[:], var[:], 1.0 / D, None, ALU.mult))
                dve.scalar_tensor_tensor(out=var[:], in0=tmpn[:], scalar=0.25, in1=var[:], op0=ALU.mult, op1=ALU.add).then_inc(s("asked"), 1)
                dve.wait_ge(s("answered"), ASKS[f"std_{k}"])
                ch(dve.reciprocal(rstd[:], var[:]))

                def norm(i, first):
                    for u in range(2):
                        t = i * 2 + u
                        if not first:
                            dve.wait_ge(s(f"tp_{k}"), t - 1)
                        tsc(xn[:, u, :], X[:, bass.ds(t, 1), :].rearrange("p a c -> p (a c)"), mean[:, bass.ds(t, 1)], rstd[:, bass.ds(t, 1)],
                            ALU.subtract, ALU.mult).then_inc(s(f"xn_{k}"), 1)
                        if k == "val":
                            value_terms(t, u, first)
                        if k == "rel":
                            for q in (1, 3):
                                dve.wait_ge(s("rel_mm"), t * 4 + q + 1)
                                if not first:
                                    dve.wait_ge(s(f"rel_out{u}{q}"), 16 * i)
                                dve.sem_inc(s("dve_turn"), 1)
                                dve.tensor_copy(rel_out[q][:, u, :], ps[2 + q][:, :]).then_inc(s("rel_ready1"), 1)

                norm(0, True)
                with dve.Fori(1, NT // 2) as i:
                    norm(i, False)

            def value_terms(t, u, first):
                dve.wait_ge(s("val_copied"), t + 1)
                n = t * 3
                tt(prod[:], rows[:, u, 0:D], ar_b[:], ALU.mult).then_inc(s("val_terms"), 1)
                dve.wait_ge(s("val_terms"), n + 1)
                red(rows[:, u, D:D + HEADS], prod[:].rearrange("p (h d) -> p h d", h=HEADS), AX.X, ALU.add).then_inc(s("val_terms"), 1)
                dve.wait_ge(s("val_terms"), n + 2)
                tt(prod[:], rows[:, u, 0:D], al_b[:], ALU.mult).then_inc(s("val_terms"), 1)
                dve.wait_ge(s("val_terms"), n + 3)
                red(rows[:, u, D + HEADS:D + 2 * HEADS], prod[:].rearrange("p (h d) -> p h d", h=HEADS), AX.X, ALU.add).then_inc(s("val_row_ready"), 1)
                dve.wait_ge(s("val_row_ready"), t + 1)

            dve.wait_ge(s("x_in"), 96)
            dve.wait_ge(s("params_in"), n_params)
            layer_norm("val")

            z, ez, mx = small[:, 0, 0:HEADS], small[:, 0, 4:4 + HEADS], small[:, 0, 8:9]
            base = ch.n

            K = 14

            def mix(i, first):
                for u in range(2):
                    t = i * 2 + u
                    c = Chain(dve, s("dve_chain"))
                    c.n = t * K + base
                    dve.wait_ge(s(f"val_got{u}"), 32 * i + 32)
                    c(tt(z, got_left[:, u, :], got[:, u, D:D + HEADS], ALU.add))
                    c(dve.scalar_tensor_tensor(out=z, in0=z, scalar=0.01, in1=z, op0=ALU.mult, op1=ALU.max))
                    c(red(mx, z, AX.X, ALU.max))
                    c(tsc(z, z, mx, None, ALU.subtract))
                    dve.sem_inc(s("val_z"), 1)
                    dve.wait_ge(s("val_e"), t + 1)
                    c(red(mx, ez, AX.X, ALU.add))
                    c(dve.reciprocal(mx, mx))
                    c(tsc(ez, ez, mx, None, ALU.mult))
                    g = got[:, u, 0:D].rearrange("p (h d) -> p h d", h=HEADS)
                    c(tsc(prod[:, 0:HD], g[:, 0, :], ez[:, 0:1], None, ALU.mult))
                    for h in range(1, HEADS):
                        c(dve.scalar_tensor_tensor(out=prod[:, 0:HD], in0=g[:, h, :], scalar=ez[:, h:h + 1], in1=prod[:, 0:HD], op0=ALU.mult, op1=ALU.add))
                    xv = X[:, bass.ds(t, 1), :].rearrange("p a (h d) -> p (a h) d", h=HEADS)
                    c(tt(xv, xv, prod[:, 0:HD].unsqueeze(1).to_broadcast([P, HEADS, HD]), ALU.add))
                    c(dve.memset(small[:, 0, 12:13], 0.0))
                    c(dve.memset(small[:, 0, 13:14], 0.0))
            mix(0, True)
            with dve.Fori(1, NT // 2) as i:
                mix(i, False)
            ch.n = base + K * NT

            layer_norm("score")
            dve.wait_ge(s("score_copied"), NT)
            fe = nodes[:, :, 0:SC]
            big = agg_b[:, :, 0:SC]
            for o, a in ((nodes[:, :, SC:SC + SH], asrc_b), (adm[:, :, 0:SH], adst_b)):
                ch(tt(big, fe, a[:].unsqueeze(1).to_broadcast([P, NT, SC]), ALU.mult))
                ch(red(o.rearrange("p t h -> p t h"), big.rearrange("p t (h e) -> p t h e", e=E0), AX.X, ALU.add))
            dve.sem_inc(s("nodes_ready"), 1)
            ch(tsc(gx[:, :, 0:SH], nodes[:, :, SC:SC + SH], -1.0, None, ALU.mult))
            red(nlow[:], gx[:, :, 0:SH].rearrange("p t h -> p h t"), AX.X, ALU.max).then_inc(s("low_ready"), 1)
            dve.wait_ge(s("low_all"), 1)
            ch(tsc(low[:], low[:], 1.0, None, ALU.add))
            mxb = adm[:, :, SH:2 * SH]
            ch(dve.memset(mxb, 0.0))
            base = ch.n
            dve.wait_ge(s("sorted_in_b"), 16)

            def hot_tile(rec_sb, j, u, key, weighted):
                tsc(hot[:, u, :], iota_row[:], rec_sb[:, bass.ds(j, 1), 1], rec_sb[:, bass.ds(j, 1), 2] if weighted else None,
                    ALU.is_equal, *([ALU.mult] if weighted else [])).then_inc(s(key), 1)

            def maxima(i, first):
                for q in range(4):
                    j = i * 4 + q
                    u = q % 2
                    if not (first and q < 2):
                        dve.wait_ge(s("spread"), j - 1)
                    hot_tile(sorted_b, j, u, "hot_b", False)
                    dve.wait_ge(s(f"src_got{q}"), i * 16 + 16)
                    tt(small[:, u, 0:SH], got[:, q, SC:SC + SH], low[:], ALU.add).then_inc(s("src_shifted"), 1)
                    dve.wait_ge(s("spread"), j + 1)
                    red(small[:, u, 8:8 + SH], ps[u][:, :].rearrange("p (h e) -> p h e", h=SH), AX.X, ALU.max).then_inc(s("spread_used"), 1)
                    dve.wait_ge(s("spread_used"), j + 1)
                    b = dve.value_load(tile_blk_b[0:1, bass.ds(j, 1)], min_val=0, max_val=NB - 1)
                    mb = mxb[:, bass.ds(b, 1), :].rearrange("p a c -> p (a c)")
                    tt(mb, mb, small[:, u, 8:8 + SH], ALU.max).then_inc(s("dve_chain"), 1)
                    dve.wait_ge(s("dve_chain"), j + 1 + base)
            maxima(0, True)
            with dve.Fori(1, TB // 4) as i:
                maxima(i, False)
            ch.n = base + TB

            lowb = low[:].unsqueeze(1).to_broadcast([P, NT, SH])
            sv, dv = nodes[:, :, SC:SC + SH], adm[:, :, 0:SH]
            ch(tt(mxb, mxb, lowb, ALU.subtract))
            ch(tt(mxb, mxb, sv, ALU.max))
            ch(tt(mxb, mxb, dv, ALU.add))
            ch(dve.scalar_tensor_tensor(out=mxb, in0=mxb, scalar=0.2, in1=mxb, op0=ALU.mult, op1=ALU.max))
            dve.sem_inc(s("maxima_ready"), 1)
            ch(tt(small2[:], sv, dv, ALU.add))
            ch(dve.scalar_tensor_tensor(out=small2[:], in0=small2[:], scalar=0.2, in1=small2[:], op0=ALU.mult, op1=ALU.max))
            ch(tt(small2[:], small2[:], mxb, ALU.subtract))
            dve.sem_inc(s("asked"), 1)
            dve.wait_ge(s("answered"), ASKS["self_exp"])
            ch(dve.tensor_copy(agg_b[:, :, SC:SC + SH], small2[:]))

            def heads(v):
                return v.rearrange("p t (h e) -> p t h e", e=E0)

            ch(tt(heads(agg_b[:, :, 0:SC]), heads(fe), small2[:].unsqueeze(3).to_broadcast([P, NT, SH, E0]), ALU.mult))
            dve.wait_ge(s("src_kept"), TB)
            dve.wait_ge(s("dst_kept"), TB)
            ze, es = edge2[:, :, 0:SH], edge1[:, :, SC:SC + SH]
            ch(tt(ze, ze, es, ALU.add))
            ch(dve.scalar_tensor_tensor(out=ze, in0=ze, scalar=0.2, in1=ze, op0=ALU.mult, op1=ALU.max))
            ch(tt(ze, ze, edge2[:, :, SH:2 * SH], ALU.subtract))
            dve.sem_inc(s("asked"), 1)
            dve.wait_ge(s("answered"), ASKS["edge_exp"])
            ch(tt(heads(edge1[:, :, 0:SC]), heads(edge1[:, :, 0:SC]), ze.unsqueeze(3).to_broadcast([P, TB, SH, E0]), ALU.mult))
            ch(dve.tensor_copy(es, ze))
            dve.sem_inc(s("messages"), 1)

            def add_up(key, T, rec_sb, blk, acc, W, weighted):
                base = ch.n

                def body(i, first):
                    for q in range(4):
                        j = i * 4 + q
                        u = q % 2
                        if not (first and q < 2):
                            dve.wait_ge(s(f"{key}_spread"), j - 1)
                        hot_tile(rec_sb, j, u, f"hot_{key}", weighted)
                        dve.wait_ge(s(f"{key}_spread"), j + 1)
                        b = dve.value_load(blk[0:1, bass.ds(j, 1)], min_val=0, max_val=NB - 1)
                        av = acc[:, bass.ds(b, 1), :].rearrange("p a c -> p (a c)")
                        tt(av, av, ps[u][:, 0:W], ALU.add).then_inc(s(f"{key}_added"), 1)
                        dve.wait_ge(s(f"{key}_added"), j + 1)
                body(0, True)
                with dve.Fori(1, T // 4) as i:
                    body(i, False)
            add_up("msg", TB, sorted_b, tile_blk_b, agg_b, SC + SH, False)

            den = agg_b[:, :, SC:SC + SH]
            ag = agg_b[:, :, 0:SC]

            def all_t(v):
                return v[:].unsqueeze(1).to_broadcast([P, NT, SC])

            def per_t(v):
                return v.unsqueeze(2).to_broadcast([P, NT, SC])
            ch(tsc(den, den, 1e-16, None, ALU.add))
            ch(dve.reciprocal(small2[:], den))
            ch(tt(heads(ag), heads(ag), small2[:].unsqueeze(3).to_broadcast([P, NT, SH, E0]), ALU.mult))
            ch(tt(ag, ag, all_t(bg_b), ALU.add))
            ch(red(gy[:], ag, AX.X, ALU.add))
            ch(tsc(gy[:], gy[:], 1.0 / SC, None, ALU.mult))
            ch(tt(ag, ag, per_t(gy[:]), ALU.subtract))
            ch(tt(fe, ag, ag, ALU.mult))
            ch(red(gy[:], fe, AX.X, ALU.add))
            ch(tsc(gy[:], gy[:], 1.0 / SC, None, ALU.mult))
            dve.sem_inc(s("asked"), 1)
            dve.wait_ge(s("answered"), ASKS["std_agg"])
            ch(dve.reciprocal(gy[:], gy[:]))
            ch(tt(ag, ag, per_t(gy[:]), ALU.mult))
            ch(tt(ag, ag, all_t(gamma_b), ALU.mult))
            ch(tt(ag, ag, all_t(beta_b), ALU.add))
            ch(red(gates[:, :, 0:E0], ag.rearrange("p t (h e) -> p t e h", e=E0), AX.X, ALU.add))
            ch(tsc(gates[:, :, 0:E0], gates[:, :, 0:E0], 1.0 / SH, None, ALU.mult))

            def top2(m, E, lower):
                g, r = gates[:, :, 0:E], gx[:, :, 0:E]
                pair = pairs[:, :, 0:E * E].rearrange("p t (i j) -> p t i j", i=E)
                pair2 = pairs2[:, :, 0:E * E].rearrange("p t (i j) -> p t i j", i=E)
                gi = g.unsqueeze(3).to_broadcast([P, NT, E, E])
                gj = g.unsqueeze(2).to_broadcast([P, NT, E, E])
                ch(tt(pair, gj, gi, ALU.is_equal))
                ch(tt(pair, pair, lower[:].unsqueeze(1).to_broadcast([P, NT, E, E]), ALU.mult))
                ch(tt(pair2, gj, gi, ALU.is_gt))
                ch(tt(pair, pair, pair2, ALU.add))
                ch(red(r, pair, AX.X, ALU.add))
                ch(tsc(r, r, 2.0, None, ALU.is_lt))
                ch(red(gy[:], g, AX.X, ALU.max))
                ch(tt(g, g, gy[:].unsqueeze(2).to_broadcast([P, NT, E]), ALU.subtract))
                dve.sem_inc(s("asked"), 1)
                dve.wait_ge(s("answered"), ASKS[f"top_exp{m}"])
                ch(tt(g, g, r, ALU.mult))
                ch(red(gy[:], g, AX.X, ALU.add))
                ch(dve.reciprocal(gy[:], gy[:]))
                ch(tt(g, g, gy[:].unsqueeze(2).to_broadcast([P, NT, E]), ALU.mult))
                dve.sem_inc(s(f"gates_ready{m}"), 1)

            def add_experts(m, E):
                dve.sem_inc(s(f"y_room{m}"), BIG_TILES)
                dve.sem_inc(s(f"acc_done{m}"), 1)
                with dve.Fori(0, E) as e:
                    with dve.Fori(0, GROUPS) as g:
                        for a in range(BIG_TILES):
                            n = (e * GROUPS + g) * BIG_TILES + a
                            t = g * BIG_TILES + a
                            dve.wait_ge(s(f"mm2_{m}"), n + 1)
                            dve.wait_ge(s(f"acc_done{m}"), n + 1)
                            xv = X[:, bass.ds(t, 1), :].rearrange("p a c -> p (a c)")
                            dve.scalar_tensor_tensor(out=xv, in0=ps[4 + a % 4][:, 0:D], scalar=gates[:, bass.ds(t, 1), bass.ds(e, 1)].rearrange("p a c -> p (a c)"),
                                                     in1=xv, op0=ALU.mult, op1=ALU.add).then_inc(s(f"acc_done{m}"), 1)
                            dve.wait_ge(s(f"acc_done{m}"), n + 2)
                            dve.sem_inc(s(f"y_room{m}"), 1)

            top2(0, E0, lower0)
            dve.sem_inc(s("moe_room0"), 1)
            add_experts(0, E0)
            dve.sem_inc(s("rel_room"), 1)

            ch(dve.memset(agg_c, 0.0))
            layer_norm("rel")
            dve.wait_ge(s("sorted_in_c"), 16)
            add_up("rel", TC, sorted_c, tile_blk_c, agg_c, D, True)
            ch(dve.scalar_tensor_tensor(out=X[:, 0:NT, :], in0=agg_c, scalar=0.0, in1=X[:, 0:NT, :], op0=ALU.max, op1=ALU.add))
            dve.sem_inc(s("moe_room1"), 1)
            layer_norm("gate")
            dve.wait_ge(s("gate_copied"), NT)
            ch(tt(gates[:], gates[:], bgate_b[:].unsqueeze(1).to_broadcast([P, NT, E1]), ALU.add))
            top2(1, E1, lower1)
            add_experts(1, E1)


_INS = ['x', 'src', 'dst', 'edge_type_8', 'edge_weight', 'L0_gnn_weight', 'L0_gnn_attn_l', 'L0_gnn_attn_r', 'L0_ffn_W_gat',
        'L0_ffn_att_src', 'L0_ffn_att_dst', 'L0_ffn_b_gat', 'L0_ffn_ln_gamma', 'L0_ffn_ln_beta', 'L0_ffn_W1', 'L0_ffn_b1',
        'L0_ffn_W2', 'L0_ffn_b2', 'L0_ffn_edge_index', 'L1_gnn_weight', 'L1_ffn_Wg', 'L1_ffn_bg', 'L1_ffn_W1', 'L1_ffn_b1',
        'L1_ffn_W2', 'L1_ffn_b2']


def kernel(**inputs):
    import numpy as _np
    import concourse.bacc as _bacc
    from concourse import mybir as _mybir
    from concourse.bass_utils import run_bass_kernel_spmd as _run

    nc = _bacc.Bacc("TRN2", target_bir_lowering=False, num_devices=1)
    arrays, args = {}, []
    for name in _INS:
        a = _np.ascontiguousarray(inputs[name])
        arrays[f"in_{name}"] = a
        args.append(nc.dram_tensor(f"in_{name}", a.shape, _mybir.dt.from_np(a.dtype), kind="ExternalInput").ap())
    args.append(nc.dram_tensor("out_0", inputs['x'].shape, _mybir.dt.float32, kind="ExternalOutput").ap())
    graph_layers(nc, *args)
    r = _run(nc, [arrays], core_ids=[0])
    return r.results[0]["out_0"]
```

```python
from contextlib import ExitStack

import concourse.bass as bass
from concourse import mybir

F32 = mybir.dt.float32
BF16 = mybir.dt.bfloat16
I32 = mybir.dt.int32
ALU = mybir.AluOpType
ACT = mybir.ActivationFunctionType
AX = mybir.AxisListType
RMAX = bass.bass_isa.ReduceOp.max

P = 128
ROW, BLOCK_BITS, LANE_MASK = 4, 7, 127
BIG_TILES = 5


class Chain:

    def __init__(self, eng, sem):
        self.eng, self.sem, self.n = eng, sem, 0

    def __call__(self, ins):
        ins.then_inc(self.sem, 1)
        self.n = self.n + 1
        self.eng.wait_ge(self.sem, self.n)


def graph_layers(nc, x, src, dst, etype, eweight, w_gat, attn_l, attn_r, w_score, att_src, att_dst, b_gat, ln_gamma,
                 ln_beta, moe0_w1, moe0_b1, moe0_w2, moe0_b2, edges0, w_rel, w_gate, b_gate, moe1_w1, moe1_b1,
                 moe1_w2, moe1_b2, out):
    N, D = x.shape
    KT = D // P
    NB = -(-N // P)
    NT = NB + NB % 2
    FULL, REST = N // P, N % P
    HEADS = attn_l.shape[0]
    HD = D // HEADS
    SH, E0 = att_src.shape
    SC = SH * E0
    R = w_rel.shape[0]
    E1 = w_gate.shape[1]
    F0, F1 = moe0_w1.shape[2] // P, moe1_w1.shape[2] // P
    EB, EC = edges0.shape[1], src.shape[0]
    CB = EB // P
    CC = -(-EC // (8 * P)) * 8
    TB = -(-((CB * P + NB * (P - 1)) // P) // 8) * 8
    TC = -(-((CC * P + NB * (P - 1)) // P) // 8) * 8
    GROUPS = NB // BIG_TILES
    MP = 2 * P
    MT = (2 * N + E1 * (MP - 1)) // MP
    MT += MT % 2
    MROWS = MT * MP
    GT = BIG_TILES * P
    HALF = GT // 2
    assert D == 2 * P and NB % BIG_TILES == 0 and NB % 2 and CB * P == EB and CB % 8 == 0

    tab_val = nc.dram_tensor("tab_val", (NT * P, D + HEADS), F32, kind="Internal").ap()
    tab_left = nc.dram_tensor("tab_left", (NT * P, HEADS), F32, kind="Internal").ap()
    tab_src = nc.dram_tensor("tab_src", (NT * P, SC + SH), F32, kind="Internal").ap()
    tab_dst = nc.dram_tensor("tab_dst", (NT * P, 2 * SH), F32, kind="Internal").ap()
    tab_rel = nc.dram_tensor("tab_rel", (NT * P * R, D), F32, kind="Internal").ap()
    tok_in = nc.dram_tensor("tok_in", (MROWS + 2 * P, D), F32, kind="Internal").ap()
    tok_out = nc.dram_tensor("tok_out", (MROWS + 2 * P, D), F32, kind="Internal").ap()
    rec_b = nc.dram_tensor("rec_b", (P * TB, ROW), F32, kind="Internal").ap()
    rec_c = nc.dram_tensor("rec_c", (P * TC, ROW), F32, kind="Internal").ap()

    with ExitStack() as ctx:
        def sb(name, shape, dt=F32):
            return ctx.enter_context(nc.sbuf_tensor(name, shape, dt))

        def sem(name):
            return ctx.enter_context(nc.semaphore(name))

        ps = [ctx.enter_context(nc.psum_tensor(f"bank{i}", [P, 512], F32)) for i in range(8)]

        X = sb("X", [P, NT, D])
        ident = sb("ident", [P, P])
        iota_row = sb("iota_row", [P, P])
        before = sb("before", [P, P], BF16)
        upto = sb("upto", [P, P], BF16)
        ones_b = sb("ones_b", [P, P], BF16)
        ones_f = sb("ones_f", [P, P])
        iota_blk = sb("iota_blk", [P, NB])
        iota_tile = sb("iota_tile", [1, TC])
        lower0 = sb("lower0", [P, E0, E0])
        lower1 = sb("lower1", [P, E1, E1])
        xn = sb("xn", [P, 2, D])
        xTs = sb("xTs", [P, 2, KT, P])
        rows = sb("rows", [P, 2, D + 2 * HEADS])
        stats = sb("stats", [P, NT, 6])
        mean = sb("mean", [P, NT])
        var = sb("var", [P, NT])
        tmpn = sb("tmpn", [P, NT])
        rstd = sb("rstd", [P, NT])
        sorted_b = sb("sorted_b", [P, TB, ROW])
        sorted_c = sb("sorted_c", [P, TC, ROW])
        tile_blk_b = sb("tile_blk_b", [1, TB], I32)
        tile_blk_c = sb("tile_blk_c", [1, TC], I32)
        pick = sb("pick", [P, 2, 8], I32)
        pick_tok = sb("pick_tok", [P, BIG_TILES, 2], I32)
        place = sb("place", [P, NT, 2], I32)
        gate2 = sb("gate2", [P, NT, 2])
        chosen = sb("chosen", [P, NT, E1])
        chosen_b = sb("chosen_b", [P, NT, E1], BF16)
        here = sb("here", [P, NT])
        away = sb("away", [P, 2])
        node_id = sb("node_id", [P, NT])
        expert_of = sb("expert_of", [1, MT], I32)
        pick_val = sb("pick_val", [P, 2, BIG_TILES, 2], I32)
        left = sb("left", [P, 2, BIG_TILES, HEADS])
        share = sb("share", [P, 2, BIG_TILES, HEADS])
        share_of = sb("share_of", [P, 2, BIG_TILES])
        index_src = sb("index_src", [P, TB], I32)
        index_dst = sb("index_dst", [P, TB], I32)
        index_rel = sb("index_rel", [P, TC], I32)
        got = sb("got", [P, 10, D + HEADS])
        hot = sb("hot", [P, 4, P])
        diag = sb("diag", [P, 4, SH, P])
        shifted = sb("shifted", [P, 4, SH])
        tile_max = sb("tile_max", [P, 4, SH])
        logit = sb("logit", [P, 2, 8, SH])
        message = sb("message", [P, 2, 8, SC + SH])
        ends = sb("ends", [P, NT, 2], I32)
        al_b = sb("al_b", [P, D])
        ar_b = sb("ar_b", [P, D])
        y_plus = sb("y_plus", [P, 2, D])
        asrc_b = sb("asrc_b", [P, SC])
        adst_b = sb("adst_b", [P, SC])
        bg_b = sb("bg_b", [P, SC])
        gamma_b = sb("gamma_b", [P, SC])
        beta_b = sb("beta_b", [P, SC])
        bgate_b = sb("bgate_b", [P, E1])
        wg_sb = sb("wg_sb", [P, KT, D + 2 * HEADS])
        ws_sb = sb("ws_sb", [P, KT, SC])
        wgate_sb = sb("wgate_sb", [P, KT, E1])
        b1_0 = sb("b1_0", [P, E0, F0])
        b1_1 = sb("b1_1", [P, E1, F1])
        b2_0 = sb("b2_0", [P, E0, D])
        b2_1 = sb("b2_1", [P, E1, D])
        nodes = sb("nodes", [P, NT, SC + SH])
        adm = sb("adm", [P, NT, 2 * SH])
        gates = sb("gates", [P, NT, E1])
        gx = sb("gx", [P, NT, E1])
        gy = sb("gy", [P, NT])
        eps = sb("eps", [P, 1])
        low = sb("low", [P, SH])
        nlow = sb("nlow", [P, SH])

        rec_slot = sb("rec_slot", [P, 2, 8, ROW])
        bf2 = sb("bf2", [1, TC])
        small2 = sb("small2", [P, NT, SH])
        ARENA = 23296
        arena = sb("arena", [P, ARENA])

        def part(at, *dims, dt=F32):
            n = 1
            for d in dims:
                n *= d
            words = n if dt != BF16 else n // 2
            assert at + words <= ARENA, (at, words)
            v = arena[:, at:at + words]
            if dt != F32:
                v = v.bitcast(dt)
            if len(dims) == 2:
                v = v.rearrange("p (a b) -> p a b", b=dims[1])
            if len(dims) == 3:
                v = v.rearrange("p (a b c) -> p a b c", b=dims[1], c=dims[2])
            return v

        def bucket_parts(C, edges_at, pk_at):
            ohv = part(0, NB, C, dt=BF16)
            cnt = part(NB * C // 2, NB, C)
            assert NB * C // 2 * 3 <= 14720
            di, si, ti = (part(edges_at + q * C, C, dt=I32) for q in range(3))
            wi = part(edges_at + 3 * C, C)
            pk, addr = part(pk_at, C, ROW), part(pk_at, C, ROW, dt=I32)[:, :, 3]
            return ohv, cnt, pk, di, si, ti, addr, wi

        bnum = sb("bnum", [P, NB])
        bint = sb("bint", [P, NB], I32)
        bnt = sb("bnt", [P, NB])
        bend = sb("bend", [P, NB])
        badj = sb("badj", [P, NB])
        bz = sb("bz", [P, 512])
        prod = part(0, BIG_TILES * D)
        mixed_v = part(BIG_TILES * D, BIG_TILES, HD)
        XT = part(0, KT, NT * P)
        R0 = KT * NT * P
        edge1 = part(R0, TB, SC + SH)
        agg_b = part(R0 + TB * (SC + SH), NT, SC + SH)
        agg_c = part(R0, NT, D)
        wrel = part(R0 + NT * D, KT, R * D)
        PK_C = ARENA - CC * ROW
        assert R0 + NT * D + KT * R * D + 4 * 1024 <= PK_C
        rel_out = [part(R0 + NT * D + KT * R * D + q * 1024, 2, 512) for q in range(4)]
        w1v, w2v = {}, {}
        half = KT * F0 * P
        w1v[0] = [part(R0 + u * 2 * half, KT, F0 * P) for u in range(2)]
        w2v[0] = [part(R0 + u * 2 * half + half, F0, D) for u in range(2)]
        R1 = R0 + 4 * half
        hT = part(R1, F0, GT)
        PAIR0 = 16384
        ranked = part(16384 + 2 * NT * E1 * E1, NT, 2, E1)
        pairs = part(PAIR0, NT, E1 * E1)
        pairs2 = part(PAIR0 + NT * E1 * E1, NT, E1 * E1)
        half = KT * F1 * P
        w1v[1] = [part(u * 2 * half, KT, F1 * P) for u in range(2)]
        w2v[1] = [part(u * 2 * half + half, F1, D) for u in range(2)]
        M0 = 4 * half
        tok = [part(M0 + u * 2 * D, 2, D) for u in range(2)]
        tokT = [part(M0 + 4 * D + u * KT * MP, KT, MP) for u in range(2)]
        hid = [part(M0 + 4 * D + 2 * KT * MP + u * F1 * MP, F1, MP) for u in range(2)]
        M1 = M0 + 4 * D + 2 * KT * MP + 2 * F1 * MP
        res = [part(M1 + u * 2 * D, 2, D) for u in range(2)]
        mb1 = [part(M1 + 4 * D + u * F1, F1) for u in range(2)]
        M2 = M1 + 4 * D + 2 * F1
        mb2 = [part(M2 + u * D, D) for u in range(2)]
        assert M2 + 2 * D <= PAIR0 and R1 + F0 * GT <= PAIR0

        block = ctx.enter_context(nc.Block())

        def in_groups(eng, n, body):
            for g in range(3):
                body(g, g % 2, True)
            with eng.Fori(1, (n - 1) // 2) as i:
                body(i * 2 + 1, 1, False)
                body(i * 2 + 2, 0, False)
            if n % 2 == 0:
                body(n - 1, 1, False)

        S = {}

        def s(name):
            if name not in S:
                S[name] = sem(name)
            return S[name]

        ASKS = {n: i + 1 for i, n in enumerate(("std_val", "std_score", "self_exp", "std_agg", "top_exp0",
                                                "std_rel", "std_gate", "top_exp1"))}
        STAGES = (("scatter_b", 8, 16, CB // 8), ("val", BIG_TILES, 32, GROUPS), ("src", 8, 16, TB // 8), ("dst", 8, 16, TB // 8),
                  ("scatter_c", 8, 16, CC // 8), ("rel", 8, 16, TC // 8), ("put", BIG_TILES, 32, GROUPS), ("take", BIG_TILES, 32, GROUPS))
        START, END, at = {}, {}, [0] * 8
        for name, slots, step, turns in STAGES:
            START[name] = list(at)
            at = [v + (step * turns if q < slots else 0) for q, v in enumerate(at)]
            END[name] = list(at)
        PICK_BASE, at = {}, [0, 0]
        for name, n in (("scatter_b", CB // 8), ("val", GROUPS), ("src", TB // 8), ("dst", TB // 8), ("scatter_c", CC // 8), ("rel", TC // 8)):
            PICK_BASE[name] = tuple(at)
            at = [at[0] + 16 * (n - n // 2), at[1] + 16 * (n // 2)]
        FEED_PARTS = (0, 20, 34, CC // 8)
        NBUCK = {"b": (CB, TB, 16), "c": (CC, TC, 14)}
        for C, _, w in NBUCK.values():
            assert C % w == 0 and NB * w <= 512 and C <= 512
        EDGES_B = 14720 + 4 * CC
        parts = {"b": bucket_parts(CB, EDGES_B, EDGES_B + 4 * CB), "c": bucket_parts(CC, 14720, PK_C)}
        chunk = part(EDGES_B + 8 * CB, 2, CC)
        bh = part(EDGES_B + 8 * CB + 2 * CC, CC, dt=BF16)
        assert EDGES_B + 8 * CB + 3 * CC <= PK_C
        rec = {"b": rec_b, "c": rec_c}
        srt = {"b": sorted_b, "c": sorted_c}
        LN_STAGES = ("val", "score", "rel", "gate")
        WIDTH = {"val": D + 2 * HEADS, "score": SC, "rel": R * D, "gate": E1}

        @block.sync
        def _(sp):
            sp.wait_ge(s("x_zeroed"), 1)
            for k in "bc":
                C, T, _ = NBUCK[k]
                ohv, cnt, pk, di, si, ti, addr, wi = parts[k]
                if k == "b":
                    sp.dma_start(si, edges0[0].rearrange("(p c) -> p c", p=P)).then_inc(s("edges_in_b"), 16)
                    sp.dma_start(di, edges0[1].rearrange("(p c) -> p c", p=P)).then_inc(s("edges_in_b"), 16)
                else:
                    full, rest = EC // C, EC % C
                    for o, i in ((si, src), (di, dst), (ti, etype), (wi, eweight)):
                        sp.dma_start(o[0:full, :], i[0:full * C].rearrange("(p c) -> p c", c=C)).then_inc(s("edges_in_c"), 16)
                        sp.dma_start(o[full:full + 1, 0:rest], i[full * C:EC].rearrange("(o c) -> o c", o=1)).then_inc(s("edges_in_c"), 16)
            sp.dma_start(X[:, 0:FULL, :], x[0:FULL * P, :].rearrange("(t p) d -> p t d", p=P)).then_inc(s("x_in"), 16)
            sp.dma_start(X[0:REST, FULL, :], x[FULL * P:N, :]).then_inc(s("x_in"), 16)
            for c, v in ((0, dst), (1, src)):
                sp.dma_start(ends[:, 0:FULL, c], v[0:FULL * P].rearrange("(t p) -> p t", p=P), allow_slow_non_contiguous=True).then_inc(s("ends_in"), 16)
                sp.dma_start(ends[0:REST, FULL:FULL + 1, c], v[FULL * P:N].rearrange("(p o) -> p o", o=1), allow_slow_non_contiguous=True).then_inc(s("ends_in"), 16)
            flat = lambda a: a.rearrange("a b -> (a b)")
            loads = [
                (al_b[:], flat(attn_l).partition_broadcast(P)), (ar_b[:], flat(attn_r).partition_broadcast(P)),
                (asrc_b[:], flat(att_src).partition_broadcast(P)), (adst_b[:], flat(att_dst).partition_broadcast(P)),
                (bg_b[:], b_gat.partition_broadcast(P)), (gamma_b[:], ln_gamma.partition_broadcast(P)),
                (beta_b[:], ln_beta.partition_broadcast(P)), (bgate_b[:], b_gate.partition_broadcast(P)),
                (wg_sb[:, :, 0:D], w_gat.rearrange("(k p) n -> p k n", p=P)),
                (ws_sb[:], w_score.rearrange("(k p) n -> p k n", p=P)),
                (wgate_sb[:], w_gate.rearrange("(k p) n -> p k n", p=P)),
                (b2_0[:].rearrange("p e d -> p (e d)"), flat(moe0_b2).partition_broadcast(P)),
                (b2_1[:].rearrange("p e d -> p (e d)"), flat(moe1_b2).partition_broadcast(P)),
            ] + [(b1_0[:, e, :], moe0_b1[e].rearrange("(f p) -> p f", p=P)) for e in range(E0)] \
              + [(b1_1[:, e, :], moe1_b1[e].rearrange("(f p) -> p f", p=P)) for e in range(E1)]
            for o, i in loads:
                sp.dma_start(o, i, allow_slow_non_contiguous=True).then_inc(s("params_in"), 16)
            S["n_params"] = 16 * len(loads)
            for k in "bc":
                sp.wait_ge(s(f"edges_zeroed_{k}"), 1)
                sp.dma_start(rec[k].rearrange("(p t) r -> p t r", p=P), srt[k][:]).then_inc(s(f"pad_out_{k}"), 16)
            zero = bz[:].unsqueeze(1).to_broadcast([P, MROWS * D // P // 512, 512])
            sp.wait_ge(s("zeros"), 1)
            sp.dma_start(tok_in[0:MROWS, :].rearrange("(p a b) d -> p a (b d)", p=P, b=2), zero).then_inc(s("tok_zeroed"), 16)
            sp.dma_start(tok_out[MROWS:MROWS + 2 * P, :].rearrange("(p b) d -> p (b d)", p=P), bz[:]).then_inc(s("tok_zeroed"), 16)

            def feed_group(key, g, w, early, slots, source):
                if not (early and g < 2):
                    for q in range(BIG_TILES if key == "val" else 8):
                        sp.wait_ge(s(f"got{q}"), START[key][q] + (32 if key == "val" else 16) * (g - 1))
                        sp.sem_inc(s("sp_turn"), 1)
                sp.dma_start(slots, source).then_inc(s(f"picked{w}"), 16)

            def feed_records(k, first, last):
                def body(g, w, early):
                    feed_group(f"scatter_{k}", g, w, early, rec_slot[:, w], parts[k][2][:, bass.ds(g * 8, 8), :])
                if first == 0:
                    sp.wait_ge(s("places"), 1 if k == "b" else 2)
                    body(0, 0, True)
                    body(1, 1, True)
                    first = 2
                with sp.Fori(first // 2, last // 2) as i:
                    for u in range(2):
                        body(i * 2 + u, u, False)
                if last % 2:
                    body(last - 1, 0, False)

            def sorted_back(k):
                for q in range(8):
                    sp.wait_ge(s(f"got{q}"), END[f"scatter_{k}"][q])
                sp.wait_ge(s(f"pad_out_{k}"), 16)
                sp.dma_start(srt[k][:], rec[k].rearrange("(p t) r -> p t r", p=P)).then_inc(s(f"sorted_in_{k}"), 16)
            feed_records("b", 0, CB // 8)
            sorted_back("b")
            sp.wait_ge(s("ends_in"), 64)

            def feed_val(g, w, early):
                feed_group("val", g, w, early, pick_val[:, w], ends[:, bass.ds(g * BIG_TILES, BIG_TILES), :])
            in_groups(sp, GROUPS, feed_val)
            def feed(key, T, index):
                def body(g, w, early):
                    feed_group(key, g, w, early, pick[:, w, :], index[:, bass.ds(g * 8, 8)])
                in_groups(sp, T // 8, body)

            sp.wait_ge(s("nodes_ready"), 1)
            sp.dma_start(tab_src.rearrange("(t p) r -> p t r", p=P), nodes[:]).then_inc(s("src_out"), 16)
            sp.wait_ge(s("index_ready"), 1)
            feed("src", TB, index_src)
            for q in range(8):
                sp.wait_ge(s(f"got{q}"), END["src"][q])
            sp.wait_ge(s("maxima_ready"), 1)
            sp.dma_start(tab_dst.rearrange("(t p) r -> p t r", p=P), adm[:]).then_inc(s("dst_out"), 16)
            feed("dst", TB, index_dst)
            def load_expert(m, e, w1, w2):
                u = e % 2
                sp.dma_start(w1v[m][u], w1[e].rearrange("(k p) f -> p k f", p=P)).then_inc(s(f"w_in{m}{u}"), 16)
                sp.dma_start(w2v[m][u], w2[e].rearrange("(f p) d -> p f d", p=P)).then_inc(s(f"w_in{m}{u}"), 16)
            assert E0 == 4
            for q in range(8):
                sp.wait_ge(s(f"got{q}"), END["dst"][q])
            sp.wait_ge(s("moe_room0"), 1)
            load_expert(0, 0, moe0_w1, moe0_w2)
            load_expert(0, 1, moe0_w1, moe0_w2)
            wr = wrel.rearrange("p k (r n) -> p k r n", r=R)
            for k2 in range(KT):
                sp.dma_start(wr[:, k2], w_rel[:, k2 * P:(k2 + 1) * P, :].rearrange("r p n -> p r n")).then_inc(s("wrel_in"), 16)
            feed_records("c", FEED_PARTS[0], FEED_PARTS[1])
            for e in (2, 3):
                sp.wait_ge(s("expert_done0"), e - 1)
                load_expert(0, e, moe0_w1, moe0_w2)
                feed_records("c", FEED_PARTS[e - 1], FEED_PARTS[e])
            sorted_back("c")
            tr = tab_rel.rearrange("(n r) d -> n (r d)", r=R)

            def store_rel(i, first):
                for u in range(2):
                    t = i * 2 + u
                    for q in range(4):
                        sp.wait_ge(s(f"rel_ready{q % 2}"), t * 2 + q // 2 + 1)
                        sp.dma_start(tr[bass.ds(t * P, P), q * 512:(q + 1) * 512], rel_out[q][:, u, :]).then_inc(s(f"rel_out{u}"), 16)
            store_rel(0, True)
            with sp.Fori(1, NT // 2) as i:
                store_rel(i, False)
            sp.wait_ge(s("index_ready"), 2)
            feed("rel", TC, index_rel)
            sp.wait_ge(s("moe_room1"), 1)
            for k2 in range(BIG_TILES):
                sp.wait_ge(s(f"got{k2}"), END["put"][k2])

            def store_tile(j, u):
                sp.wait_ge(s("y_copied"), j * 2 + 2)
                sp.dma_start(tok_out[bass.ds(j * MP, MP), :].rearrange("(b p) d -> p b d", b=2), res[u]).then_inc(s(f"y_out{u}"), 16)

            def tile(i, first):
                for u in range(2):
                    j = i * 2 + u
                    if not first:
                        sp.wait_ge(s("tile_done"), j - 1)
                        sp.sem_inc(s("sp_turn"), 1)
                    e = sp.value_load(expert_of[0:1, bass.ds(j, 1)], min_val=0, max_val=E1 - 1)
                    arrived = s(f"tile_in{u}")
                    sp.dma_start(tok[u], tok_in[bass.ds(j * MP, MP), :].rearrange("(b p) d -> p b d", b=2)).then_inc(arrived, 16)
                    sp.dma_start(w1v[1][u], moe1_w1[bass.ds(e, 1)].rearrange("a (k p) f -> p (a k) f", p=P)).then_inc(arrived, 16)
                    sp.dma_start(mb1[u], b1_1[:, bass.ds(e, 1), :].rearrange("p a f -> p (a f)")).then_inc(arrived, 16)
                    sp.dma_start(w2v[1][u], moe1_w2[bass.ds(e, 1)].rearrange("a (f p) d -> p (a f) d", p=P)).then_inc(arrived, 16)
                    if not first:
                        store_tile(j - 2, u)
                    sp.dma_start(mb2[u], b2_1[:, bass.ds(e, 1), :].rearrange("p a d -> p (a d)")).then_inc(arrived, 16)
            tile(0, True)
            with sp.Fori(1, MT // 2) as i:
                tile(i, False)
            for j in range(MT - 2, MT):
                store_tile(j, j % 2)
            with sp.Fori(0, GROUPS - 1) as i:
                sp.wait_ge(s("mixed"), (i + 1) * 2 * BIG_TILES)
                sp.sem_inc(s("sp_turn"), 1)
                sp.dma_start(out[bass.ds(i * GT, GT), :].rearrange("(t p) d -> p t d", p=P), X[:, bass.ds(i * BIG_TILES, BIG_TILES), :]).then_inc(s("result_out"), 16)
            sp.wait_ge(s("mixed"), NB * 2)
            t0 = (GROUPS - 1) * BIG_TILES
            sp.dma_start(out[t0 * P:FULL * P, :].rearrange("(t p) d -> p t d", p=P), X[:, t0:FULL, :]).then_inc(s("result_out"), 16)
            sp.dma_start(out[FULL * P:N, :], X[0:REST, FULL, :]).then_inc(s("result_out"), 16)
            sp.wait_ge(s("result_out"), 16 * (GROUPS + 1))

        n_params = S.pop("n_params")

        @block.gpsimd
        def _(pool):
            ch = Chain(pool, s("pool_chain"))
            ch(pool.memset(ident[:], 0.0))
            ch(pool.affine_select(out=ident[:], in_=ident[:], compare_op=ALU.not_equal, fill=1.0, base=0,
                                  pattern=[[-1, P]], channel_multiplier=1))
            ch(pool.memset(ones_f[:], 1.0))
            ch(pool.memset(ones_b[:], 1.0))
            ch(pool.affine_select(out=before[:], in_=ones_b[:], compare_op=ALU.is_gt, fill=0.0, base=0,
                                  pattern=[[1, P]], channel_multiplier=-1))
            ch(pool.memset(upto[:], -1.0))
            ch(pool.affine_select(out=upto[:], in_=upto[:], compare_op=ALU.is_gt, fill=0.0, base=1,
                                  pattern=[[-1, P]], channel_multiplier=1))
            ch(pool.iota(iota_row[:], [[1, P]], base=0, channel_multiplier=0, allow_small_or_imprecise_dtypes=True))
            ch(pool.iota(iota_blk[:], [[1, NB]], base=0, channel_multiplier=0, allow_small_or_imprecise_dtypes=True))
            ch(pool.iota(iota_tile[:], [[1, TC]], base=0, channel_multiplier=0, allow_small_or_imprecise_dtypes=True))
            ch(pool.iota(node_id[:], [[P, NT]], base=0, channel_multiplier=1, allow_small_or_imprecise_dtypes=True))
            for low_m, E in ((lower0, E0), (lower1, E1)):
                ch(pool.memset(low_m[:], 1.0))
                ch(pool.affine_select(out=low_m[:], in_=low_m[:], compare_op=ALU.is_gt, fill=0.0, base=0,
                                      pattern=[[1, E], [-1, E]], channel_multiplier=0))
            pool.memset(eps[:], 1e-5).then_inc(s("consts"), 1)

            def scatter(k):
                base = PICK_BASE[f"scatter_{k}"]

                def body(g, w, early):
                    pool.wait_ge(s(f"picked{w}"), base[w] + 16 * (g // 2) + 16 if early else base[w] + 8 * (g - w) + 16)
                    for q in range(8):
                        if not (early and g < 1):
                            pool.wait_ge(s(f"got{q}"), START[f"scatter_{k}"][q] + 16 * g)
                        pool.sem_inc(s("pool_turn"), 1)
                        pool.indirect_dma_start(rec[k], bass.IndirectOffsetOnAxis(ap=rec_slot[:, w, q, 3:4].bitcast(I32), axis=0),
                                                rec_slot[:, w, q, :], None).then_inc(s(f"got{q}"), 16)
                pool.wait_ge(s(f"pad_out_{k}"), 16)
                in_groups(pool, NBUCK[k][0] // 8, body)
            scatter("b")

            for u in range(2):
                pool.wait_ge(s(f"val_out{u}"), 32 * (NT // 2))

            def gather_val(g, w, early):
                base = PICK_BASE["val"]
                pool.wait_ge(s(f"picked{w}"), base[w] + 16 * (g // 2) + 16 if early else base[w] + 8 * (g - w) + 16)
                for q in range(BIG_TILES):
                    if not (early and g < 1):
                        pool.wait_ge(s(f"got{q}"), START["val"][q] + 32 * g)
                    if not (early and g < 2):
                        pool.wait_ge(s("val_used"), g - 1)
                    pool.sem_inc(s("pool_turn"), 1)
                    pool.indirect_dma_start(got[:, w * BIG_TILES + q, 0:D + HEADS], None, tab_val,
                                            bass.IndirectOffsetOnAxis(ap=pick_val[:, w, q, 0:1], axis=0)).then_inc(s(f"got{q}"), 16)
                    pool.indirect_dma_start(left[:, w, q, :], None, tab_left,
                                            bass.IndirectOffsetOnAxis(ap=pick_val[:, w, q, 1:2], axis=0)).then_inc(s(f"got{q}"), 16)
            in_groups(pool, GROUPS, gather_val)

            pool.wait_ge(s("low_ready"), 1)
            pool.partition_all_reduce(low[:], nlow[:], P, RMAX).then_inc(s("low_all"), 1)

            def gathers(key, T, table, width, used):
                def body(g, w, early):
                    pool.wait_ge(s(f"picked{w}"), PICK_BASE[key][w] + 16 * (g // 2) + 16 if early else PICK_BASE[key][w] + 8 * (g - w) + 16)
                    for q in range(8):
                        if not (early and g < 1):
                            for name, per in used:
                                pool.wait_ge(s(name), g * 2 + q // 4 - 1 if per == 4 else g * 8 + q - 7)
                        pool.sem_inc(s("pool_turn"), 1)
                        pool.indirect_dma_start(got[:, q, 0:width], None, table,
                                                bass.IndirectOffsetOnAxis(ap=pick[:, w, q:q + 1], axis=0)).then_inc(s(f"got{q}"), 16)
                in_groups(pool, T // 8, body)
            pool.wait_ge(s("val_used"), GROUPS)
            pool.wait_ge(s("src_out"), 16)
            gathers("src", TB, tab_src, SC + SH, [("src_kept", 4), ("src_shifted", 1)])
            pool.wait_ge(s("dst_out"), 16)
            pool.wait_ge(s("src_kept"), TB // 4)
            pool.wait_ge(s("src_shifted"), TB)
            gathers("dst", TB, tab_dst, 2 * SH, [("logits_used", 1)])
            scatter("c")
            for u in range(2):
                pool.wait_ge(s(f"rel_out{u}"), 64 * (NT // 2))
            pool.wait_ge(s("logits_used"), TB)
            gathers("rel", TC, tab_rel, D, [("rel_spread", 1)])

            pool.wait_ge(s("tok_zeroed"), 32)

            def put(i, first):
                for a in range(BIG_TILES):
                    pool.wait_ge(s("tok_ready"), i * BIG_TILES + a + 1)
                    pool.sem_inc(s("pool_turn"), 1)
                    for c in range(2):
                        pool.indirect_dma_start(tok_in, bass.IndirectOffsetOnAxis(ap=pick_tok[:, a, c:c + 1], axis=0),
                                                got[:, a, 0:D], None).then_inc(s(f"got{a}"), 16)
            with pool.Fori(0, GROUPS) as i:
                put(i, False)
            for u in range(2):
                pool.wait_ge(s(f"y_out{u}"), 16 * (MT // 2))

            def take(i, first):
                for a in range(BIG_TILES):
                    pool.wait_ge(s("take_ready"), i * BIG_TILES + a + 1)
                    pool.sem_inc(s("pool_turn"), 1)
                    for c in range(2):
                        pool.indirect_dma_start(got[:, 2 * a + c, 0:D], None, tok_out,
                                                bass.IndirectOffsetOnAxis(ap=pick_tok[:, a, c:c + 1], axis=0)).then_inc(s(f"got{a}"), 16)
            with pool.Fori(0, GROUPS) as i:
                take(i, False)

        @block.scalar
        def _(act):
            def settle():
                act.sem_inc(s("act_turn"), 1)

            act.wait_ge(s("consts"), 1)

            def std(k):
                act.wait_ge(s("asked"), ASKS[f"std_{k}"])
                act.activation(var[:], var[:], ACT.Sqrt, bias=eps[:, 0:1]).then_inc(s("answered"), 1)

            def copies(k, keep):
                def transposed(t, u, early):
                    act.wait_ge(s(f"tp_{k}"), t + 1)
                    if not early:
                        act.wait_ge(s("rel_mm" if k == "rel" else f"prod_{k}"), (t - 1) * 4 if k == "rel" else t - 1)
                    settle()
                    v = ps[u][:, 0:D].rearrange("p (k n) -> p k n", k=KT)
                    if keep:
                        act.copy(XT[:, :, bass.ds(t * P, P)], v)
                    act.copy(xTs[:, u, :, :], v).then_inc(s(f"xT_{k}"), 1)

                def results(t, u, early):
                    if k == "rel":
                        for q in (0, 2):
                            act.wait_ge(s("rel_mm"), t * 4 + q + 1)
                            if not early:
                                act.wait_ge(s(f"rel_out{u}"), 32 * (t - u))
                            settle()
                            act.copy(rel_out[q][:, u, :], ps[2 + q][:, :]).then_inc(s("rel_ready0"), 1)
                        return
                    act.wait_ge(s(f"prod_{k}"), t + 1)
                    if k == "val" and not early:
                        act.wait_ge(s(f"val_out{u}"), 16 * (t - u))
                    settle()
                    o = {"val": rows[:, u, :],
                         "score": nodes[:, bass.ds(t, 1), 0:SC].rearrange("p a c -> p (a c)"),
                         "gate": gates[:, bass.ds(t, 1), :].rearrange("p a c -> p (a c)")}[k]
                    act.copy(o, ps[2 + u][:, 0:WIDTH[k]]).then_inc(s(f"{k}_copied"), 1)
                    if k == "val":
                        act.wait_ge(s("val_copied"), t + 1)
                        settle()
                        act.dma_start(tab_val[bass.ds(t * P, P), :], rows[:, u, 0:D + HEADS]).then_inc(s(f"val_out{u}"), 16)
                        act.dma_start(tab_left[bass.ds(t * P, P), :], rows[:, u, D + HEADS:D + 2 * HEADS]).then_inc(s(f"val_out{u}"), 16)

                def both(i, first, last):
                    for u in range(2):
                        t = i * 2 + u
                        if not (last and u == 1):
                            transposed(t + 1, 1 - u, first and u == 0)
                        results(t, u, first)
                transposed(0, 0, True)
                both(0, True, False)
                with act.Fori(1, NT // 2 - 1) as i:
                    both(i, False, False)
                both(NT // 2 - 1, False, True)

            std("val")
            copies("val", False)
            def exps(g, w, early):
                act.wait_ge(s("val_z"), g + 1)
                act.activation(share[:, w], share[:, w], ACT.Exp).then_inc(s("val_e"), 1)
            in_groups(act, GROUPS, exps)

            std("score")
            copies("score", True)

            act.wait_ge(s("sorted_in_b"), 16)

            def src_rows(i, first):
                for q in range(8):
                    j = i * 8 + q
                    r = q % 4
                    act.wait_ge(s("src_shifted"), j + 1)
                    if not (first and q < 4):
                        act.wait_ge(s("spread"), j - 3)
                    settle()
                    for h in range(SH):
                        act.activation(diag[:, r, h, :], ident[:], ACT.Copy, scale=shifted[:, r, h:h + 1]).then_inc(s("diag_ready"), 1)
                    if r == 3:
                        for q2 in range(q - 3, q + 1):
                            act.wait_ge(s(f"got{q2}"), START["src"][q2] + i * 16 + 16)
                        settle()
                        act.copy(edge1[:, bass.ds(j - 3, 4), :], got[:, q - 3:q + 1, 0:SC + SH]).then_inc(s("src_kept"), 1)
            src_rows(0, True)
            with act.Fori(1, TB // 8) as i:
                src_rows(i, False)

            act.wait_ge(s("asked"), ASKS["self_exp"])
            act.activation(small2[:], small2[:], ACT.Exp).then_inc(s("answered"), 1)
            def weigh(i, w):
                act.wait_ge(s("logits"), i + 1)
                act.activation(logit[:, w], logit[:, w], ACT.Exp).then_inc(s("weights"), 1)
            weigh(0, 0)
            with act.Fori(0, (TB // 8 - 1) // 2) as i:
                weigh(i * 2 + 1, 1)
                weigh(i * 2 + 2, 0)
            act.wait_ge(s("asked"), ASKS["std_agg"])
            act.activation(gy[:], gy[:], ACT.Sqrt, bias=eps[:, 0:1]).then_inc(s("answered"), 1)
            act.wait_ge(s("asked"), ASKS["top_exp0"])
            act.activation(gates[:, :, 0:E0], gates[:, :, 0:E0], ACT.Exp).then_inc(s("answered"), 1)

            def hidden(m, E, FC, b1):
                act.sem_inc(s(f"h_room{m}"), 4)
                with act.Fori(0, E) as e:
                    with act.Fori(0, GROUPS) as g:
                        for f in range(FC):
                            for half in range(2):
                                n = ((e * GROUPS + g) * FC + f) * 2 + half
                                act.wait_ge(s(f"mm1_{m}"), n + 1)
                                if f == 0 and half == 0:
                                    act.wait_ge(s(f"group_done{m}"), e * GROUPS + g + 1)
                                settle()
                                act.activation(hT[:, f, half * HALF:(half + 1) * HALF], ps[(f * 2 + half) % 4][:, 0:HALF],
                                               ACT.Gelu, bias=b1[:, bass.ds(e, 1), f]).then_inc(s(f"h_room{m}"), 1)
            hidden(0, E0, F0, b1_0)
            std("rel")
            copies("rel", False)

            std("gate")
            copies("gate", False)
            act.wait_ge(s("asked"), ASKS["top_exp1"])
            act.activation(gates[:, :, 0:E1], gates[:, :, 0:E1], ACT.Exp).then_inc(s("answered"), 1)

            def token_tile(j, u, first):
                act.wait_ge(s("tokT_mm"), j + 1)
                if not first:
                    act.wait_ge(s("mid_mm"), F1 * (j - 1))
                settle()
                act.copy(tokT[u], ps[0][:, :].rearrange("p (k n) -> p k n", k=KT)).then_inc(s("tokT_ready"), 1)

            def gelus(j, u, first):
                if not first:
                    act.wait_ge(s("y_mm"), (j - 1) * 2)
                for f in range(F1):
                    act.wait_ge(s("mid_mm"), F1 * j + f + 1)
                    settle()
                    act.activation(hid[u][:, f, :], ps[1 + f % 4][:, 0:MP], ACT.Gelu, bias=mb1[u][:, f:f + 1]).then_inc(s("gelu_done"), 1)

            token_tile(0, 0, True)
            gelus(0, 0, True)
            token_tile(1, 1, True)
            gelus(1, 1, True)
            with act.Fori(1, MT // 2) as i:
                for u in range(2):
                    token_tile(i * 2 + u, u, False)
                    gelus(i * 2 + u, u, False)

        @block.tensor
        def _(pe):
            pe.wait_ge(s("consts"), 1)
            for k in "bc":
                C, T, w = NBUCK[k]
                ohv = parts[k][0]
                pe.wait_ge(s("hot_blocks"), NB if k == "b" else 2 * NB)

                def count(c, start, stop):
                    return pe.matmul(ps[4][:, 0:NB * w].rearrange("p (b c) -> p b c", c=w), ones_b[:], ohv[:, :, bass.ds(c * w, w)],
                                     start=start, stop=stop)
                count(0, True, False)
                with pe.Fori(1, C // w - 1) as c:
                    count(c, False, False)
                count(C // w - 1, False, True).then_inc(s("totals"), 1)

                base = 0 if k == "b" else NB

                def counts(n, u, first):
                    if not first:
                        pe.wait_ge(s("placed"), base + n - 1)
                    o = ohv[:, bass.ds(n, 1), :].rearrange("p a c -> p (a c)")
                    pe.matmul(ps[u][:, 0:C], ones_b[:], o, start=True, stop=True)
                    pe.matmul(ps[2 + u][:, 0:C], upto[:], o, start=True, stop=True).then_inc(s("block_sums"), 1)
                counts(0, 0, k == "b")
                counts(1, 1, k == "b")
                with pe.Fori(1, NB // 2) as i:
                    counts(i * 2, 0, False)
                    counts(i * 2 + 1, 1, False)
                counts(NB - 1, 0, False)

            def tiles(k, weights):
                W = WIDTH[k]

                def transpose(t, u, early):
                    pe.wait_ge(s(f"xn_{k}"), t + 1)
                    if not early:
                        pe.wait_ge(s(f"xT_{k}"), t - 1)
                    pe.transpose(ps[u][:, 0:P], xn[:, u, 0:P], ident[:])
                    pe.transpose(ps[u][:, P:2 * P], xn[:, u, P:2 * P], ident[:]).then_inc(s(f"tp_{k}"), 1)

                def product(t, u, early, very_first):
                    pe.wait_ge(s(f"xT_{k}"), t + 1)
                    if k == "rel":
                        for q in range(4):
                            if not very_first:
                                pe.wait_ge(s(f"rel_ready{q % 2}"), (t - 1) * 2 + q // 2 + 1)
                            for kt in range(KT):
                                mm = pe.matmul(ps[2 + q][:, :], xTs[:, u, kt, :], wrel[:, kt, q * 512:(q + 1) * 512],
                                               start=(kt == 0), stop=(kt == KT - 1))
                            mm.then_inc(s("rel_mm"), 1)
                        return
                    if not early:
                        pe.wait_ge(s(f"{k}_copied"), t - 1)
                    for kt in range(KT):
                        mm = pe.matmul(ps[2 + u][:, 0:W], xTs[:, u, kt, :], weights[:, kt, :],
                                       start=(kt == 0), stop=(kt == KT - 1))
                    mm.then_inc(s(f"prod_{k}"), 1)

                def both(i, first, last):
                    for u in range(2):
                        t = i * 2 + u
                        if not (last and u == 1):
                            transpose(t + 1, 1 - u, first and u == 0)
                        product(t, u, first, first and u == 0)
                transpose(0, 0, True)
                both(0, True, False)
                with pe.Fori(1, NT // 2 - 1) as i:
                    both(i, False, False)
                both(NT // 2 - 1, False, True)

            pe.wait_ge(s("params_in"), n_params)
            pe.wait_ge(s("attn_weights"), 1)
            pe.wait_ge(s("placed"), 2 * NB)
            tiles("val", wg_sb)
            tiles("score", ws_sb)

            def spread(i, first):
                for q in range(4):
                    j = i * 4 + q
                    pe.wait_ge(s("hot_b"), j + 1)
                    pe.wait_ge(s("diag_ready"), SH * j + SH)
                    if not first:
                        pe.wait_ge(s("spread_used"), j - 3)
                    pe.matmul(ps[q][:, :], hot[:, q, :], diag[:, q, :, :].rearrange("p h e -> p (h e)"), start=True, stop=True).then_inc(s("spread"), 1)
            spread(0, True)
            with pe.Fori(1, TB // 4) as i:
                spread(i, False)

            def msg_sums(i, w, first):
                for q in range(8):
                    j = i * 8 + q
                    if q == 0:
                        pe.wait_ge(s("messages"), i + 1)
                    pe.wait_ge(s("hot_msg"), j + 1)
                    if not (first and q < 4):
                        pe.wait_ge(s("msg_added"), j - 3)
                    pe.matmul(ps[q % 4][:, 0:SC + SH], hot[:, q % 4, :], message[:, w, q, :], start=True, stop=True).then_inc(s("msg_spread"), 1)
            pe.wait_ge(s("spread_used"), TB)
            msg_sums(0, 0, True)
            with pe.Fori(0, (TB // 8 - 1) // 2) as i:
                msg_sums(i * 2 + 1, 1, False)
                msg_sums(i * 2 + 2, 0, False)

            def rel_sums(i, first):
                for q in range(8):
                    j = i * 8 + q
                    pe.wait_ge(s("hot_rel"), j + 1)
                    if not (first and q < 4):
                        pe.wait_ge(s("rel_added"), j - 3)
                    pe.wait_ge(s(f"got{q}"), START["rel"][q] + 16 * i + 16)
                    pe.matmul(ps[q % 4][:, 0:D], hot[:, q % 4, :], got[:, q, 0:D], start=True, stop=True).then_inc(s("rel_spread"), 1)

            def experts(m, E, FC):
                pe.wait_ge(s(f"gates_ready{m}"), 1)
                with pe.Fori(0, E // 2) as ep:
                    for u in range(2):
                        e = ep * 2 + u
                        pe.wait_ge(s(f"w_in{m}{u}"), ep * 32 + 32)
                        pe.sem_inc(s("pe_turn"), 1)
                        with pe.Fori(0, GROUPS) as g:
                            ge = e * GROUPS + g
                            for f in range(FC):
                                for half in range(2):
                                    pe.wait_ge(s(f"h_room{m}"), (ge * FC + f) * 2 + half + 1)
                                    for kt in range(KT):
                                        mm = pe.matmul(ps[(f * 2 + half) % 4][:, 0:HALF], w1v[m][u][:, kt, f * P:(f + 1) * P],
                                                       XT[:, kt, bass.ds(g * GT + half * HALF, HALF)],
                                                       start=(kt == 0), stop=(kt == KT - 1))
                                    mm.then_inc(s(f"mm1_{m}"), 1)
                            pe.wait_ge(s(f"h_room{m}"), (ge + 1) * FC * 2 + 4)
                            for a in range(BIG_TILES):
                                pe.wait_ge(s(f"y_room{m}"), ge * BIG_TILES + a + (4 if a == 0 else 1 if a == 4 else 0))
                                pe.sem_inc(s("pe_turn"), 1)
                                y = ps[4 + a % 4][:, 0:D]
                                for f in range(FC):
                                    mm = pe.matmul(y, hT[:, f, a * P:(a + 1) * P], w2v[m][u][:, f, :], start=(f == 0), stop=(f == FC - 1))
                                mm.then_inc(s(f"mm2_{m}"), 1)
                            pe.wait_ge(s(f"mm2_{m}"), (ge + 1) * BIG_TILES)
                            pe.sem_inc(s(f"group_done{m}"), 1)
                        pe.sem_inc(s(f"expert_done{m}"), 1)
            pe.sem_inc(s("group_done0"), 1)
            pe.sem_inc(s("group_done1"), 1)
            experts(0, E0, F0)
            pe.wait_ge(s("wrel_in"), 32)
            tiles("rel", None)
            rel_sums(0, True)
            with pe.Fori(1, TC // 8) as i:
                rel_sums(i, False)
            tiles("gate", wgate_sb)
            pe.wait_ge(s("chosen_ready"), 1)
            cv = chosen_b[:].rearrange("p t e -> p (t e)")
            pe.matmul(ps[0][:, 0:NT * E1], ones_b[:], cv, start=True, stop=True)
            pe.matmul(ps[1][:, 0:NT * E1], before[:], cv, start=True, stop=True).then_inc(s("token_counts"), 1)

            def turn_tokens(j, u, first):
                pe.wait_ge(s(f"tile_in{u}"), j * 40 + 80 - 40 * u)
                if not first:
                    pe.wait_ge(s("tokT_ready"), j)
                for b in range(2):
                    for k in range(KT):
                        mm = pe.transpose(ps[0][:, k * MP + b * P:k * MP + (b + 1) * P], tok[u][:, b, k * P:(k + 1) * P], ident[:])
                mm.then_inc(s("tokT_mm"), 1)

            def middle(j, u, first):
                pe.wait_ge(s("tokT_ready"), j + 1)
                for f in range(F1):
                    if not (first and f < 4):
                        pe.wait_ge(s("gelu_done"), F1 * j + f - 3)
                    for k in range(KT):
                        mm = pe.matmul(ps[1 + f % 4][:, 0:MP], w1v[1][u][:, k, f * P:(f + 1) * P], tokT[u][:, k, :], start=(k == 0), stop=(k == KT - 1))
                    mm.then_inc(s("mid_mm"), 1)

            def last(j, u, first):
                for b in range(2):
                    if not first:
                        pe.wait_ge(s("y_copied"), j * 2 + b - 1)
                    y = ps[5 + b][:, 0:D]
                    for f in range(F1):
                        if b == 0:
                            pe.wait_ge(s("gelu_done"), F1 * j + f + 1)
                        mm = pe.matmul(y, hid[u][:, f, b * P:(b + 1) * P], w2v[1][u][:, f, :], start=(f == 0), stop=(f == F1 - 1))
                    mm.then_inc(s("y_mm"), 1)
                pe.wait_ge(s("y_mm"), j * 2 + 2)
                pe.sem_inc(s("tile_done"), 1)

            pe.wait_ge(s("places_known"), 1)
            turn_tokens(0, 0, True)
            middle(0, 0, True)
            turn_tokens(1, 1, False)
            last(0, 0, True)
            with pe.Fori(0, MT // 2 - 1) as i:
                for u in (1, 0):
                    j = i * 2 + 2 - u
                    middle(j, u, False)
                    turn_tokens(j + 1, 1 - u, False)
                    last(j, u, False)
            middle(MT - 1, 1, False)
            last(MT - 1, 1, False)

        @block.vector
        def _(dve):
            ch = Chain(dve, s("dve_chain"))
            tt, tsc, red = dve.tensor_tensor, dve.tensor_scalar, dve.tensor_reduce

            ch(dve.memset(X[:, FULL:NT, :], 0.0))
            ch(dve.memset(ends[:], 0))
            for a in parts["c"][3:6]:
                ch(dve.memset(a, 0))
            ch(dve.memset(parts["c"][7], 0.0))
            dve.sem_inc(s("x_zeroed"), 1)
            ch(dve.memset(bz[:], 0.0))
            dve.sem_inc(s("zeros"), 1)
            for k in "bc":
                ch(dve.memset(srt[k][:], 0.0))
                ch(dve.memset(srt[k][:, :, 1:2], -1.0))
                dve.sem_inc(s(f"edges_zeroed_{k}"), 1)
            dve.wait_ge(s("consts"), 1)
            ch(tsc(here[:], node_id[:], float(N), None, ALU.is_lt))
            for k in "bc":
                C, T, w = NBUCK[k]
                ohv, cnt, pk, di, si, ti, addr, wi = parts[k]
                base = 0 if k == "b" else NB
                dve.wait_ge(s(f"edges_in_{k}"), 32 if k == "b" else 128)
                ch(tsc(addr, di, LANE_MASK, None, ALU.bitwise_and))
                ch(dve.tensor_copy(pk[:, :, 1], addr))
                ch(tsc(addr, di, BLOCK_BITS, None, ALU.arith_shift_right))
                ch(dve.tensor_copy(bh[:, 0:C], addr))
                if k == "b":
                    ch(dve.tensor_copy(pk[:, :, 0], si))
                    ch(dve.tensor_copy(pk[:, :, 2], di))
                else:
                    ch(dve.scalar_tensor_tensor(out=pk[:, :, 0], in0=si, scalar=float(R), in1=ti, op0=ALU.mult, op1=ALU.add))
                    ch(dve.tensor_copy(pk[:, :, 2], wi))
                with dve.Fori(0, NB) as b:
                    tsc(ohv[:, bass.ds(b, 1), :].rearrange("p a c -> p (a c)"), bh[:, 0:C], iota_blk[:, bass.ds(b, 1)], None,
                        ALU.is_equal).then_inc(s("hot_blocks"), 1)
                dve.wait_ge(s("totals"), 1 if k == "b" else 2)
                ch(red(bnum[:], ps[4][:, 0:NB * w].rearrange("p (b c) -> p b c", c=w), AX.X, ALU.add))
                ch(tsc(bint[:], bnum[:], float(P - 1), None, ALU.add))
                ch(tsc(bint[:], bint[:], BLOCK_BITS, None, ALU.arith_shift_right))
                ch(dve.tensor_copy(bnt[:], bint[:]))
                ch(dve.tensor_tensor_scan(bend[:], bnt[:], bz[:, 0:NB], 0.0, ALU.add, ALU.add))
                ch(tt(bnt[:], bend[:], bnt[:], ALU.subtract))
                ch(tsc(badj[:], bnt[:], float(P), None, ALU.mult))

                def scan(n, u, first):
                    dve.wait_ge(s("block_sums"), base + n + 1)
                    if not first:
                        dve.wait_ge(s("placed"), base + n - 1)
                    dve.tensor_tensor_scan(chunk[:, u, 0:C], ps[u][:, 0:C], bz[:, 0:C], 0.0, ALU.add, ALU.add).then_inc(s("scanned"), 1)

                def settle_place(n, u):
                    dve.wait_ge(s("scanned"), base + n + 1)
                    dve.scalar_tensor_tensor(out=cnt[:, bass.ds(n, 1), :].rearrange("p a c -> p (a c)"), in0=chunk[:, u, 0:C],
                                             scalar=badj[:, bass.ds(n, 1)], in1=ps[2 + u][:, 0:C], op0=ALU.add, op1=ALU.add).then_inc(s("placed"), 1)
                scan(0, 0, k == "b")
                scan(1, 1, k == "b")
                with dve.Fori(0, NB // 2 - 1) as i:
                    for u in range(2):
                        settle_place(i * 2 + u, u)
                        scan(i * 2 + u + 2, u, False)
                settle_place(NB - 3, 0)
                scan(NB - 1, 0, False)
                settle_place(NB - 2, 1)
                settle_place(NB - 1, 0)
                dve.wait_ge(s("placed"), base + NB)
                ch(tt(cnt, cnt, ohv, ALU.mult))
                pos = chunk[:, 0, 0:C]
                ch(red(pos, cnt.rearrange("p b c -> p c b"), AX.X, ALU.add))
                ch(dve.tensor_copy(di, pos))
                ch(tsc(addr, di, BLOCK_BITS, None, ALU.arith_shift_right))
                ch(tsc(di, di, LANE_MASK, None, ALU.bitwise_and))
                ch(dve.scalar_tensor_tensor(out=addr, in0=di, scalar=float(T), in1=addr, op0=ALU.mult, op1=ALU.add))
                dve.sem_inc(s("places"), 1)
                blk_i = tile_blk_b if k == "b" else tile_blk_c
                blk_f = bf2[0:1, 0:T]
                ch(dve.memset(blk_f, 0.0))
                for b in range(NB):
                    ch(dve.scalar_tensor_tensor(out=blk_f, in0=iota_tile[0:1, 0:T], scalar=bend[0:1, b:b + 1], in1=blk_f,
                                                op0=ALU.is_ge, op1=ALU.add))
                ch(tsc(blk_i[:], blk_f, float(NB - 1), None, ALU.min))

            def layer_norm(k):
                def st(i, first):
                    for u in range(2):
                        dve.bn_stats(stats[:, bass.ds(i * 2 + u, 1), :].rearrange("p a c -> p (a c)"),
                                     X[:, bass.ds(i * 2 + u, 1), :].rearrange("p a c -> p (a c)")).then_inc(s("stats_done"), 1)
                S["ln"] = S.get("ln", 0) + NT
                with dve.Fori(0, NT // 2) as i:
                    st(i, False)
                dve.wait_ge(s("stats_done"), S["ln"])
                me, mo, ve, vo = (stats[:, :, c] for c in (1, 4, 2, 5))
                ch(tt(mean[:], me, mo, ALU.add))
                ch(tsc(mean[:], mean[:], 0.5, None, ALU.mult))
                ch(tt(tmpn[:], me, mo, ALU.subtract))
                ch(tt(tmpn[:], tmpn[:], tmpn[:], ALU.mult))
                ch(tt(var[:], ve, vo, ALU.add))
                ch(tsc(var[:], var[:], 1.0 / D, None, ALU.mult))
                dve.scalar_tensor_tensor(out=var[:], in0=tmpn[:], scalar=0.25, in1=var[:], op0=ALU.mult, op1=ALU.add).then_inc(s("asked"), 1)
                dve.wait_ge(s("answered"), ASKS[f"std_{k}"])
                ch(dve.reciprocal(rstd[:], var[:]))

                def norm(t, u, early):
                    if not early:
                        dve.wait_ge(s(f"tp_{k}"), t - 1)
                    tsc(xn[:, u, :], X[:, bass.ds(t, 1), :].rearrange("p a c -> p (a c)"), mean[:, bass.ds(t, 1)], rstd[:, bass.ds(t, 1)],
                        ALU.subtract, ALU.mult).then_inc(s(f"xn_{k}"), 1)

                def rel_results(t, u, early):
                    for q in (1, 3):
                        dve.wait_ge(s("rel_mm"), t * 4 + q + 1)
                        if not early:
                            dve.wait_ge(s(f"rel_out{u}"), 32 * (t - u))
                        dve.sem_inc(s("dve_turn"), 1)
                        dve.tensor_copy(rel_out[q][:, u, :], ps[2 + q][:, :]).then_inc(s("rel_ready1"), 1)

                def both(i, first, last):
                    for u in range(2):
                        if not last:
                            norm(i * 2 + u + 2, u, False)
                        if k == "rel":
                            rel_results(i * 2 + u, u, first)
                norm(0, 0, True)
                norm(1, 1, True)
                both(0, True, False)
                with dve.Fori(1, NT // 2 - 1) as i:
                    both(i, False, False)
                both(NT // 2 - 1, False, True)

            dve.wait_ge(s("x_in"), 32)
            dve.wait_ge(s("params_in"), n_params)
            for c, a in ((D, ar_b), (D + HEADS, al_b)):
                for k2 in range(KT):
                    ch(tt(prod[:, 0:D], wg_sb[:, k2, 0:D], a[:], ALU.mult))
                    ch(red(wg_sb[:, k2, c:c + HEADS], prod[:, 0:D].rearrange("p (h d) -> p h d", h=HEADS), AX.X, ALU.add))
            dve.sem_inc(s("attn_weights"), 1)
            layer_norm("val")

            base = ch.n
            K = 10

            def mix(g, w, early):
                c = Chain(dve, s("dve_chain"))
                c.n = g * K + base
                for q in range(BIG_TILES):
                    dve.wait_ge(s(f"got{q}"), START["val"][q] + 32 * g + 32)
                z, m = share[:, w], share_of[:, w]
                mb = m.unsqueeze(2).to_broadcast([P, BIG_TILES, HEADS])
                v = got[:, w * BIG_TILES:(w + 1) * BIG_TILES, 0:D]
                c(tt(z, left[:, w], got[:, w * BIG_TILES:(w + 1) * BIG_TILES, D:D + HEADS], ALU.add))
                c(dve.scalar_tensor_tensor(out=z, in0=z, scalar=0.01, in1=z, op0=ALU.mult, op1=ALU.max))
                c(red(m, z, AX.X, ALU.max))
                c(tt(z, z, mb, ALU.subtract))
                dve.sem_inc(s("val_z"), 1)
                dve.wait_ge(s("val_e"), g + 1)
                c(red(m, z, AX.X, ALU.add))
                c(dve.reciprocal(m, m))
                c(tt(z, z, mb, ALU.mult))
                pv = prod[:].rearrange("p (t h d) -> p t h d", t=BIG_TILES, h=HEADS)
                c(tt(pv, v.rearrange("p t (h d) -> p t h d", h=HEADS), z.unsqueeze(3).to_broadcast([P, BIG_TILES, HEADS, HD]), ALU.mult))
                c(red(mixed_v[:], pv.rearrange("p t h d -> p t d h"), AX.X, ALU.add))
                xv = X[:, bass.ds(g * BIG_TILES, BIG_TILES), :].rearrange("p t (h d) -> p t h d", h=HEADS)
                c(tt(xv, xv, mixed_v[:].unsqueeze(2).to_broadcast([P, BIG_TILES, HEADS, HD]), ALU.add))
                dve.sem_inc(s("val_used"), 1)
            in_groups(dve, GROUPS, mix)
            ch.n = base + K * GROUPS

            layer_norm("score")
            dve.wait_ge(s("score_copied"), NT)
            fe = nodes[:, :, 0:SC]
            big = agg_b[:, :, 0:SC]
            for o, a in ((nodes[:, :, SC:SC + SH], asrc_b), (adm[:, :, 0:SH], adst_b)):
                ch(tt(big, fe, a[:].unsqueeze(1).to_broadcast([P, NT, SC]), ALU.mult))
                ch(red(o.rearrange("p t h -> p t h"), big.rearrange("p t (h e) -> p t h e", e=E0), AX.X, ALU.add))
            dve.sem_inc(s("nodes_ready"), 1)
            ch(tsc(gx[:, :, 0:SH], nodes[:, :, SC:SC + SH], -1.0, None, ALU.mult))
            red(nlow[:], gx[:, :, 0:SH].rearrange("p t h -> p h t"), AX.X, ALU.max).then_inc(s("low_ready"), 1)
            dve.wait_ge(s("low_all"), 1)
            ch(tsc(low[:], low[:], 1.0, None, ALU.add))
            mxb = adm[:, :, SH:2 * SH]
            ch(dve.memset(mxb, 0.0))
            base = ch.n
            dve.wait_ge(s("sorted_in_b"), 16)

            ch(dve.tensor_copy(index_src[:], sorted_b[:, :, 0]))
            ch(dve.tensor_copy(index_dst[:], sorted_b[:, :, 2]))
            dve.sem_inc(s("index_ready"), 1)
            base = ch.n

            def hot_tile(rec_sb, j, r, key, weighted):
                tsc(hot[:, r, :], iota_row[:], rec_sb[:, bass.ds(j, 1), 1], rec_sb[:, bass.ds(j, 1), 2] if weighted else None,
                    ALU.is_equal, *([ALU.mult] if weighted else [])).then_inc(s(key), 1)

            def block_of(blk, j):
                return dve.value_load(blk[0:1, bass.ds(j, 1)], min_val=0, max_val=NB - 1)

            def shift(i, q, j, first):
                r = q % 4
                dve.wait_ge(s(f"got{q}"), START["src"][q] + i * 16 + 16)
                if not (first and q < 4):
                    dve.wait_ge(s("diag_ready"), SH * (j - 3))
                tt(shifted[:, r, :], got[:, q, SC:SC + SH], low[:], ALU.add).then_inc(s("src_shifted"), 1)
                if not (first and q < 4):
                    dve.wait_ge(s("spread"), j - 3)
                hot_tile(sorted_b, j, r, "hot_b", False)

            def reduce_tile(j, r):
                dve.wait_ge(s("spread"), j + 1)
                red(tile_max[:, r, :], ps[r][:, :].rearrange("p (h e) -> p h e", h=SH), AX.X, ALU.max).then_inc(s("spread_used"), 1)

            def keep_max(j, r, first):
                dve.wait_ge(s("spread_used"), j + 1)
                if not first:
                    dve.wait_ge(s("max_kept"), j)
                mb = mxb[:, bass.ds(block_of(tile_blk_b, j), 1), :].rearrange("p a c -> p (a c)")
                tt(mb, mb, tile_max[:, r, :], ALU.max).then_inc(s("max_kept"), 1)

            def maxima(i, first):
                for q in range(8):
                    j = i * 8 + q
                    shift(i, q, j, first)
                    if not (first and q < 3):
                        reduce_tile(j - 3, (q - 3) % 4)
                    if not (first and q < 4):
                        keep_max(j - 4, q % 4, first and q == 4)
            maxima(0, True)
            with dve.Fori(1, TB // 8) as i:
                maxima(i, False)
            for j in range(TB - 4, TB):
                if j + 1 < TB:
                    reduce_tile(j + 1, (j + 1) % 4)
                keep_max(j, j % 4, False)
            dve.wait_ge(s("max_kept"), TB)

            lowb = low[:].unsqueeze(1).to_broadcast([P, NT, SH])
            sv, dv = nodes[:, :, SC:SC + SH], adm[:, :, 0:SH]
            ch(tt(mxb, mxb, lowb, ALU.subtract))
            ch(tt(mxb, mxb, sv, ALU.max))
            ch(tt(mxb, mxb, dv, ALU.add))
            ch(dve.scalar_tensor_tensor(out=mxb, in0=mxb, scalar=0.2, in1=mxb, op0=ALU.mult, op1=ALU.max))
            dve.sem_inc(s("maxima_ready"), 1)
            ch(tt(small2[:], sv, dv, ALU.add))
            ch(dve.scalar_tensor_tensor(out=small2[:], in0=small2[:], scalar=0.2, in1=small2[:], op0=ALU.mult, op1=ALU.max))
            ch(tt(small2[:], small2[:], mxb, ALU.subtract))
            dve.sem_inc(s("asked"), 1)
            dve.wait_ge(s("answered"), ASKS["self_exp"])
            ch(dve.tensor_copy(agg_b[:, :, SC:SC + SH], small2[:]))

            def heads(v):
                return v.rearrange("p t (h e) -> p t h e", e=E0)

            ch(tt(heads(agg_b[:, :, 0:SC]), heads(fe), small2[:].unsqueeze(3).to_broadcast([P, NT, SH, E0]), ALU.mult))
            def add_tile(key, blk, acc, W, j, r, first):
                dve.wait_ge(s(f"{key}_spread"), j + 1)
                if not first:
                    dve.wait_ge(s(f"{key}_added"), j)
                av = acc[:, bass.ds(block_of(blk, j), 1), :].rearrange("p a c -> p (a c)")
                tt(av, av, ps[r][:, 0:W], ALU.add).then_inc(s(f"{key}_added"), 1)

            def logits(i, w):
                for q in range(8):
                    dve.wait_ge(s(f"got{q}"), START["dst"][q] + i * 16 + 16)
                n = i * 5
                z = logit[:, w]
                tt(z, got[:, 0:8, 0:SH], edge1[:, bass.ds(i * 8, 8), SC:SC + SH], ALU.add).then_inc(s("msg_steps"), 1)
                dve.wait_ge(s("msg_steps"), n + 1)
                dve.scalar_tensor_tensor(out=z, in0=z, scalar=0.2, in1=z, op0=ALU.mult, op1=ALU.max).then_inc(s("msg_steps"), 1)
                dve.wait_ge(s("msg_steps"), n + 2)
                tt(z, z, got[:, 0:8, SH:2 * SH], ALU.subtract).then_inc(s("msg_steps"), 1)
                dve.wait_ge(s("msg_steps"), n + 3)
                dve.sem_inc(s("logits"), 1)
                dve.sem_inc(s("logits_used"), 8)

            def messages(i, w):
                dve.wait_ge(s("weights"), i + 1)
                z, n = logit[:, w], i * 5 + 3
                e1v = edge1[:, bass.ds(i * 8, 8), 0:SC]
                tt(heads(message[:, w, :, 0:SC]), heads(e1v), z.unsqueeze(3).to_broadcast([P, 8, SH, E0]), ALU.mult).then_inc(s("msg_steps"), 1)
                dve.tensor_copy(message[:, w, :, SC:SC + SH], z).then_inc(s("msg_steps"), 1)
                dve.wait_ge(s("msg_steps"), n + 2)
                dve.sem_inc(s("messages"), 1)

            def sum_tiles(i, first):
                for q in range(8):
                    j = i * 8 + q
                    if not (first and q < 4):
                        dve.wait_ge(s("msg_spread"), j - 3)
                    hot_tile(sorted_b, j, q % 4, "hot_msg", False)
                    if not (first and q < 3):
                        add_tile("msg", tile_blk_b, agg_b, SC + SH, j - 3, (q - 3) % 4, first and q == 3)

            def eight(i, w, first):
                logits(i, w)
                sum_tiles(i - 1, first)
                messages(i, w)

            assert TB // 8 % 2
            logits(0, 0)
            messages(0, 0)
            eight(1, 1, True)
            eight(2, 0, False)
            with dve.Fori(1, (TB // 8 - 1) // 2) as i:
                eight(i * 2 + 1, 1, False)
                eight(i * 2 + 2, 0, False)
            sum_tiles(TB // 8 - 1, False)
            for j in range(TB - 3, TB):
                add_tile("msg", tile_blk_b, agg_b, SC + SH, j, j % 4, False)
            dve.wait_ge(s("msg_added"), TB)

            den = agg_b[:, :, SC:SC + SH]
            ag = agg_b[:, :, 0:SC]

            def all_t(v):
                return v[:].unsqueeze(1).to_broadcast([P, NT, SC])

            def per_t(v):
                return v.unsqueeze(2).to_broadcast([P, NT, SC])
            ch(tsc(den, den, 1e-16, None, ALU.add))
            ch(dve.reciprocal(small2[:], den))
            ch(tt(heads(ag), heads(ag), small2[:].unsqueeze(3).to_broadcast([P, NT, SH, E0]), ALU.mult))
            ch(tt(ag, ag, all_t(bg_b), ALU.add))
            ch(red(gy[:], ag, AX.X, ALU.add))
            ch(tsc(gy[:], gy[:], 1.0 / SC, None, ALU.mult))
            ch(tt(ag, ag, per_t(gy[:]), ALU.subtract))
            ch(tt(fe, ag, ag, ALU.mult))
            ch(red(gy[:], fe, AX.X, ALU.add))
            ch(tsc(gy[:], gy[:], 1.0 / SC, None, ALU.mult))
            dve.sem_inc(s("asked"), 1)
            dve.wait_ge(s("answered"), ASKS["std_agg"])
            ch(dve.reciprocal(gy[:], gy[:]))
            ch(tt(ag, ag, per_t(gy[:]), ALU.mult))
            ch(tt(ag, ag, all_t(gamma_b), ALU.mult))
            ch(tt(ag, ag, all_t(beta_b), ALU.add))
            ch(red(gates[:, :, 0:E0], ag.rearrange("p t (h e) -> p t e h", e=E0), AX.X, ALU.add))
            ch(tsc(gates[:, :, 0:E0], gates[:, :, 0:E0], 1.0 / SH, None, ALU.mult))

            def top2(m, E, lower):
                g, r = gates[:, :, 0:E], gx[:, :, 0:E]
                pair = pairs[:, :, 0:E * E].rearrange("p t (i j) -> p t i j", i=E)
                pair2 = pairs2[:, :, 0:E * E].rearrange("p t (i j) -> p t i j", i=E)
                gi = g.unsqueeze(3).to_broadcast([P, NT, E, E])
                gj = g.unsqueeze(2).to_broadcast([P, NT, E, E])
                ch(tt(pair, gj, gi, ALU.is_equal))
                ch(tt(pair, pair, lower[:].unsqueeze(1).to_broadcast([P, NT, E, E]), ALU.mult))
                ch(tt(pair2, gj, gi, ALU.is_gt))
                ch(tt(pair, pair, pair2, ALU.add))
                ch(red(r, pair, AX.X, ALU.add))
                if m == 1:
                    for c in range(2):
                        ch(tsc(ranked[:, :, c, :], r, float(c), None, ALU.is_equal))
                ch(tsc(r, r, 2.0, None, ALU.is_lt))
                ch(red(gy[:], g, AX.X, ALU.max))
                ch(tt(g, g, gy[:].unsqueeze(2).to_broadcast([P, NT, E]), ALU.subtract))
                dve.sem_inc(s("asked"), 1)
                dve.wait_ge(s("answered"), ASKS[f"top_exp{m}"])
                ch(tt(g, g, r, ALU.mult))
                ch(red(gy[:], g, AX.X, ALU.add))
                ch(dve.reciprocal(gy[:], gy[:]))
                ch(tt(g, g, gy[:].unsqueeze(2).to_broadcast([P, NT, E]), ALU.mult))
                dve.sem_inc(s(f"gates_ready{m}"), 1)

            def add_experts(m, E, b2):
                dve.sem_inc(s(f"y_room{m}"), 4)
                with dve.Fori(0, E) as e:
                    with dve.Fori(0, GROUPS) as g:
                        for a in range(BIG_TILES):
                            n = (e * GROUPS + g) * BIG_TILES + a
                            t = g * BIG_TILES + a
                            dve.wait_ge(s(f"mm2_{m}"), n + 1)
                            if a >= 2:
                                dve.wait_ge(s(f"acc_done{m}"), n - 1)
                            dve.sem_inc(s("dve_turn"), 1)
                            tt(y_plus[:, a % 2, :], ps[4 + a % 4][:, 0:D], b2[:, bass.ds(e, 1), :].rearrange("p a c -> p (a c)"), ALU.add).then_inc(s(f"y_room{m}"), 1)
                            dve.wait_ge(s(f"y_room{m}"), n + 5)
                            xv = X[:, bass.ds(t, 1), :].rearrange("p a c -> p (a c)")
                            dve.scalar_tensor_tensor(out=xv, in0=y_plus[:, a % 2, :], scalar=gates[:, bass.ds(t, 1), bass.ds(e, 1)].rearrange("p a c -> p (a c)"),
                                                     in1=xv, op0=ALU.mult, op1=ALU.add).then_inc(s(f"acc_done{m}"), 1)
                        dve.wait_ge(s(f"acc_done{m}"), (e * GROUPS + g + 1) * BIG_TILES)

            top2(0, E0, lower0)
            dve.sem_inc(s("moe_room0"), 1)
            add_experts(0, E0, b2_0)

            layer_norm("rel")
            ch(dve.memset(agg_c, 0.0))
            dve.wait_ge(s("sorted_in_c"), 16)
            ch(dve.tensor_copy(index_rel[:], sorted_c[:, :, 0]))
            dve.sem_inc(s("index_ready"), 1)

            def rel_tiles(i, first):
                for q in range(8):
                    j = i * 8 + q
                    if not (first and q < 4):
                        dve.wait_ge(s("rel_spread"), j - 3)
                    hot_tile(sorted_c, j, q % 4, "hot_rel", True)
                    if not (first and q < 3):
                        add_tile("rel", tile_blk_c, agg_c, D, j - 3, (q - 3) % 4, first and q == 3)
            rel_tiles(0, True)
            with dve.Fori(1, TC // 8) as i:
                rel_tiles(i, False)
            for j in range(TC - 3, TC):
                add_tile("rel", tile_blk_c, agg_c, D, j, j % 4, False)
            dve.wait_ge(s("rel_added"), TC)
            ch(dve.scalar_tensor_tensor(out=X[:, 0:NT, :], in0=agg_c, scalar=0.0, in1=X[:, 0:NT, :], op0=ALU.max, op1=ALU.add))
            layer_norm("gate")
            dve.wait_ge(s("gate_copied"), NT)
            ch(tt(gates[:], gates[:], bgate_b[:].unsqueeze(1).to_broadcast([P, NT, E1]), ALU.add))
            top2(1, E1, lower1)
            g, r = gates[:, :, 0:E1], gx[:, :, 0:E1]
            ch(tt(r, r, here[:].unsqueeze(2).to_broadcast([P, NT, E1]), ALU.mult))
            ch(dve.tensor_copy(chosen_b[:], r))
            dve.sem_inc(s("chosen_ready"), 1)
            dve.wait_ge(s("token_counts"), 1)
            tot = ps[0][:, 0:NT * E1].rearrange("p (t e) -> p t e", e=E1)
            for e in range(E1):
                ch(dve.tensor_tensor_scan(chosen[:, :, e], tot[:, :, e], bz[:, 0:NT], 0.0, ALU.add, ALU.add))
            ch(tsc(bint[:, 0:E1], chosen[:, NT - 1, :], float(MP - 1), None, ALU.add))
            ch(tsc(bint[:, 0:E1], bint[:, 0:E1], BLOCK_BITS + 1, None, ALU.arith_shift_right))
            ch(dve.tensor_copy(bnt[:, 0:E1], bint[:, 0:E1]))
            ch(dve.tensor_tensor_scan(bend[:, 0:E1], bnt[:, 0:E1], bz[:, 0:E1], 0.0, ALU.add, ALU.add))
            ch(tt(bnt[:, 0:E1], bend[:, 0:E1], bnt[:, 0:E1], ALU.subtract))
            ch(tsc(bnt[:, 0:E1], bnt[:, 0:E1], float(MP), None, ALU.mult))
            ch(tt(chosen[:], chosen[:], tot, ALU.subtract))
            ch(tt(chosen[:], chosen[:], ps[1][:, 0:NT * E1].rearrange("p (t e) -> p t e", e=E1), ALU.add))
            ch(tt(chosen[:], chosen[:], bnt[:, 0:E1].unsqueeze(1).to_broadcast([P, NT, E1]), ALU.add))
            ch(tsc(away[:, 0:1], node_id[:, 0:1], float(MROWS), None, ALU.add))
            ch(tsc(away[:, 1:2], node_id[:, 0:1], float(MROWS + P), None, ALU.add))
            for c in range(2):
                ch(tt(pairs[:, :, 0:E1], ranked[:, :, c, :], g, ALU.mult))
                ch(red(gate2[:, :, c], pairs[:, :, 0:E1], AX.X, ALU.add))
                ch(tt(pairs[:, :, 0:E1], ranked[:, :, c, :], chosen[:], ALU.mult))
                ch(red(gy[:], pairs[:, :, 0:E1], AX.X, ALU.add))
                ch(tsc(gy[:], gy[:], away[:, c:c + 1], None, ALU.subtract))
                ch(tt(gy[:], gy[:], here[:], ALU.mult))
                ch(tsc(gy[:], gy[:], away[:, c:c + 1], None, ALU.add))
                ch(dve.tensor_copy(place[:, :, c], gy[:]))
            ch(dve.memset(bf2[0:1, 0:MT], 0.0))
            for e in range(E1):
                ch(dve.scalar_tensor_tensor(out=bf2[0:1, 0:MT], in0=iota_tile[0:1, 0:MT], scalar=bend[0:1, e:e + 1], in1=bf2[0:1, 0:MT],
                                            op0=ALU.is_ge, op1=ALU.add))
            ch(tsc(expert_of[:], bf2[0:1, 0:MT], float(E1 - 1), None, ALU.min))
            dve.sem_inc(s("places_known"), 1)
            dve.sem_inc(s("moe_room1"), 1)
            dve.wait_ge(s("rel_spread"), TC)

            def token_rows(i, first):
                for a in range(BIG_TILES):
                    t = i * BIG_TILES + a
                    if not first:
                        dve.wait_ge(s(f"got{a}"), START["put"][a] + 32 * i)
                    dve.tensor_copy(pick_tok[:, a, :], place[:, bass.ds(t, 1), :].rearrange("p a c -> p (a c)")).then_inc(s("tok_pick"), 1)
                    dve.wait_ge(s("tok_pick"), t + 1)
                    tsc(got[:, a, 0:D], X[:, bass.ds(t, 1), :].rearrange("p a c -> p (a c)"), mean[:, bass.ds(t, 1)], rstd[:, bass.ds(t, 1)],
                        ALU.subtract, ALU.mult).then_inc(s("tok_ready"), 1)
            token_rows(0, True)
            with dve.Fori(1, GROUPS) as i:
                token_rows(i, False)
            for a in range(BIG_TILES):
                dve.wait_ge(s(f"got{a}"), END["put"][a])

            def copy_y(j, u, early):
                for b in range(2):
                    dve.wait_ge(s("y_mm"), j * 2 + b + 1)
                    if not early and b == 0:
                        dve.wait_ge(s(f"y_out{u}"), 8 * (j - u))
                    dve.sem_inc(s("dve_turn"), 1)
                    tt(res[u][:, b, :], ps[5 + b][:, 0:D], mb2[u], ALU.add).then_inc(s("y_copied"), 1)
            copy_y(0, 0, True)
            copy_y(1, 1, True)
            with dve.Fori(1, MT // 2) as i:
                copy_y(i * 2, 0, False)
                copy_y(i * 2 + 1, 1, False)

            def take_pick(t, a):
                dve.tensor_copy(pick_tok[:, a, :], place[:, bass.ds(t, 1), :].rearrange("p a c -> p (a c)")).then_inc(s("take_ready"), 1)
            for a in range(BIG_TILES):
                take_pick(a, a)

            def mix_back(i, more):
                for a in range(BIG_TILES):
                    t = i * BIG_TILES + a
                    dve.wait_ge(s(f"got{a}"), START["take"][a] + 32 * i + 32)
                    xv = X[:, bass.ds(t, 1), :].rearrange("p a c -> p (a c)")
                    for c in range(2):
                        dve.scalar_tensor_tensor(out=xv, in0=got[:, 2 * a + c, 0:D], scalar=gate2[:, bass.ds(t, 1), c], in1=xv,
                                                 op0=ALU.mult, op1=ALU.add).then_inc(s("mixed"), 1)
                        dve.wait_ge(s("mixed"), t * 2 + c + 1)
                    if more:
                        take_pick(t + BIG_TILES, a)
            with dve.Fori(0, GROUPS - 1) as i:
                mix_back(i, True)
            mix_back(GROUPS - 1, False)


_INS = ['x', 'src', 'dst', 'edge_type_8', 'edge_weight', 'L0_gnn_weight', 'L0_gnn_attn_l', 'L0_gnn_attn_r', 'L0_ffn_W_gat',
        'L0_ffn_att_src', 'L0_ffn_att_dst', 'L0_ffn_b_gat', 'L0_ffn_ln_gamma', 'L0_ffn_ln_beta', 'L0_ffn_W1', 'L0_ffn_b1',
        'L0_ffn_W2', 'L0_ffn_b2', 'L0_ffn_edge_index', 'L1_gnn_weight', 'L1_ffn_Wg', 'L1_ffn_bg', 'L1_ffn_W1', 'L1_ffn_b1',
        'L1_ffn_W2', 'L1_ffn_b2']


def kernel(**inputs):
    import numpy as _np
    import concourse.bacc as _bacc
    from concourse import mybir as _mybir
    from concourse.bass_utils import run_bass_kernel_spmd as _run

    nc = _bacc.Bacc("TRN2", target_bir_lowering=False, num_devices=1)
    arrays, args = {}, []
    for name in _INS:
        a = _np.ascontiguousarray(inputs[name])
        arrays[f"in_{name}"] = a
        args.append(nc.dram_tensor(f"in_{name}", a.shape, _mybir.dt.from_np(a.dtype), kind="ExternalInput").ap())
    args.append(nc.dram_tensor("out_0", inputs['x'].shape, _mybir.dt.float32, kind="ExternalOutput").ap())
    graph_layers(nc, *args)
    r = _run(nc, [arrays], core_ids=[0])
    return r.results[0]["out_0"]
```

```python
from contextlib import ExitStack

import concourse.bass as bass
from concourse import mybir

F32 = mybir.dt.float32
BF16 = mybir.dt.bfloat16
I32 = mybir.dt.int32
ALU = mybir.AluOpType
ACT = mybir.ActivationFunctionType
AX = mybir.AxisListType
RMAX = bass.bass_isa.ReduceOp.max

P = 128
ROW, BLOCK_BITS, LANE_MASK = 4, 7, 127
BIG_TILES = 5


class Chain:

    def __init__(self, eng, sem):
        self.eng, self.sem, self.n = eng, sem, 0

    def __call__(self, ins):
        ins.then_inc(self.sem, 1)
        self.n = self.n + 1
        self.eng.wait_ge(self.sem, self.n)


def graph_layers(nc, x, src, dst, etype, eweight, w_gat, attn_l, attn_r, w_score, att_src, att_dst, b_gat, ln_gamma,
                 ln_beta, moe0_w1, moe0_b1, moe0_w2, moe0_b2, edges0, w_rel, w_gate, b_gate, moe1_w1, moe1_b1,
                 moe1_w2, moe1_b2, out):
    N, D = x.shape
    KT = D // P
    NB = -(-N // P)
    NT = NB + NB % 2
    FULL, REST = N // P, N % P
    HEADS = attn_l.shape[0]
    HD = D // HEADS
    SH, E0 = att_src.shape
    SC = SH * E0
    R = w_rel.shape[0]
    E1 = w_gate.shape[1]
    F0, F1 = moe0_w1.shape[2] // P, moe1_w1.shape[2] // P
    EB, EC = edges0.shape[1], src.shape[0]
    CB = EB // P
    CC = -(-EC // (8 * P)) * 8
    TB = -(-((CB * P + NB * (P - 1)) // P) // 8) * 8
    TC = -(-((CC * P + NB * (P - 1)) // P) // 8) * 8
    GROUPS = NB // BIG_TILES
    MP = 2 * P
    MT = (2 * N + E1 * (MP - 1)) // MP
    MT += MT % 2
    MROWS = MT * MP
    GT = BIG_TILES * P
    HALF = GT // 2
    assert D == 2 * P and NB % BIG_TILES == 0 and NB % 2 and CB * P == EB and CB % 8 == 0

    tab_val = nc.dram_tensor("tab_val", (NT * P, D + HEADS), F32, kind="Internal").ap()
    tab_left = nc.dram_tensor("tab_left", (NT * P, HEADS), F32, kind="Internal").ap()
    tab_src = nc.dram_tensor("tab_src", (NT * P, SC + SH), F32, kind="Internal").ap()
    tab_rel = nc.dram_tensor("tab_rel", (NT * P * R, D), F32, kind="Internal").ap()
    tok_in = nc.dram_tensor("tok_in", (MROWS + 2 * P, D), F32, kind="Internal").ap()
    tok_out = nc.dram_tensor("tok_out", (MROWS + 2 * P, D), F32, kind="Internal").ap()
    tab_y = nc.dram_tensor("tab_y", (E0, NB * P, D), F32, kind="Internal").ap()
    rec_b = nc.dram_tensor("rec_b", (P * TB, ROW), F32, kind="Internal").ap()
    rec_c = nc.dram_tensor("rec_c", (P * TC, ROW), F32, kind="Internal").ap()

    with ExitStack() as ctx:
        def sb(name, shape, dt=F32):
            return ctx.enter_context(nc.sbuf_tensor(name, shape, dt))

        def sem(name):
            return ctx.enter_context(nc.semaphore(name))

        psum = ctx.enter_context(nc.psum_tensor("psum", [P, 8 * 512], F32))
        ps = [psum[:, i * 512:(i + 1) * 512] for i in range(8)]
        MSG_W = 64
        msg_acc = psum[:, 3 * 512:7 * 512]
        assert 3 * (SC + SH) <= MSG_W and NT * MSG_W <= 4 * 512 and 512 % MSG_W == 0

        X = sb("X", [P, NT, D])
        ident = sb("ident", [P, P])
        iota_row = sb("iota_row", [P, P])
        before = sb("before", [P, P], BF16)
        upto = sb("upto", [P, P], BF16)
        ones_b = sb("ones_b", [P, P], BF16)
        ones_f = sb("ones_f", [P, P])
        iota_blk = sb("iota_blk", [P, NB])
        iota_tile = sb("iota_tile", [1, TC])
        lower0 = sb("lower0", [P, E0, E0])
        lower1 = sb("lower1", [P, E1, E1])
        xn = sb("xn", [P, 2, D])
        xTs = sb("xTs", [P, 2, KT, P])
        rows = sb("rows", [P, 2, D + HEADS])
        left_all = sb("left_all", [P, NT, HEADS])
        stats = sb("stats", [P, NT, 6])
        mean = sb("mean", [P, NT])
        var = sb("var", [P, NT])
        tmpn = sb("tmpn", [P, NT])
        rstd = sb("rstd", [P, NT])
        sorted_b = sb("sorted_b", [P, TB, ROW])
        sorted_c = sb("sorted_c", [P, TC, ROW])
        tile_blk_b = sb("tile_blk_b", [1, TB], I32)
        tile_blk_c = sb("tile_blk_c", [1, TC], I32)
        pick = sb("pick", [P, 2, 8], I32)
        pick_tok = sb("pick_tok", [P, BIG_TILES, 2], I32)
        place = sb("place", [P, NT, 2], I32)
        gate2 = sb("gate2", [P, NT, 2])
        chosen = sb("chosen", [P, NT, E1])
        chosen_b = sb("chosen_b", [P, NT, E1], BF16)
        here = sb("here", [P, NT])
        away = sb("away", [P, 2])
        node_id = sb("node_id", [P, NT])
        expert_of = sb("expert_of", [1, MT], I32)
        pick_val = sb("pick_val", [P, 2, BIG_TILES, 2], I32)
        left = sb("left", [P, 2, BIG_TILES, HEADS])
        share = sb("share", [P, 2, BIG_TILES, HEADS])
        share_of = sb("share_of", [P, 2, BIG_TILES])
        index_src = sb("index_src", [P, TB], I32)
        index_rel = sb("index_rel", [P, TC], I32)
        got = sb("got", [P, 2 * BIG_TILES, D + HEADS])
        terms = sb("terms", [P, 16, SC + SH])
        hot = sb("hot", [P, 4, P])
        diag = sb("diag", [P, 4, SH, P])
        shifted = sb("shifted", [P, 8, SH])
        tile_max = sb("tile_max", [P, 4, SH])
        logit = sb("logit", [P, 2, 8, SH])
        message = sb("message", [P, 8, SC + SH])
        msg_parts = sb("msg_parts", [P, 2, 8, 3, SC + SH], BF16)
        adm_parts = sb("adm_parts", [P, NT, 3, 2 * SH], BF16)
        ident_b = sb("ident_b", [P, P], BF16)
        found = sb("found", [P, 8, 2 * SH])
        ends = sb("ends", [P, NT, 2], I32)
        al_b = sb("al_b", [P, D])
        ar_b = sb("ar_b", [P, D])
        asrc_b = sb("asrc_b", [P, SC])
        adst_b = sb("adst_b", [P, SC])
        bg_b = sb("bg_b", [P, SC])
        gamma_b = sb("gamma_b", [P, SC])
        beta_b = sb("beta_b", [P, SC])
        bgate_b = sb("bgate_b", [P, E1])
        wg_sb = sb("wg_sb", [P, KT, D + 2 * HEADS])
        ws_sb = sb("ws_sb", [P, KT, SC])
        wgate_sb = sb("wgate_sb", [P, KT, E1])
        b1_0 = sb("b1_0", [P, E0, F0])
        b1_1 = sb("b1_1", [P, E1, F1])
        b2_0 = sb("b2_0", [P, E0, D])
        b2_1 = sb("b2_1", [P, E1, D])
        nodes = sb("nodes", [P, NT, SC + SH])
        adm = sb("adm", [P, NT, 2 * SH])
        gates = sb("gates", [P, NT, E1])
        gx = sb("gx", [P, NT, E1])
        gy = sb("gy", [P, NT])
        eps = sb("eps", [P, 1])
        low = sb("low", [P, SH])
        nlow = sb("nlow", [P, SH])

        rec_slot = sb("rec_slot", [P, 2, 8, ROW])
        bf2 = sb("bf2", [1, TC])
        small2 = sb("small2", [P, NT, SH])
        ARENA = 23296
        arena = sb("arena", [P, ARENA])

        def part(at, *dims, dt=F32):
            n = 1
            for d in dims:
                n *= d
            words = n if dt != BF16 else n // 2
            assert at + words <= ARENA, (at, words)
            v = arena[:, at:at + words]
            if dt != F32:
                v = v.bitcast(dt)
            if len(dims) == 2:
                v = v.rearrange("p (a b) -> p a b", b=dims[1])
            if len(dims) == 3:
                v = v.rearrange("p (a b c) -> p a b c", b=dims[1], c=dims[2])
            return v

        def bucket_parts(C, edges_at, pk_at):
            ohv = part(0, NB, C, dt=BF16)
            cnt = part(NB * C // 2, NB, C)
            assert NB * C // 2 * 3 <= 14720
            di, si, ti = (part(edges_at + q * C, C, dt=I32) for q in range(3))
            wi = part(edges_at + 3 * C, C)
            pk, addr = part(pk_at, C, ROW), part(pk_at, C, ROW, dt=I32)[:, :, 3]
            return ohv, cnt, pk, di, si, ti, addr, wi

        bnum = sb("bnum", [P, NB])
        bint = sb("bint", [P, NB], I32)
        bnt = sb("bnt", [P, NB])
        bend = sb("bend", [P, E1])
        block_end = {"b": sb("end_b", [P, NB]), "c": sb("end_c", [P, NB])}
        badj = sb("badj", [P, NB])
        bz = sb("bz", [P, 512])
        prod = part(0, BIG_TILES * D)
        mixed_v = part(BIG_TILES * D, BIG_TILES, HD)
        rel_rows = part(0, 16, D)
        TURNED = 12800
        assert TURNED >= KT * NT * P + TB * (SC + SH) + NT * (SC + SH)
        turned = part(TURNED, 8, P, dt=BF16)
        hots = part(TURNED + 1024, 2, 8, P, dt=BF16)
        XT = part(0, KT, NT * P)
        R0 = KT * NT * P
        MID = R0 + NT * D
        LATE = MID + KT * R * D
        edge1 = part(R0, TB, SC + SH)
        agg_b = part(R0 + TB * (SC + SH), NT, SC + SH)
        agg_c = part(R0, NT, D)
        wrel = part(MID, KT, R * D)
        PK_C = ARENA - CC * ROW
        assert LATE + 4 * 1024 <= PK_C
        rel_out = [part(LATE + q * 1024, 2, 512) for q in range(4)]
        w1v, w2v = {}, {}
        half = KT * F0 * P
        w1v[0] = [part(R0 + u * 2 * half, KT, F0 * P) for u in range(2)]
        w2v[0] = [part(R0 + u * 2 * half + half, F0, D) for u in range(2)]
        R1 = R0 + 4 * half
        hT = [part(R1, F0, GT), part(LATE, F0, GT)]
        y_stage = [part(MID + p * BIG_TILES * D, BIG_TILES, D) for p in range(2)]
        y_back = [part(at, E0 * BIG_TILES, D) for at in (0, LATE)]
        term_prods = part(LATE + F0 * GT, NT, SC)
        pairs_0, pairs2_0 = part(TURNED, NT, E0 * E0), part(TURNED + NT * E0 * E0, NT, E0 * E0)
        assert LATE + F0 * GT + NT * SC <= PK_C - CB * ROW
        PAIR0 = 16384
        ranked = part(PAIR0 + 2 * NT * E1 * E1, NT, 2, E1)
        pairs = part(PAIR0, NT, E1 * E1)
        pairs2 = part(PAIR0 + NT * E1 * E1, NT, E1 * E1)
        half = KT * F1 * P
        w1v[1] = [part(u * 2 * half, KT, F1 * P) for u in range(2)]
        w2v[1] = [part(u * 2 * half + half, F1, D) for u in range(2)]
        M0 = 4 * half
        tok = [part(M0 + u * 2 * D, 2, D) for u in range(2)]
        tokT = [part(M0 + 4 * D + u * KT * MP, KT, MP) for u in range(2)]
        hid = [part(M0 + 4 * D + 2 * KT * MP + u * F1 * MP, F1, MP) for u in range(2)]
        M1 = M0 + 4 * D + 2 * KT * MP + 2 * F1 * MP
        res = [part(M1 + u * 2 * D, 2, D) for u in range(2)]
        mb1 = [part(M1 + 4 * D + u * F1, F1) for u in range(2)]
        M2 = M1 + 4 * D + 2 * F1
        mb2 = [part(M2 + u * D, D) for u in range(2)]
        assert M2 + 2 * D <= PAIR0 and R1 + F0 * GT <= PAIR0

        block = ctx.enter_context(nc.Block())

        def in_groups(eng, n, body):
            for g in range(3):
                body(g, g % 2, True)
            with eng.Fori(1, (n - 1) // 2) as i:
                body(i * 2 + 1, 1, False)
                body(i * 2 + 2, 0, False)
            if n % 2 == 0:
                body(n - 1, 1, False)

        def first_groups(eng, step, ahead=None):
            pairs_e = E0 // 2

            def two(ep, last):
                for u in range(2):
                    e = ep * 2 + u
                    with eng.Fori(0, GROUPS // 2) as i:
                        for v in range(2):
                            g = i * 2 + v
                            if ahead:
                                ahead(e, u, g + 1, (u + v + 1) % 2)
                            step(e, u, g, (u + v) % 2)
                    if ahead and not (last and u == 1):
                        ahead(e + 1, 1 - u, 0, 1 - u)
                    step(e, u, GROUPS - 1, u)
            if ahead:
                ahead(0, 0, 0, 0)
            with eng.Fori(0, pairs_e - 1) as ep:
                two(ep, False)
            two(pairs_e - 1, True)

        def squares(i, q):
            return i * (4 * SH - 2) + (q + 1) * SH - (q + 1) // 2

        MM2_CREDIT = 2 * BIG_TILES
        S = {}

        def s(name):
            if name not in S:
                S[name] = sem(name)
            return S[name]

        ASKS = {n: i + 1 for i, n in enumerate(("std_val", "std_score", "self_exp", "std_agg", "top_exp0",
                                                "std_rel", "std_gate", "top_exp1"))}
        RECORDS = {"b1": ("b", 0, 10), "b2": ("b", 10, CB // 8), "c1": ("c", 0, 10), "c2": ("c", 10, 24), "c3": ("c", 24, CC // 8)}
        STAGES = [("b1", 8, 16, 10), ("val", BIG_TILES, 32, GROUPS), ("b2", 8, 16, CB // 8 - 10), ("c1", 8, 16, 10), ("c2", 8, 16, 14),
                  ("src", 8, 16, TB // 8), ("c3", 8, 16, CC // 8 - 24),
                  ("rel", 8, 16, TC // 8), ("put", BIG_TILES, 32, GROUPS), ("take", BIG_TILES, 32, GROUPS)]
        PER = {name: per for name, per, step, n in STAGES}
        STEP = {name: step for name, per, step, n in STAGES}
        COUNT = {name: n for name, per, step, n in STAGES}
        START, END, PICK_START = {}, {}, {}
        at, fed = [0] * 16, [0, 0]
        for name, per, step, n in STAGES:
            START[name], PICK_START[name] = list(at), list(fed)
            for w in range(2):
                turns = n - n // 2 if w == 0 else n // 2
                fed[w] += 16 * turns
                if name in ("put", "take"):
                    turns = n if w == 0 else 0
                for q in range(per):
                    at[w * per + q] += step * turns
            END[name] = list(at)

        def landed(key, g, w, early, q):
            base, step = START[key][w * PER[key] + q] + STEP[key], STEP[key]
            return base + step * (g // 2) if early else (g - w) * (step // 2) + base

        def fed_count(key, g, w, early):
            base = PICK_START[key][w] + 16
            return base + 16 * (g // 2) if early else (g - w) * 8 + base
        NBUCK = {"b": (CB, TB, 16), "c": (CC, TC, 14)}
        for C, _, w in NBUCK.values():
            assert C % w == 0 and NB * w <= 512 and C <= 512
        assert NB % 4 == 1
        EDGES_B = 14720 + 4 * CC
        PK_B = PK_C - CB * ROW
        parts = {"b": bucket_parts(CB, EDGES_B, PK_B), "c": bucket_parts(CC, 14720, PK_C)}
        chunk = part(EDGES_B + 4 * CB, 4, CC)
        bh = part(EDGES_B + 4 * CB + 4 * CC, CC, dt=BF16)
        assert EDGES_B + 4 * CB + 4 * CC + CC // 2 <= PK_B
        rec = {"b": rec_b, "c": rec_c}
        srt = {"b": sorted_b, "c": sorted_c}
        WIDTH = {"val": D + 2 * HEADS, "score": SC, "rel": R * D, "gate": E1}

        @block.sync
        def _(sp):
            sp.wait_ge(s("x_zeroed"), 1)
            for k in "bc":
                C, T, _ = NBUCK[k]
                ohv, cnt, pk, di, si, ti, addr, wi = parts[k]
                if k == "b":
                    sp.dma_start(si, edges0[0].rearrange("(p c) -> p c", p=P)).then_inc(s("edges_in_b"), 16)
                    sp.dma_start(di, edges0[1].rearrange("(p c) -> p c", p=P)).then_inc(s("edges_in_b"), 16)
                else:
                    full, rest = EC // C, EC % C
                    for o, i in ((si, src), (di, dst), (ti, etype), (wi, eweight)):
                        sp.dma_start(o[0:full, :], i[0:full * C].rearrange("(p c) -> p c", c=C)).then_inc(s("edges_in_c"), 16)
                        sp.dma_start(o[full:full + 1, 0:rest], i[full * C:EC].rearrange("(o c) -> o c", o=1)).then_inc(s("edges_in_c"), 16)
            sp.dma_start(X[:, 0:FULL, :], x[0:FULL * P, :].rearrange("(t p) d -> p t d", p=P)).then_inc(s("x_in"), 16)
            sp.dma_start(X[0:REST, FULL, :], x[FULL * P:N, :]).then_inc(s("x_in"), 16)
            for c, v in ((0, dst), (1, src)):
                sp.dma_start(ends[:, 0:FULL, c], v[0:FULL * P].rearrange("(t p) -> p t", p=P), allow_slow_non_contiguous=True).then_inc(s("ends_in"), 16)
                sp.dma_start(ends[0:REST, FULL:FULL + 1, c], v[FULL * P:N].rearrange("(p o) -> p o", o=1), allow_slow_non_contiguous=True).then_inc(s("ends_in"), 16)
            flat = lambda a: a.rearrange("a b -> (a b)")
            loads = [
                (al_b[:], flat(attn_l).partition_broadcast(P)), (ar_b[:], flat(attn_r).partition_broadcast(P)),
                (asrc_b[:], flat(att_src).partition_broadcast(P)), (adst_b[:], flat(att_dst).partition_broadcast(P)),
                (bg_b[:], b_gat.partition_broadcast(P)), (gamma_b[:], ln_gamma.partition_broadcast(P)),
                (beta_b[:], ln_beta.partition_broadcast(P)), (bgate_b[:], b_gate.partition_broadcast(P)),
                (wg_sb[:, :, 0:D], w_gat.rearrange("(k p) n -> p k n", p=P)),
                (ws_sb[:], w_score.rearrange("(k p) n -> p k n", p=P)),
                (wgate_sb[:], w_gate.rearrange("(k p) n -> p k n", p=P)),
                (b2_0[:].rearrange("p e d -> p (e d)"), flat(moe0_b2).partition_broadcast(P)),
                (b2_1[:].rearrange("p e d -> p (e d)"), flat(moe1_b2).partition_broadcast(P)),
            ] + [(b1_0[:, e, :], moe0_b1[e].rearrange("(f p) -> p f", p=P)) for e in range(E0)] \
              + [(b1_1[:, e, :], moe1_b1[e].rearrange("(f p) -> p f", p=P)) for e in range(E1)]
            for o, i in loads:
                sp.dma_start(o, i, allow_slow_non_contiguous=True).then_inc(s("params_in"), 16)
            S["n_params"] = 16 * len(loads)
            for k in "bc":
                sp.wait_ge(s(f"edges_zeroed_{k}"), 1)
                sp.dma_start(rec[k].rearrange("(p t) r -> p t r", p=P), srt[k][:]).then_inc(s(f"pad_out_{k}"), 16)
            zero = bz[:].unsqueeze(1).to_broadcast([P, MROWS * D // P // 512, 512])
            sp.wait_ge(s("zeros"), 1)
            sp.dma_start(tok_in[0:MROWS, :].rearrange("(p a b) d -> p a (b d)", p=P, b=2), zero).then_inc(s("tok_zeroed"), 16)
            sp.dma_start(tok_out[MROWS:MROWS + 2 * P, :].rearrange("(p b) d -> p (b d)", p=P), bz[:]).then_inc(s("tok_zeroed"), 16)

            def feed_group(key, g, w, early, slots, source):
                for q in range(PER[key]):
                    done = landed(key, g, w, early, q) - STEP[key]
                    if not early or done > 0:
                        sp.wait_ge(s(f"got{w * PER[key] + q}"), done)
                        sp.sem_inc(s("sp_turn"), 1)
                sp.dma_start(slots, source).then_inc(s(f"picked{w}"), 16)

            def feed_records(key):
                k, at, _ = RECORDS[key]

                def body(g, w, early):
                    feed_group(key, g, w, early, rec_slot[:, w], parts[k][2][:, bass.ds((g + at) * 8, 8), :])
                in_groups(sp, COUNT[key], body)

            def sorted_back(k, key):
                for q in range(16):
                    sp.wait_ge(s(f"got{q}"), END[key][q])
                sp.wait_ge(s(f"pad_out_{k}"), 16)
                sp.dma_start(srt[k][:], rec[k].rearrange("(p t) r -> p t r", p=P)).then_inc(s(f"sorted_in_{k}"), 16)

            def feed_val(g, w, early):
                feed_group("val", g, w, early, pick_val[:, w], ends[:, bass.ds(g * BIG_TILES, BIG_TILES), :])
            sp.wait_ge(s("places"), 1)
            feed_records("b1")
            sp.wait_ge(s("ends_in"), 64)
            in_groups(sp, GROUPS, feed_val)
            def load_expert(e):
                u = e % 2
                sp.dma_start(w1v[0][u], moe0_w1[e].rearrange("(k p) f -> p k f", p=P)).then_inc(s(f"w_in0{u}"), 16)
                sp.dma_start(w2v[0][u], moe0_w2[e].rearrange("(f p) d -> p f d", p=P)).then_inc(s(f"w_in0{u}"), 16)

            def feed(key, index):
                def body(g, w, early):
                    feed_group(key, g, w, early, pick[:, w, :], index[:, bass.ds(g * 8, 8)])
                in_groups(sp, COUNT[key], body)

            assert E0 == 4
            sp.wait_ge(s("places"), 2)
            load_expert(0)
            load_expert(1)
            feed_records("b2")
            sp.wait_ge(s("mm2_0"), NB + MM2_CREDIT)
            load_expert(2)
            sorted_back("b", "b2")
            sp.wait_ge(s("nodes_ready"), 1)
            sp.dma_start(tab_src.rearrange("(t p) r -> p t r", p=P), nodes[:]).then_inc(s("src_out"), 16)
            feed_records("c1")
            sp.wait_ge(s("mm2_0"), 2 * NB + MM2_CREDIT)
            load_expert(3)
            feed_records("c2")
            sp.wait_ge(s("index_ready"), 1)
            feed("src", index_src)
            feed_records("c3")
            sorted_back("c", "c3")

            def load_y(g, w, early):
                if not (early and g < 2):
                    sp.wait_ge(s("acc_done"), (g - 1) * E0 * BIG_TILES)
                    sp.sem_inc(s("sp_turn"), 1)
                for e in range(E0):
                    sp.dma_start(y_back[w][:, e * BIG_TILES:(e + 1) * BIG_TILES, :],
                                 tab_y[e, bass.ds(g * GT, GT), :].rearrange("(t p) d -> p t d", p=P)).then_inc(s(f"y_in{w}"), 16)
            for p in range(2):
                sp.wait_ge(s(f"y_stored{p}"), 16 + 16 * E0 * GROUPS // 2)
            load_y(0, 0, True)
            load_y(1, 1, True)
            sp.wait_ge(s("wrel_room"), 1)
            wr = wrel.rearrange("p k (r n) -> p k r n", r=R)
            for k2 in range(KT):
                sp.dma_start(wr[:, k2], w_rel[:, k2 * P:(k2 + 1) * P, :].rearrange("r p n -> p r n")).then_inc(s("wrel_in"), 16)
            for g in range(2, GROUPS):
                load_y(g, g % 2, True)
            tr = tab_rel.rearrange("(n r) d -> n (r d)", r=R)

            def store_rel(i, first):
                for u in range(2):
                    t = i * 2 + u
                    for q in range(4):
                        sp.wait_ge(s(f"rel_ready{q % 2}"), t * 2 + q // 2 + 1)
                        sp.dma_start(tr[bass.ds(t * P, P), q * 512:(q + 1) * 512], rel_out[q][:, u, :]).then_inc(s(f"rel_out{u}"), 16)
            store_rel(0, True)
            with sp.Fori(1, NT // 2) as i:
                store_rel(i, False)
            sp.wait_ge(s("index_ready"), 2)
            feed("rel", index_rel)
            sp.wait_ge(s("moe_room1"), 1)
            for k2 in range(BIG_TILES):
                sp.wait_ge(s(f"got{k2}"), END["put"][k2])

            def store_tile(j, u):
                sp.wait_ge(s("y_copied"), j * 2 + 2)
                sp.sem_inc(s("sp_turn"), 1)
                sp.dma_start(tok_out[bass.ds(j * MP, MP), :].rearrange("(b p) d -> p b d", b=2), res[u]).then_inc(s(f"y_out{u}"), 16)

            def tile(i, first):
                for u in range(2):
                    j = i * 2 + u
                    if not first:
                        sp.wait_ge(s("mid_mm"), F1 * (j - 1))
                        sp.wait_ge(s("gelu_done"), F1 * (j - 1))
                        sp.sem_inc(s("sp_turn"), 1)
                    e = sp.value_load(expert_of[0:1, bass.ds(j, 1)], min_val=0, max_val=E1 - 1)
                    sp.dma_start(tok[u], tok_in[bass.ds(j * MP, MP), :].rearrange("(b p) d -> p b d", b=2)).then_inc(s(f"tokens_in{u}"), 16)
                    sp.dma_start(w1v[1][u], moe1_w1[bass.ds(e, 1)].rearrange("a (k p) f -> p (a k) f", p=P)).then_inc(s(f"w1_in{u}"), 16)
                    sp.dma_start(mb1[u], b1_1[:, bass.ds(e, 1), :].rearrange("p a f -> p (a f)")).then_inc(s(f"w1_in{u}"), 16)
                    if not first:
                        sp.wait_ge(s("y_mm"), (j - 1) * 2)
                        sp.sem_inc(s("sp_turn"), 1)
                        store_tile(j - 2, u)
                    sp.dma_start(w2v[1][u], moe1_w2[bass.ds(e, 1)].rearrange("a (f p) d -> p (a f) d", p=P)).then_inc(s(f"w2_in{u}"), 16)
                    sp.dma_start(mb2[u], b2_1[:, bass.ds(e, 1), :].rearrange("p a d -> p (a d)")).then_inc(s(f"w2_in{u}"), 16)
            tile(0, True)
            with sp.Fori(1, MT // 2) as i:
                tile(i, False)
            for j in range(MT - 2, MT):
                store_tile(j, j % 2)
            with sp.Fori(0, GROUPS - 1) as i:
                sp.wait_ge(s("mixed"), (i + 1) * 2 * BIG_TILES)
                sp.sem_inc(s("sp_turn"), 1)
                sp.dma_start(out[bass.ds(i * GT, GT), :].rearrange("(t p) d -> p t d", p=P), X[:, bass.ds(i * BIG_TILES, BIG_TILES), :]).then_inc(s("result_out"), 16)
            sp.wait_ge(s("mixed"), NB * 2)
            t0 = (GROUPS - 1) * BIG_TILES
            sp.dma_start(out[t0 * P:FULL * P, :].rearrange("(t p) d -> p t d", p=P), X[:, t0:FULL, :]).then_inc(s("result_out"), 16)
            sp.dma_start(out[FULL * P:N, :], X[0:REST, FULL, :]).then_inc(s("result_out"), 16)
            sp.wait_ge(s("result_out"), 16 * (GROUPS + 1))

        n_params = S.pop("n_params")

        @block.gpsimd
        def _(pool):
            ch = Chain(pool, s("pool_chain"))
            ch(pool.memset(ident[:], 0.0))
            ch(pool.affine_select(out=ident[:], in_=ident[:], compare_op=ALU.not_equal, fill=1.0, base=0,
                                  pattern=[[-1, P]], channel_multiplier=1))
            ch(pool.memset(ones_f[:], 1.0))
            ch(pool.memset(ones_b[:], 1.0))
            ch(pool.affine_select(out=before[:], in_=ones_b[:], compare_op=ALU.is_gt, fill=0.0, base=0,
                                  pattern=[[1, P]], channel_multiplier=-1))
            ch(pool.memset(upto[:], -1.0))
            ch(pool.affine_select(out=upto[:], in_=upto[:], compare_op=ALU.is_gt, fill=0.0, base=1,
                                  pattern=[[-1, P]], channel_multiplier=1))
            ch(pool.iota(iota_row[:], [[1, P]], base=0, channel_multiplier=0, allow_small_or_imprecise_dtypes=True))
            ch(pool.iota(iota_blk[:], [[1, NB]], base=0, channel_multiplier=0, allow_small_or_imprecise_dtypes=True))
            ch(pool.iota(iota_tile[:], [[1, TC]], base=0, channel_multiplier=0, allow_small_or_imprecise_dtypes=True))
            ch(pool.iota(node_id[:], [[P, NT]], base=0, channel_multiplier=1, allow_small_or_imprecise_dtypes=True))
            for low_m, E in ((lower0, E0), (lower1, E1)):
                ch(pool.memset(low_m[:], 1.0))
                ch(pool.affine_select(out=low_m[:], in_=low_m[:], compare_op=ALU.is_gt, fill=0.0, base=0,
                                      pattern=[[1, E], [-1, E]], channel_multiplier=0))
            pool.memset(eps[:], 1e-5).then_inc(s("consts"), 1)

            def scatter(key):
                k = RECORDS[key][0]

                def body(g, w, early):
                    pool.wait_ge(s(f"picked{w}"), fed_count(key, g, w, early))
                    for q in range(8):
                        slot, done = w * 8 + q, landed(key, g, w, early, q) - 16
                        if not early or done > 0:
                            pool.wait_ge(s(f"got{slot}"), done)
                        pool.sem_inc(s("pool_turn"), 1)
                        pool.indirect_dma_start(rec[k], bass.IndirectOffsetOnAxis(ap=rec_slot[:, w, q, 3:4].bitcast(I32), axis=0),
                                                rec_slot[:, w, q, :], None).then_inc(s(f"got{slot}"), 16)
                pool.wait_ge(s(f"pad_out_{k}"), 16)
                in_groups(pool, COUNT[key], body)
            scatter("b1")

            for u in range(2):
                pool.wait_ge(s(f"val_out{u}"), 16 * (NT // 2))
            pool.wait_ge(s("left_out"), 16)

            def gather_val(g, w, early):
                pool.wait_ge(s(f"picked{w}"), fed_count("val", g, w, early))
                for q in range(BIG_TILES):
                    slot = w * BIG_TILES + q
                    if not (early and g < 2):
                        pool.wait_ge(s("val_used"), g - 1)
                    else:
                        pool.wait_ge(s(f"got{slot}"), START["val"][slot])
                    pool.sem_inc(s("pool_turn"), 1)
                    pool.indirect_dma_start(got[:, slot, 0:D + HEADS], None, tab_val,
                                            bass.IndirectOffsetOnAxis(ap=pick_val[:, w, q, 0:1], axis=0)).then_inc(s(f"got{slot}"), 16)
                    pool.indirect_dma_start(left[:, w, q, :], None, tab_left,
                                            bass.IndirectOffsetOnAxis(ap=pick_val[:, w, q, 1:2], axis=0)).then_inc(s(f"got{slot}"), 16)
            in_groups(pool, GROUPS, gather_val)
            scatter("b2")

            pool.wait_ge(s("low_ready"), 1)
            pool.partition_all_reduce(low[:], nlow[:], P, RMAX).then_inc(s("low_all"), 1)
            scatter("c1")
            scatter("c2")

            def gathers(key, table, into, width, used):
                def body(g, w, early):
                    pool.wait_ge(s(f"picked{w}"), fed_count(key, g, w, early))
                    for q in range(8):
                        slot = w * 8 + q
                        if early and g < 2:
                            pool.wait_ge(s(f"got{slot}"), START[key][slot])
                        else:
                            for name, per in used:
                                pool.wait_ge(s(name), g * 2 + q // 4 - 3 if per == 4 else g * 8 + q - 15)
                        pool.sem_inc(s("pool_turn"), 1)
                        pool.indirect_dma_start(into[:, slot, 0:width], None, table,
                                                bass.IndirectOffsetOnAxis(ap=pick[:, w, q:q + 1], axis=0)).then_inc(s(f"got{slot}"), 16)
                in_groups(pool, COUNT[key], body)
            pool.wait_ge(s("val_used"), GROUPS)
            pool.wait_ge(s("src_out"), 16)
            gathers("src", tab_src, terms, SC + SH, [("src_kept", 4), ("src_shifted", 4)])
            pool.wait_ge(s("src_kept"), TB // 4)
            pool.wait_ge(s("src_shifted"), TB // 4)
            scatter("c3")
            for u in range(2):
                pool.wait_ge(s(f"rel_out{u}"), 64 * (NT // 2))
            gathers("rel", tab_rel, rel_rows, D, [("rel_spread", 1)])

            pool.wait_ge(s("tok_zeroed"), 32)

            def put(i, first):
                for a in range(BIG_TILES):
                    pool.wait_ge(s("tok_ready"), i * BIG_TILES + a + 1)
                    pool.sem_inc(s("pool_turn"), 1)
                    for c in range(2):
                        pool.indirect_dma_start(tok_in, bass.IndirectOffsetOnAxis(ap=pick_tok[:, a, c:c + 1], axis=0),
                                                got[:, a, 0:D], None).then_inc(s(f"got{a}"), 16)
            with pool.Fori(0, GROUPS) as i:
                put(i, False)
            for u in range(2):
                pool.wait_ge(s(f"y_out{u}"), 16 * (MT // 2))

            def take(i, first):
                for a in range(BIG_TILES):
                    pool.wait_ge(s("take_ready"), i * BIG_TILES + a + 1)
                    pool.sem_inc(s("pool_turn"), 1)
                    for c in range(2):
                        pool.indirect_dma_start(got[:, 2 * a + c, 0:D], None, tok_out,
                                                bass.IndirectOffsetOnAxis(ap=pick_tok[:, a, c:c + 1], axis=0)).then_inc(s(f"got{a}"), 16)
            with pool.Fori(0, GROUPS) as i:
                take(i, False)

        @block.scalar
        def _(act):
            def settle():
                act.sem_inc(s("act_turn"), 1)

            act.wait_ge(s("consts"), 1)

            def std(k):
                act.wait_ge(s("asked"), ASKS[f"std_{k}"])
                act.activation(var[:], var[:], ACT.Sqrt, bias=eps[:, 0:1]).then_inc(s("answered"), 1)

            def copies(k, keep):
                def transposed(t, u, early):
                    act.wait_ge(s(f"tp_{k}"), t + 1)
                    if not early:
                        act.wait_ge(s("rel_mm" if k == "rel" else f"prod_{k}"), (t - 1) * 4 if k == "rel" else t - 1)
                    settle()
                    v = ps[u][:, 0:D].rearrange("p (k n) -> p k n", k=KT)
                    if keep:
                        act.copy(XT[:, :, bass.ds(t * P, P)], v)
                    act.copy(xTs[:, u, :, :], v).then_inc(s(f"xT_{k}"), 1)

                def results(t, u, early):
                    if k == "rel":
                        for q in (0, 2):
                            act.wait_ge(s("rel_mm"), t * 4 + q + 1)
                            if not early:
                                act.wait_ge(s(f"rel_out{u}"), 32 * (t - u))
                            settle()
                            act.copy(rel_out[q][:, u, :], ps[2 + q][:, :]).then_inc(s("rel_ready0"), 1)
                        return
                    act.wait_ge(s(f"prod_{k}"), t + 1)
                    if k == "val" and not early:
                        act.wait_ge(s(f"val_out{u}"), 8 * (t - u))
                    settle()
                    if k == "val":
                        act.copy(left_all[:, bass.ds(t, 1), :].rearrange("p a h -> p (a h)"), ps[2 + u][:, D + HEADS:D + 2 * HEADS]).then_inc(s("left_copied"), 1)
                    o = {"val": rows[:, u, :],
                         "score": nodes[:, bass.ds(t, 1), 0:SC].rearrange("p a c -> p (a c)"),
                         "gate": gates[:, bass.ds(t, 1), :].rearrange("p a c -> p (a c)")}[k]
                    act.copy(o, ps[2 + u][:, 0:D + HEADS if k == "val" else WIDTH[k]]).then_inc(s(f"{k}_copied"), 1)
                    if k == "val":
                        act.wait_ge(s("val_copied"), t + 1)
                        settle()
                        act.dma_start(tab_val[bass.ds(t * P, P), :], rows[:, u, 0:D + HEADS]).then_inc(s(f"val_out{u}"), 16)

                def both(i, first, last):
                    for u in range(2):
                        t = i * 2 + u
                        if not (last and u == 1):
                            transposed(t + 1, 1 - u, first and u == 0)
                        results(t, u, first)
                transposed(0, 0, True)
                both(0, True, False)
                with act.Fori(1, NT // 2 - 1) as i:
                    both(i, False, False)
                both(NT // 2 - 1, False, True)

            std("val")
            copies("val", False)
            act.wait_ge(s("left_copied"), NT)
            act.dma_start(tab_left.rearrange("(t p) h -> p t h", p=P), left_all[:]).then_inc(s("left_out"), 16)
            def exps(g, w, early):
                act.wait_ge(s("val_z"), g + 1)
                act.activation(share[:, w], share[:, w], ACT.Exp).then_inc(s("val_e"), 1)
            in_groups(act, GROUPS, exps)

            std("score")
            copies("score", True)

            def store_y(e, g, p):
                n = e * GROUPS + g
                act.wait_ge(s("y_room0"), (n + 1) * BIG_TILES + 4)
                settle()
                act.dma_start(tab_y[bass.ds(e, 1), bass.ds(g * GT, GT), :].rearrange("e (t p) d -> p (e t) d", p=P), y_stage[p]).then_inc(s(f"y_stored{p}"), 16)

            def hidden(e, u, g, p):
                n = e * GROUPS + g
                act.wait_ge(s("mm2_0"), (n + 1) * BIG_TILES)
                for f in range(F0):
                    for half in range(2):
                        act.wait_ge(s("mm1_0"), (n * F0 + f) * 2 + half + 1)
                        settle()
                        act.activation(hT[p][:, f, half * HALF:(half + 1) * HALF], ps[(f * 2 + half) % 4][:, 0:HALF],
                                       ACT.Gelu, bias=b1_0[:, bass.ds(e, 1), f]).then_inc(s("h_room0"), 1)

            def store_after(e, u, g, p):
                store_y(e, g, p)
            act.sem_inc(s("h_room0"), 4)
            for p in range(2):
                act.sem_inc(s(f"y_stored{p}"), 16)
            first_groups(act, store_after, hidden)

            act.wait_ge(s("sorted_in_b"), 16)

            def src_rows(g, w, early):
                for q in range(8):
                    j = g * 8 + q
                    r = q % 4
                    if r == 0:
                        act.wait_ge(s("src_shifted"), g * 2 + q // 4 + 1)
                    if not (early and g == 0 and q < 4):
                        act.wait_ge(s("spread"), j - 3)
                    settle()
                    for h in range(SH - r % 2):
                        act.activation(diag[:, r, h, :], ident[:], ACT.Copy, scale=shifted[:, q, h:h + 1]).then_inc(s("diag_ready"), 1)
                    if r == 3:
                        for q2 in range(q - 3, q + 1):
                            act.wait_ge(s(f"got{w * 8 + q2}"), landed("src", g, w, early, q2))
                        settle()
                        act.copy(edge1[:, bass.ds(j - 3, 4), :], terms[:, w * 8 + q - 3:w * 8 + q + 1, :]).then_inc(s("src_kept"), 1)
            in_groups(act, TB // 8, src_rows)

            act.wait_ge(s("asked"), ASKS["self_exp"])
            act.activation(small2[:], small2[:], ACT.Exp).then_inc(s("answered"), 1)
            def weigh(g, w):
                act.wait_ge(s("logits"), g + 1)
                act.activation(logit[:, w], logit[:, w], ACT.Exp).then_inc(s("weights"), 1)

            def copy_turned(g, w, early):
                if not (early and g == 0):
                    weigh(g - 1, 1 - w)
                for half in range(2):
                    act.wait_ge(s("turned_mm"), g * 2 + half + 1)
                    if not (early and g == 0):
                        act.wait_ge(s("looked_up"), g)
                    act.copy(turned[:, half * 4:half * 4 + 4, :], ps[half][:, :].rearrange("p (t l) -> p t l", t=4)).then_inc(s("turned_copied"), 1)
            in_groups(act, TB // 8, copy_turned)
            weigh(TB // 8 - 1, (TB // 8 - 1) % 2)
            act.wait_ge(s("asked"), ASKS["std_agg"])
            act.activation(gy[:], gy[:], ACT.Sqrt, bias=eps[:, 0:1]).then_inc(s("answered"), 1)
            act.wait_ge(s("asked"), ASKS["top_exp0"])
            act.activation(gates[:, :, 0:E0], gates[:, :, 0:E0], ACT.Exp).then_inc(s("answered"), 1)

            std("rel")
            copies("rel", False)

            std("gate")
            copies("gate", False)
            act.wait_ge(s("asked"), ASKS["top_exp1"])
            act.activation(gates[:, :, 0:E1], gates[:, :, 0:E1], ACT.Exp).then_inc(s("answered"), 1)

            def token_tile(j, u, first):
                act.wait_ge(s("tokT_mm"), j + 1)
                if not first:
                    act.wait_ge(s("mid_mm"), F1 * (j - 1))
                settle()
                act.copy(tokT[u], ps[0][:, :].rearrange("p (k n) -> p k n", k=KT)).then_inc(s("tokT_ready"), 1)

            def gelus(j, u, first):
                if not first:
                    act.wait_ge(s("y_mm"), (j - 1) * 2)
                for f in range(F1):
                    act.wait_ge(s("mid_mm"), F1 * j + f + 1)
                    settle()
                    act.activation(hid[u][:, f, :], ps[1 + f % 4][:, 0:MP], ACT.Gelu, bias=mb1[u][:, f:f + 1]).then_inc(s("gelu_done"), 1)

            token_tile(0, 0, True)
            gelus(0, 0, True)
            token_tile(1, 1, True)
            gelus(1, 1, True)
            with act.Fori(1, MT // 2) as i:
                for u in range(2):
                    token_tile(i * 2 + u, u, False)
                    gelus(i * 2 + u, u, False)

        @block.tensor
        def _(pe):
            pe.wait_ge(s("consts"), 1)
            def bucket_counts(k):
                C, T, w = NBUCK[k]
                ohv = parts[k][0]
                pe.wait_ge(s("hot_blocks"), NB if k == "b" else 2 * NB)

                def count(c, start, stop):
                    return pe.matmul(ps[7][:, 0:NB * w].rearrange("p (b c) -> p b c", c=w), ones_b[:], ohv[:, :, bass.ds(c * w, w)],
                                     start=start, stop=stop)
                count(0, True, False)
                with pe.Fori(1, C // w - 1) as c:
                    count(c, False, False)
                count(C // w - 1, False, True).then_inc(s("totals"), 1)

                base = 0 if k == "b" else NB

                def counts(n, u, first):
                    if u == 3 and first:
                        pe.wait_ge(s("totals_read"), 1 if k == "b" else 2)
                    if not (k == "b" and first):
                        pe.wait_ge(s("placed"), base + n - 3)
                    o = ohv[:, bass.ds(n, 1), :].rearrange("p a c -> p (a c)")
                    pe.matmul(ps[u][:, 0:C], ones_b[:], o, start=True, stop=True)
                    pe.matmul(ps[4 + u][:, 0:C], upto[:], o, start=True, stop=True).then_inc(s("block_sums"), 1)
                for u in range(4):
                    counts(u, u, True)
                with pe.Fori(1, NB // 4) as i:
                    for u in range(4):
                        counts(i * 4 + u, u, False)
                counts(NB - 1, 0, False)

            def tiles(k, weights):
                W = WIDTH[k]

                def transpose(t, u, early):
                    pe.wait_ge(s(f"xn_{k}"), t + 1)
                    if not early:
                        pe.wait_ge(s(f"xT_{k}"), t - 1)
                    pe.transpose(ps[u][:, 0:P], xn[:, u, 0:P], ident[:])
                    pe.transpose(ps[u][:, P:2 * P], xn[:, u, P:2 * P], ident[:]).then_inc(s(f"tp_{k}"), 1)

                def product(t, u, early, very_first):
                    pe.wait_ge(s(f"xT_{k}"), t + 1)
                    if k == "rel":
                        for q in range(4):
                            if not very_first:
                                pe.wait_ge(s(f"rel_ready{q % 2}"), (t - 1) * 2 + q // 2 + 1)
                            for kt in range(KT):
                                mm = pe.matmul(ps[2 + q][:, :], xTs[:, u, kt, :], wrel[:, kt, q * 512:(q + 1) * 512],
                                               start=(kt == 0), stop=(kt == KT - 1))
                            mm.then_inc(s("rel_mm"), 1)
                        return
                    if not early:
                        pe.wait_ge(s(f"{k}_copied"), t - 1)
                    for kt in range(KT):
                        mm = pe.matmul(ps[2 + u][:, 0:W], xTs[:, u, kt, :], weights[:, kt, :],
                                       start=(kt == 0), stop=(kt == KT - 1))
                    mm.then_inc(s(f"prod_{k}"), 1)

                def both(i, first, last):
                    for u in range(2):
                        t = i * 2 + u
                        if not (last and u == 1):
                            transpose(t + 1, 1 - u, first and u == 0)
                        product(t, u, first, first and u == 0)
                transpose(0, 0, True)
                both(0, True, False)
                with pe.Fori(1, NT // 2 - 1) as i:
                    both(i, False, False)
                both(NT // 2 - 1, False, True)

            bucket_counts("b")
            pe.wait_ge(s("params_in"), n_params)
            pe.wait_ge(s("attn_weights"), 1)
            pe.wait_ge(s("placed"), NB)
            tiles("val", wg_sb)
            pe.wait_ge(s("val_copied"), NT)
            bucket_counts("c")
            pe.wait_ge(s("placed"), 2 * NB)
            tiles("score", ws_sb)
            def mm1(e, u, g, p):
                n = e * GROUPS + g
                if isinstance(g, int) and g == 0:
                    pe.wait_ge(s(f"w_in0{u}"), (e - u) * 16 + 32)
                for f in range(F0):
                    for half in range(2):
                        pe.wait_ge(s("h_room0"), (n * F0 + f) * 2 + half + 1)
                        pe.sem_inc(s("pe_turn"), 1)
                        for kt in range(KT):
                            mm = pe.matmul(ps[(f * 2 + half) % 4][:, 0:HALF], w1v[0][u][:, kt, f * P:(f + 1) * P],
                                           XT[:, kt, bass.ds(g * GT + half * HALF, HALF)],
                                           start=(kt == 0), stop=(kt == KT - 1))
                        mm.then_inc(s("mm1_0"), 1)

            def mm2(e, u, g, p):
                n = e * GROUPS + g
                pe.wait_ge(s("h_room0"), (n + 1) * F0 * 2 + 4)
                for a in range(BIG_TILES):
                    pe.wait_ge(s("y_room0"), n * BIG_TILES + a + (4 if a == 0 else 1 if a == 4 else 0))
                    for f in range(F0):
                        mm = pe.matmul(ps[4 + a % 4][:, 0:D], hT[p][:, f, a * P:(a + 1) * P], w2v[0][u][:, f, :],
                                       start=(f == 0), stop=(f == F0 - 1))
                    mm.then_inc(s("mm2_0"), 1)
            pe.sem_inc(s("mm2_0"), MM2_CREDIT)
            pe.wait_ge(s("score_copied"), NT)
            first_groups(pe, mm2, mm1)

            def spread(i, first):
                for q in range(4):
                    j = i * 4 + q
                    pe.wait_ge(s("hot_b"), j + 1)
                    pe.wait_ge(s("diag_ready"), squares(i, q))
                    if q % 2:
                        pe.wait_ge(s("diag_last"), i * 2 + q // 2 + 1)
                    if not first:
                        pe.wait_ge(s("spread_used"), j - 3)
                    pe.matmul(ps[q][:, :], hot[:, q, :], diag[:, q, :, :].rearrange("p h e -> p (h e)"), start=True, stop=True).then_inc(s("spread"), 1)
            pe.wait_ge(s("y_room0"), E0 * NB + 4)
            spread(0, True)
            with pe.Fori(1, TB // 4) as i:
                spread(i, False)

            def turn(g, w, early):
                for q in range(8):
                    pe.wait_ge(s("hot_msg"), g * 8 + q + 1)
                    if not (early and g == 0) and q % 4 == 0:
                        pe.wait_ge(s("turned_copied"), (g - 1) * 2 + q // 4 + 1)
                    mm = pe.matmul(ps[q // 4][:, q % 4 * P:(q % 4 + 1) * P], hots[:, w, q, :], ident_b[:], start=True, stop=True)
                    if q % 4 == 3:
                        mm.then_inc(s("turned_mm"), 1)

            def blocks_of_group(g):
                _, values = nc.values_load_multi_w_load_instructions(tile_blk_b[0:1, bass.ds(g * 8, 8)], engines=(mybir.EngineType.PE,),
                                                                     min_val=0, max_val=NB - 1,
                                                                     skip_runtime_bounds_check_because="the table's blocks are at most NB - 1")
                return values

            def look_up(g, w, early, blocks):
                for q in range(8):
                    if q % 4 == 0:
                        pe.wait_ge(s("turned_copied"), g * 2 + q // 4 + 1)
                        if not (early and g == 0):
                            pe.wait_ge(s("found_read"), g)
                        pe.sem_inc(s("pe_turn"), 1)
                    mm = pe.matmul(ps[2][:, q * 6 * SH:(q + 1) * 6 * SH], turned[:, q, :],
                                   adm_parts[:, bass.ds(blocks[q], 1), :, :].rearrange("p a k c -> p (a k c)"), start=True, stop=True)
                mm.then_inc(s("looked_up"), 1)

            W3 = 3 * (SC + SH)

            def msg_sums(g, w, early):
                blocks = blocks_of_group(g)
                pe.wait_ge(s("messages"), g + 1)
                pe.sem_inc(s("pe_turn"), 1)
                for q in range(8):
                    mm = pe.matmul(msg_acc[:, bass.ds(blocks[q] * MSG_W, W3)], hots[:, w, q, :], msg_parts[:, w, q].rearrange("p k c -> p (k c)"), start=False, stop=False)
                mm.then_inc(s("msg_spread"), 1)

            def msg_group(g, w, early):
                if not (early and g < 2):
                    msg_sums(g - 2, w, early and g == 2)
                blocks = blocks_of_group(g)
                turn(g, w, early)
                look_up(g, w, early, blocks)
            pe.wait_ge(s("spread_used"), TB)
            pe.wait_ge(s("maxima_ready"), 1)
            zeros_b = bz[:].bitcast(BF16)[:, 0:512]
            for bank in range(3, 7):
                pe.matmul(ps[bank], ident_b[:], zeros_b, start=True, stop=False)
            in_groups(pe, TB // 8, msg_group)
            for g in range(TB // 8 - 2, TB // 8):
                msg_sums(g, g % 2, False)
            for bank in range(3, 7):
                mm = pe.matmul(ps[bank], ident_b[:], zeros_b, start=False, stop=True)
            mm.then_inc(s("msg_closed"), 1)

            def rel_sums(g, w, early):
                first = early and g == 0
                for q in range(8):
                    j = g * 8 + q
                    pe.wait_ge(s("hot_rel"), j + 1)
                    if not (first and q < 4):
                        pe.wait_ge(s("rel_added"), j - 3)
                    pe.wait_ge(s(f"got{w * 8 + q}"), landed("rel", g, w, early, q))
                    pe.matmul(ps[q % 4][:, 0:D], hot[:, q % 4, :], rel_rows[:, w * 8 + q, :], start=True, stop=True).then_inc(s("rel_spread"), 1)

            pe.wait_ge(s("wrel_in"), 32)
            tiles("rel", None)
            in_groups(pe, TC // 8, rel_sums)
            tiles("gate", wgate_sb)
            pe.wait_ge(s("chosen_ready"), 1)
            cv = chosen_b[:].rearrange("p t e -> p (t e)")
            pe.matmul(ps[0][:, 0:NT * E1], ones_b[:], cv, start=True, stop=True)
            pe.matmul(ps[1][:, 0:NT * E1], before[:], cv, start=True, stop=True).then_inc(s("token_counts"), 1)

            def turn_tokens(j, u, first):
                pe.wait_ge(s(f"tokens_in{u}"), (j - u) * 8 + 16)
                if not first:
                    pe.wait_ge(s("tokT_ready"), j)
                for b in range(2):
                    for k in range(KT):
                        mm = pe.transpose(ps[0][:, k * MP + b * P:k * MP + (b + 1) * P], tok[u][:, b, k * P:(k + 1) * P], ident[:])
                mm.then_inc(s("tokT_mm"), 1)

            def middle(j, u, first):
                pe.wait_ge(s("tokT_ready"), j + 1)
                pe.wait_ge(s(f"w1_in{u}"), (j - u) * 16 + 32)
                for f in range(F1):
                    if not (first and f < 4):
                        pe.wait_ge(s("gelu_done"), F1 * j + f - 3)
                    for k in range(KT):
                        mm = pe.matmul(ps[1 + f % 4][:, 0:MP], w1v[1][u][:, k, f * P:(f + 1) * P], tokT[u][:, k, :], start=(k == 0), stop=(k == KT - 1))
                    mm.then_inc(s("mid_mm"), 1)

            def last(j, u, first):
                pe.wait_ge(s(f"w2_in{u}"), (j - u) * 16 + 32)
                for b in range(2):
                    if not first:
                        pe.wait_ge(s("y_copied"), j * 2 + b - 1)
                    y = ps[5 + b][:, 0:D]
                    for f in range(F1):
                        if b == 0:
                            pe.wait_ge(s("gelu_done"), F1 * j + f + 1)
                        mm = pe.matmul(y, hid[u][:, f, b * P:(b + 1) * P], w2v[1][u][:, f, :], start=(f == 0), stop=(f == F1 - 1))
                    mm.then_inc(s("y_mm"), 1)

            pe.wait_ge(s("places_known"), 1)
            turn_tokens(0, 0, True)
            middle(0, 0, True)
            turn_tokens(1, 1, False)
            last(0, 0, True)
            with pe.Fori(0, MT // 2 - 1) as i:
                for u in (1, 0):
                    j = i * 2 + 2 - u
                    middle(j, u, False)
                    turn_tokens(j + 1, 1 - u, False)
                    last(j, u, False)
            middle(MT - 1, 1, False)
            last(MT - 1, 1, False)

        @block.vector
        def _(dve):
            ch = Chain(dve, s("dve_chain"))
            tt, tsc, red = dve.tensor_tensor, dve.tensor_scalar, dve.tensor_reduce

            ch(dve.memset(X[:, FULL:NT, :], 0.0))
            ch(dve.memset(ends[:], 0))
            for a in parts["c"][3:6]:
                ch(dve.memset(a, 0))
            ch(dve.memset(parts["c"][7], 0.0))
            dve.sem_inc(s("x_zeroed"), 1)
            ch(dve.memset(bz[:], 0.0))
            dve.sem_inc(s("zeros"), 1)
            for k in "bc":
                ch(dve.memset(srt[k][:], 0.0))
                ch(dve.memset(srt[k][:, :, 1:2], -1.0))
                dve.sem_inc(s(f"edges_zeroed_{k}"), 1)
            dve.wait_ge(s("consts"), 1)
            ch(tsc(here[:], node_id[:], float(N), None, ALU.is_lt))
            def bucket_places(k):
                C, T, w = NBUCK[k]
                ohv, cnt, pk, di, si, ti, addr, wi = parts[k]
                base = 0 if k == "b" else NB
                dve.wait_ge(s(f"edges_in_{k}"), 32 if k == "b" else 128)
                ch(tsc(addr, di, LANE_MASK, None, ALU.bitwise_and))
                ch(dve.tensor_copy(pk[:, :, 1], addr))
                ch(tsc(addr, di, BLOCK_BITS, None, ALU.arith_shift_right))
                ch(dve.tensor_copy(bh[:, 0:C], addr))
                if k == "b":
                    ch(dve.tensor_copy(pk[:, :, 0], si))
                    ch(dve.tensor_copy(pk[:, :, 2], di))
                else:
                    ch(dve.scalar_tensor_tensor(out=pk[:, :, 0], in0=si, scalar=float(R), in1=ti, op0=ALU.mult, op1=ALU.add))
                    ch(dve.tensor_copy(pk[:, :, 2], wi))
                with dve.Fori(0, GROUPS) as g:
                    for q in range(BIG_TILES):
                        b = g * BIG_TILES + q
                        tsc(ohv[:, bass.ds(b, 1), :].rearrange("p a c -> p (a c)"), bh[:, 0:C], iota_blk[:, bass.ds(b, 1)], None,
                            ALU.is_equal).then_inc(s("hot_blocks"), 1)
                dve.wait_ge(s("totals"), 1 if k == "b" else 2)
                ch(red(bnum[:], ps[7][:, 0:NB * w].rearrange("p (b c) -> p b c", c=w), AX.X, ALU.add))
                dve.sem_inc(s("totals_read"), 1)
                ch(tsc(bint[:], bnum[:], float(P - 1), None, ALU.add))
                ch(tsc(bint[:], bint[:], BLOCK_BITS, None, ALU.arith_shift_right))
                ch(dve.tensor_copy(bnt[:], bint[:]))
                ch(dve.tensor_tensor_scan(block_end[k][:], bnt[:], bz[:, 0:NB], 0.0, ALU.add, ALU.add))
                ch(tt(bnt[:], block_end[k][:], bnt[:], ALU.subtract))
                ch(tsc(badj[:], bnt[:], float(P), None, ALU.mult))

                def scan(n, u, first):
                    dve.wait_ge(s("block_sums"), base + n + 1)
                    if not first:
                        dve.wait_ge(s("placed"), base + n - 3)
                    dve.tensor_tensor_scan(chunk[:, u, 0:C], ps[u][:, 0:C], bz[:, 0:C], 0.0, ALU.add, ALU.add).then_inc(s("scanned"), 1)

                def settle_place(n, u):
                    dve.wait_ge(s("scanned"), base + n + 1)
                    dve.scalar_tensor_tensor(out=cnt[:, bass.ds(n, 1), :].rearrange("p a c -> p (a c)"), in0=chunk[:, u, 0:C],
                                             scalar=badj[:, bass.ds(n, 1)], in1=ps[4 + u][:, 0:C], op0=ALU.add, op1=ALU.add).then_inc(s("placed"), 1)

                def four(i, first):
                    for u in range(4):
                        settle_place(i * 4 + u, u)
                        scan(i * 4 + u + 2, (u + 2) % 4, first and u < 2)
                scan(0, 0, True)
                scan(1, 1, True)
                four(0, True)
                with dve.Fori(1, NB // 4 - 1) as i:
                    four(i, False)
                for n in range(NB - 5, NB):
                    settle_place(n, n % 4)
                    if n + 2 < NB:
                        scan(n + 2, (n + 2) % 4, False)
                dve.wait_ge(s("placed"), base + NB)
                ch(tt(cnt, cnt, ohv, ALU.mult))
                pos = chunk[:, 0, 0:C]
                ch(red(pos, cnt.rearrange("p b c -> p c b"), AX.X, ALU.add))
                ch(dve.tensor_copy(di, pos))
                ch(tsc(addr, di, BLOCK_BITS, None, ALU.arith_shift_right))
                ch(tsc(di, di, LANE_MASK, None, ALU.bitwise_and))
                ch(dve.scalar_tensor_tensor(out=addr, in0=di, scalar=float(T), in1=addr, op0=ALU.mult, op1=ALU.add))
                dve.sem_inc(s("places"), 1)

            def tile_blocks(k):
                T = NBUCK[k][1]
                blk_i = tile_blk_b if k == "b" else tile_blk_c
                blk_f = bf2[0:1, 0:T]
                ch(dve.memset(blk_f, 0.0))
                for b in range(NB):
                    ch(dve.scalar_tensor_tensor(out=blk_f, in0=iota_tile[0:1, 0:T], scalar=block_end[k][0:1, b:b + 1], in1=blk_f,
                                                op0=ALU.is_ge, op1=ALU.add))
                ch(tsc(blk_i[:], blk_f, float(NB - 1), None, ALU.min))

            bucket_places("b")

            def tile_stats(n):
                dve.bn_stats(stats[:, bass.ds(n, 1), :].rearrange("p a c -> p (a c)"),
                             X[:, bass.ds(n, 1), :].rearrange("p a c -> p (a c)")).then_inc(s("stats_done"), 1)

            def layer_norm(k):
                S["ln"] = S.get("ln", 0) + NT
                with dve.Fori(0, GROUPS) as i:
                    for q in range(BIG_TILES):
                        tile_stats(i * BIG_TILES + q)
                for n in range(NB, NT):
                    tile_stats(n)
                dve.wait_ge(s("stats_done"), S["ln"])
                me, mo, ve, vo = (stats[:, :, c] for c in (1, 4, 2, 5))
                ch(tt(mean[:], me, mo, ALU.add))
                ch(tsc(mean[:], mean[:], 0.5, None, ALU.mult))
                ch(tt(tmpn[:], me, mo, ALU.subtract))
                ch(tt(tmpn[:], tmpn[:], tmpn[:], ALU.mult))
                ch(tt(var[:], ve, vo, ALU.add))
                ch(tsc(var[:], var[:], 1.0 / D, None, ALU.mult))
                dve.scalar_tensor_tensor(out=var[:], in0=tmpn[:], scalar=0.25, in1=var[:], op0=ALU.mult, op1=ALU.add).then_inc(s("asked"), 1)
                dve.wait_ge(s("answered"), ASKS[f"std_{k}"])
                ch(dve.reciprocal(rstd[:], var[:]))

                def norm(t, u, early):
                    if not early:
                        dve.wait_ge(s(f"tp_{k}"), t - 1)
                    tsc(xn[:, u, :], X[:, bass.ds(t, 1), :].rearrange("p a c -> p (a c)"), mean[:, bass.ds(t, 1)], rstd[:, bass.ds(t, 1)],
                        ALU.subtract, ALU.mult).then_inc(s(f"xn_{k}"), 1)

                def rel_results(t, u, early):
                    for q in (1, 3):
                        dve.wait_ge(s("rel_mm"), t * 4 + q + 1)
                        if not early:
                            dve.wait_ge(s(f"rel_out{u}"), 32 * (t - u))
                        dve.sem_inc(s("dve_turn"), 1)
                        dve.tensor_copy(rel_out[q][:, u, :], ps[2 + q][:, :]).then_inc(s("rel_ready1"), 1)

                def both(i, first, last):
                    for u in range(2):
                        if not last:
                            norm(i * 2 + u + 2, u, False)
                        if k == "rel":
                            rel_results(i * 2 + u, u, first)
                norm(0, 0, True)
                norm(1, 1, True)
                both(0, True, False)
                with dve.Fori(1, NT // 2 - 1) as i:
                    both(i, False, False)
                both(NT // 2 - 1, False, True)

            dve.wait_ge(s("x_in"), 32)
            dve.wait_ge(s("params_in"), n_params)
            for c, a in ((D, ar_b), (D + HEADS, al_b)):
                for k2 in range(KT):
                    ch(tt(prod[:, 0:D], wg_sb[:, k2, 0:D], a[:], ALU.mult))
                    ch(red(wg_sb[:, k2, c:c + HEADS], prod[:, 0:D].rearrange("p (h d) -> p h d", h=HEADS), AX.X, ALU.add))
            dve.sem_inc(s("attn_weights"), 1)
            layer_norm("val")

            bucket_places("c")

            base = ch.n
            K = 10

            def mix(g, w, early):
                c = Chain(dve, s("dve_chain"))
                c.n = g * K + base
                for q in range(BIG_TILES):
                    dve.wait_ge(s(f"got{w * BIG_TILES + q}"), landed("val", g, w, early, q))
                z, m = share[:, w], share_of[:, w]
                mb = m.unsqueeze(2).to_broadcast([P, BIG_TILES, HEADS])
                v = got[:, w * BIG_TILES:(w + 1) * BIG_TILES, 0:D]
                c(tt(z, left[:, w], got[:, w * BIG_TILES:(w + 1) * BIG_TILES, D:D + HEADS], ALU.add))
                c(dve.scalar_tensor_tensor(out=z, in0=z, scalar=0.01, in1=z, op0=ALU.mult, op1=ALU.max))
                c(red(m, z, AX.X, ALU.max))
                c(tt(z, z, mb, ALU.subtract))
                dve.sem_inc(s("val_z"), 1)
                dve.wait_ge(s("val_e"), g + 1)
                c(red(m, z, AX.X, ALU.add))
                c(dve.reciprocal(m, m))
                c(tt(z, z, mb, ALU.mult))
                pv = prod[:].rearrange("p (t h d) -> p t h d", t=BIG_TILES, h=HEADS)
                c(tt(pv, v.rearrange("p t (h d) -> p t h d", h=HEADS), z.unsqueeze(3).to_broadcast([P, BIG_TILES, HEADS, HD]), ALU.mult))
                c(red(mixed_v[:], pv.rearrange("p t h d -> p t d h"), AX.X, ALU.add))
                xv = X[:, bass.ds(g * BIG_TILES, BIG_TILES), :].rearrange("p t (h d) -> p t h d", h=HEADS)
                c(tt(xv, xv, mixed_v[:].unsqueeze(2).to_broadcast([P, BIG_TILES, HEADS, HD]), ALU.add))
                dve.sem_inc(s("val_used"), 1)
            in_groups(dve, GROUPS, mix)
            ch.n = base + K * GROUPS

            layer_norm("score")
            dve.wait_ge(s("score_copied"), NT)
            fe = nodes[:, :, 0:SC]
            big = term_prods
            for o, a in ((nodes[:, :, SC:SC + SH], asrc_b), (adm[:, :, 0:SH], adst_b)):
                ch(tt(big, fe, a[:].unsqueeze(1).to_broadcast([P, NT, SC]), ALU.mult))
                ch(red(o.rearrange("p t h -> p t h"), big.rearrange("p t (h e) -> p t h e", e=E0), AX.X, ALU.add))
            dve.sem_inc(s("nodes_ready"), 1)
            ch(tsc(gx[:, :, 0:SH], nodes[:, :, SC:SC + SH], -1.0, None, ALU.mult))
            red(nlow[:], gx[:, :, 0:SH].rearrange("p t h -> p h t"), AX.X, ALU.max).then_inc(s("low_ready"), 1)
            dve.sem_inc(s("y_room0"), 4)

            def results(e, u, g, p):
                n = e * GROUPS + g
                for a in range(BIG_TILES):
                    dve.wait_ge(s("mm2_0"), n * BIG_TILES + a + 1 + MM2_CREDIT)
                    if a == 0:
                        dve.wait_ge(s(f"y_stored{p}"), (n - p) * 8 + 16)
                    dve.sem_inc(s("dve_turn"), 1)
                    tt(y_stage[p][:, a, :], ps[4 + a % 4][:, 0:D], b2_0[:, bass.ds(e, 1), :].rearrange("p a c -> p (a c)"), ALU.add).then_inc(s("y_room0"), 1)
            first_groups(dve, results)
            dve.wait_ge(s("low_all"), 1)
            ch(tsc(low[:], low[:], 1.0, None, ALU.add))
            mxb = adm[:, :, SH:2 * SH]
            ch(dve.memset(mxb, 0.0))
            base = ch.n
            dve.wait_ge(s("sorted_in_b"), 16)

            ch(dve.tensor_copy(index_src[:], sorted_b[:, :, 0]))
            dve.sem_inc(s("index_ready"), 1)
            tile_blocks("b")
            base = ch.n

            def hot_tile(rec_sb, j, r, key, weighted):
                tsc(hot[:, r, :], ps[7][:, 0:P], rec_sb[:, bass.ds(j, 1), 1], rec_sb[:, bass.ds(j, 1), 2] if weighted else None,
                    ALU.is_equal, *([ALU.mult] if weighted else [])).then_inc(s(key), 1)

            def blocks_of(blk, j, n=4):
                _, values = nc.values_load_multi_w_load_instructions(blk[0:1, bass.ds(j, n)], engines=(mybir.EngineType.DVE,),
                                                                     min_val=0, max_val=NB - 1,
                                                                     skip_runtime_bounds_check_because="the table's blocks are at most NB - 1")
                return values

            lift = low[:].unsqueeze(1).to_broadcast([P, 4, SH])

            def shift(g, w, early, half):
                n = g * 2 + half
                for q in range(half * 4, half * 4 + 4):
                    dve.wait_ge(s(f"got{w * 8 + q}"), landed("src", g, w, early, q))
                if not (early and g == 0):
                    dve.wait_ge(s("diag_ready"), squares(n - 1, -1))
                    dve.wait_ge(s("diag_last"), (n - 1) * 2)
                at = w * 8 + half * 4
                tt(shifted[:, half * 4:half * 4 + 4, :], terms[:, at:at + 4, SC:SC + SH], lift, ALU.add).then_inc(s("src_shifted"), 1)

            def reduce_tile(j, r):
                dve.wait_ge(s("spread"), j + 1)
                red(tile_max[:, r, :], ps[r][:, :].rearrange("p (h e) -> p h e", h=SH), AX.X, ALU.max).then_inc(s("spread_used"), 1)

            def keep_max(j, r, first, block):
                dve.wait_ge(s("spread_used"), j + 1)
                if not first:
                    dve.wait_ge(s("max_kept"), j)
                mb = mxb[:, bass.ds(block, 1), :].rearrange("p a c -> p (a c)")
                tt(mb, mb, tile_max[:, r, :], ALU.max).then_inc(s("max_kept"), 1)

            def maxima(g, w, early, last=False):
                first = early and g == 0
                for q in range(8):
                    j = g * 8 + q
                    if q == 4 and not last:
                        shift(g + 1, 1 - w, early and g < 2, 0)
                    if q == 0:
                        shift(g, w, early, 1)
                    if q % 4 == 0 and not (first and q < 4):
                        blocks = blocks_of(tile_blk_b, j - 4)
                    if not (first and q < 4):
                        dve.wait_ge(s("spread"), j - 3)
                    hot_tile(sorted_b, j, q % 4, "hot_b", False)
                    if q % 2:
                        if q % 4 == 1:
                            dve.wait_ge(s("src_shifted"), g * 2 + q // 4 + 1)
                        tsc(diag[:, q % 4, SH - 1, :], ps[6][:, 0:P], shifted[:, q, SH - 1:SH], None, ALU.mult).then_inc(s("diag_last"), 1)
                    if not (first and q < 3):
                        reduce_tile(j - 3, (q - 3) % 4)
                    if not (first and q < 4):
                        keep_max(j - 4, q % 4, first and q == 4, blocks[q % 4])
            ch(dve.tensor_copy(ps[7][:, 0:P], iota_row[:]))
            ch(dve.tensor_copy(ps[6][:, 0:P], ident[:]))
            shift(0, 0, True, 0)
            in_groups(dve, TB // 8 - 1, maxima)
            maxima(TB // 8 - 1, 0, False, True)
            blocks = blocks_of(tile_blk_b, TB - 4)
            for j in range(TB - 4, TB):
                if j + 1 < TB:
                    reduce_tile(j + 1, (j + 1) % 4)
                keep_max(j, j % 4, False, blocks[j % 4])
            dve.wait_ge(s("max_kept"), TB)

            lowb = low[:].unsqueeze(1).to_broadcast([P, NT, SH])
            sv, dv = nodes[:, :, SC:SC + SH], adm[:, :, 0:SH]
            ch(tt(mxb, mxb, lowb, ALU.subtract))
            ch(tt(mxb, mxb, sv, ALU.max))
            ch(tt(mxb, mxb, dv, ALU.add))
            ch(dve.scalar_tensor_tensor(out=mxb, in0=mxb, scalar=0.2, in1=mxb, op0=ALU.mult, op1=ALU.max))
            ch(dve.tensor_copy(ident_b[:], ident[:]))
            rest = agg_b[:, :, 0:2 * SH]
            ch(dve.tensor_copy(rest, adm[:]))
            for k in range(3):
                ch(dve.tensor_copy(adm_parts[:, :, k, :], rest))
                if k < 2:
                    ch(tt(rest, rest, adm_parts[:, :, k, :], ALU.subtract))
            dve.sem_inc(s("maxima_ready"), 1)
            ch(tt(small2[:], sv, dv, ALU.add))
            ch(dve.scalar_tensor_tensor(out=small2[:], in0=small2[:], scalar=0.2, in1=small2[:], op0=ALU.mult, op1=ALU.max))
            ch(tt(small2[:], small2[:], mxb, ALU.subtract))
            dve.sem_inc(s("asked"), 1)
            dve.wait_ge(s("answered"), ASKS["self_exp"])
            ch(dve.tensor_copy(agg_b[:, :, SC:SC + SH], small2[:]))

            def heads(v):
                return v.rearrange("p t (h e) -> p t h e", e=E0)

            ch(tt(heads(agg_b[:, :, 0:SC]), heads(fe), small2[:].unsqueeze(3).to_broadcast([P, NT, SH, E0]), ALU.mult))
            def add_tile(key, acc, W, j, r, first, block):
                dve.wait_ge(s(f"{key}_spread"), j + 1)
                if not first:
                    dve.wait_ge(s(f"{key}_added"), j)
                av = acc[:, bass.ds(block, 1), :].rearrange("p a c -> p (a c)")
                tt(av, av, ps[r][:, 0:W], ALU.add).then_inc(s(f"{key}_added"), 1)

            MSG_STEPS = 4 + 2 + 5

            def logits(g, w, early):
                dve.wait_ge(s("looked_up"), g + 1)
                n = g * MSG_STEPS
                z = logit[:, w]
                red(found[:], ps[2][:, 0:48 * SH].rearrange("p (t k c) -> p t c k", t=8, k=3), AX.X, ALU.add).then_inc(s("msg_steps"), 1)
                dve.wait_ge(s("msg_steps"), n + 1)
                dve.sem_inc(s("found_read"), 1)
                tt(z, found[:, :, 0:SH], edge1[:, bass.ds(g * 8, 8), SC:SC + SH], ALU.add).then_inc(s("msg_steps"), 1)
                dve.wait_ge(s("msg_steps"), n + 2)
                dve.scalar_tensor_tensor(out=z, in0=z, scalar=0.2, in1=z, op0=ALU.mult, op1=ALU.max).then_inc(s("msg_steps"), 1)
                dve.wait_ge(s("msg_steps"), n + 3)
                tt(z, z, found[:, :, SH:2 * SH], ALU.subtract).then_inc(s("msg_steps"), 1)
                dve.wait_ge(s("msg_steps"), n + 4)
                dve.sem_inc(s("logits"), 1)

            def messages(g, w):
                dve.wait_ge(s("weights"), g + 1)
                z, n = logit[:, w], g * MSG_STEPS + 4
                e1v = edge1[:, bass.ds(g * 8, 8), 0:SC]
                tt(heads(message[:, :, 0:SC]), heads(e1v), z.unsqueeze(3).to_broadcast([P, 8, SH, E0]), ALU.mult).then_inc(s("msg_steps"), 1)
                dve.tensor_copy(message[:, :, SC:SC + SH], z).then_inc(s("msg_steps"), 1)
                n = n + 2
                for k in range(3):
                    dve.wait_ge(s("msg_steps"), n)
                    dve.tensor_copy(msg_parts[:, w, :, k, :], message[:]).then_inc(s("msg_steps"), 1)
                    dve.wait_ge(s("msg_steps"), n + 1)
                    if k < 2:
                        tt(message[:], message[:], msg_parts[:, w, :, k, :], ALU.subtract).then_inc(s("msg_steps"), 1)
                    n = n + 2
                dve.sem_inc(s("messages"), 1)

            def msg_group(g, w, early):
                if not (early and g == 0):
                    logits(g - 1, 1 - w, early)
                if not (early and g < 2):
                    dve.wait_ge(s("msg_spread"), g - 1)
                for q in range(8):
                    tsc(hots[:, w, q, :], ps[7][:, 0:P], sorted_b[:, bass.ds(g * 8 + q, 1), 1], None, ALU.is_equal).then_inc(s("hot_msg"), 1)
                if not (early and g == 0):
                    messages(g - 1, 1 - w)
            for p in range(2):
                dve.wait_ge(s(f"y_stored{p}"), 16 + 16 * E0 * GROUPS // 2)
            in_groups(dve, TB // 8, msg_group)
            last = TB // 8 - 1
            logits(last, last % 2, False)
            messages(last, last % 2)
            dve.wait_ge(s("msg_closed"), 1)
            msg_sum = y_stage[0].rearrange("p a b -> p (a b)")[:, 0:NT * (SC + SH)].rearrange("p (t c) -> p t c", t=NT)
            sums = msg_acc[:, 0:NT * MSG_W].rearrange("p (t w) -> p t w", w=MSG_W)[:, :, 0:3 * (SC + SH)].rearrange("p t (k c) -> p t c k", k=3)
            ch(red(msg_sum, sums, AX.X, ALU.add))
            ch(tt(agg_b, agg_b, msg_sum, ALU.add))

            den = agg_b[:, :, SC:SC + SH]
            ag = agg_b[:, :, 0:SC]

            def all_t(v):
                return v[:].unsqueeze(1).to_broadcast([P, NT, SC])

            def per_t(v):
                return v.unsqueeze(2).to_broadcast([P, NT, SC])
            ch(tsc(den, den, 1e-16, None, ALU.add))
            ch(dve.reciprocal(small2[:], den))
            ch(tt(heads(ag), heads(ag), small2[:].unsqueeze(3).to_broadcast([P, NT, SH, E0]), ALU.mult))
            ch(tt(ag, ag, all_t(bg_b), ALU.add))
            ch(red(gy[:], ag, AX.X, ALU.add))
            ch(tsc(gy[:], gy[:], 1.0 / SC, None, ALU.mult))
            ch(tt(ag, ag, per_t(gy[:]), ALU.subtract))
            ch(tt(fe, ag, ag, ALU.mult))
            ch(red(gy[:], fe, AX.X, ALU.add))
            ch(tsc(gy[:], gy[:], 1.0 / SC, None, ALU.mult))
            dve.sem_inc(s("asked"), 1)
            dve.wait_ge(s("answered"), ASKS["std_agg"])
            ch(dve.reciprocal(gy[:], gy[:]))
            ch(tt(ag, ag, per_t(gy[:]), ALU.mult))
            ch(tt(ag, ag, all_t(gamma_b), ALU.mult))
            ch(tt(ag, ag, all_t(beta_b), ALU.add))
            ch(red(gates[:, :, 0:E0], ag.rearrange("p t (h e) -> p t e h", e=E0), AX.X, ALU.add))
            ch(tsc(gates[:, :, 0:E0], gates[:, :, 0:E0], 1.0 / SH, None, ALU.mult))

            def top2(m, E, lower):
                g, r = gates[:, :, 0:E], gx[:, :, 0:E]
                pair = (pairs if m else pairs_0).rearrange("p t (i j) -> p t i j", i=E)
                pair2 = (pairs2 if m else pairs2_0).rearrange("p t (i j) -> p t i j", i=E)
                gi = g.unsqueeze(3).to_broadcast([P, NT, E, E])
                gj = g.unsqueeze(2).to_broadcast([P, NT, E, E])
                ch(tt(pair, gj, gi, ALU.is_equal))
                ch(tt(pair, pair, lower[:].unsqueeze(1).to_broadcast([P, NT, E, E]), ALU.mult))
                ch(tt(pair2, gj, gi, ALU.is_gt))
                ch(tt(pair, pair, pair2, ALU.add))
                ch(red(r, pair, AX.X, ALU.add))
                if m == 1:
                    for c in range(2):
                        ch(tsc(ranked[:, :, c, :], r, float(c), None, ALU.is_equal))
                ch(tsc(r, r, 2.0, None, ALU.is_lt))
                ch(red(gy[:], g, AX.X, ALU.max))
                ch(tt(g, g, gy[:].unsqueeze(2).to_broadcast([P, NT, E]), ALU.subtract))
                dve.sem_inc(s("asked"), 1)
                dve.wait_ge(s("answered"), ASKS[f"top_exp{m}"])
                ch(tt(g, g, r, ALU.mult))
                ch(red(gy[:], g, AX.X, ALU.add))
                ch(dve.reciprocal(gy[:], gy[:]))
                ch(tt(g, g, gy[:].unsqueeze(2).to_broadcast([P, NT, E]), ALU.mult))
                dve.sem_inc(s(f"gates_ready{m}"), 1)

            top2(0, E0, lower0)
            dve.sem_inc(s("wrel_room"), 1)

            def add_experts(g, w, early):
                dve.wait_ge(s(f"y_in{w}"), 16 * E0 * (g // 2) + 16 * E0 if early else (g - w) * 8 * E0 + 16 * E0)
                for e in range(E0):
                    for a in range(BIG_TILES):
                        n = (g * E0 + e) * BIG_TILES + a
                        t = g * BIG_TILES + a
                        if e > 0:
                            dve.wait_ge(s("acc_done"), n - BIG_TILES + 1)
                        xv = X[:, bass.ds(t, 1), :].rearrange("p a c -> p (a c)")
                        dve.scalar_tensor_tensor(out=xv, in0=y_back[w][:, e * BIG_TILES + a, :], scalar=gates[:, bass.ds(t, 1), e],
                                                 in1=xv, op0=ALU.mult, op1=ALU.add).then_inc(s("acc_done"), 1)
            in_groups(dve, GROUPS, add_experts)
            dve.wait_ge(s("acc_done"), E0 * NB)

            layer_norm("rel")
            ch(dve.memset(agg_c, 0.0))
            tile_blocks("c")
            dve.wait_ge(s("sorted_in_c"), 16)
            ch(dve.tensor_copy(index_rel[:], sorted_c[:, :, 0]))
            dve.sem_inc(s("index_ready"), 1)

            def rel_tiles(i, first):
                for q in range(8):
                    j = i * 8 + q
                    if not (first and q < 4):
                        dve.wait_ge(s("rel_spread"), j - 3)
                    hot_tile(sorted_c, j, q % 4, "hot_rel", True)
                    if not (first and q < 4):
                        if q % 4 == 0:
                            blocks = blocks_of(tile_blk_c, j - 4)
                        add_tile("rel", agg_c, D, j - 4, q % 4, first and q == 4, blocks[q % 4])
            ch(dve.tensor_copy(ps[7][:, 0:P], iota_row[:]))
            rel_tiles(0, True)
            with dve.Fori(1, TC // 8) as i:
                rel_tiles(i, False)
            blocks = blocks_of(tile_blk_c, TC - 4)
            for j in range(TC - 4, TC):
                add_tile("rel", agg_c, D, j, j % 4, False, blocks[j % 4])
            dve.wait_ge(s("rel_added"), TC)
            ch(dve.scalar_tensor_tensor(out=X[:, 0:NT, :], in0=agg_c, scalar=0.0, in1=X[:, 0:NT, :], op0=ALU.max, op1=ALU.add))
            layer_norm("gate")
            dve.wait_ge(s("gate_copied"), NT)
            ch(tt(gates[:], gates[:], bgate_b[:].unsqueeze(1).to_broadcast([P, NT, E1]), ALU.add))
            top2(1, E1, lower1)
            g, r = gates[:, :, 0:E1], gx[:, :, 0:E1]
            ch(tt(r, r, here[:].unsqueeze(2).to_broadcast([P, NT, E1]), ALU.mult))
            ch(dve.tensor_copy(chosen_b[:], r))
            dve.sem_inc(s("chosen_ready"), 1)
            dve.wait_ge(s("token_counts"), 1)
            tot = ps[0][:, 0:NT * E1].rearrange("p (t e) -> p t e", e=E1)
            for e in range(E1):
                ch(dve.tensor_tensor_scan(chosen[:, :, e], tot[:, :, e], bz[:, 0:NT], 0.0, ALU.add, ALU.add))
            ch(tsc(bint[:, 0:E1], chosen[:, NT - 1, :], float(MP - 1), None, ALU.add))
            ch(tsc(bint[:, 0:E1], bint[:, 0:E1], BLOCK_BITS + 1, None, ALU.arith_shift_right))
            ch(dve.tensor_copy(bnt[:, 0:E1], bint[:, 0:E1]))
            ch(dve.tensor_tensor_scan(bend[:, 0:E1], bnt[:, 0:E1], bz[:, 0:E1], 0.0, ALU.add, ALU.add))
            ch(tt(bnt[:, 0:E1], bend[:, 0:E1], bnt[:, 0:E1], ALU.subtract))
            ch(tsc(bnt[:, 0:E1], bnt[:, 0:E1], float(MP), None, ALU.mult))
            ch(tt(chosen[:], chosen[:], tot, ALU.subtract))
            ch(tt(chosen[:], chosen[:], ps[1][:, 0:NT * E1].rearrange("p (t e) -> p t e", e=E1), ALU.add))
            ch(tt(chosen[:], chosen[:], bnt[:, 0:E1].unsqueeze(1).to_broadcast([P, NT, E1]), ALU.add))
            ch(tsc(away[:, 0:1], node_id[:, 0:1], float(MROWS), None, ALU.add))
            ch(tsc(away[:, 1:2], node_id[:, 0:1], float(MROWS + P), None, ALU.add))
            for c in range(2):
                ch(tt(pairs[:, :, 0:E1], ranked[:, :, c, :], g, ALU.mult))
                ch(red(gate2[:, :, c], pairs[:, :, 0:E1], AX.X, ALU.add))
                ch(tt(pairs[:, :, 0:E1], ranked[:, :, c, :], chosen[:], ALU.mult))
                ch(red(gy[:], pairs[:, :, 0:E1], AX.X, ALU.add))
                ch(tsc(gy[:], gy[:], away[:, c:c + 1], None, ALU.subtract))
                ch(tt(gy[:], gy[:], here[:], ALU.mult))
                ch(tsc(gy[:], gy[:], away[:, c:c + 1], None, ALU.add))
                ch(dve.tensor_copy(place[:, :, c], gy[:]))
            ch(dve.memset(bf2[0:1, 0:MT], 0.0))
            for e in range(E1):
                ch(dve.scalar_tensor_tensor(out=bf2[0:1, 0:MT], in0=iota_tile[0:1, 0:MT], scalar=bend[0:1, e:e + 1], in1=bf2[0:1, 0:MT],
                                            op0=ALU.is_ge, op1=ALU.add))
            ch(tsc(expert_of[:], bf2[0:1, 0:MT], float(E1 - 1), None, ALU.min))
            dve.sem_inc(s("places_known"), 1)
            dve.sem_inc(s("moe_room1"), 1)
            dve.wait_ge(s("rel_spread"), TC)

            def token_rows(i, first):
                for a in range(BIG_TILES):
                    t = i * BIG_TILES + a
                    if not first:
                        dve.wait_ge(s(f"got{a}"), START["put"][a] + 32 * i)
                    dve.tensor_copy(pick_tok[:, a, :], place[:, bass.ds(t, 1), :].rearrange("p a c -> p (a c)")).then_inc(s("tok_pick"), 1)
                    dve.wait_ge(s("tok_pick"), t + 1)
                    tsc(got[:, a, 0:D], X[:, bass.ds(t, 1), :].rearrange("p a c -> p (a c)"), mean[:, bass.ds(t, 1)], rstd[:, bass.ds(t, 1)],
                        ALU.subtract, ALU.mult).then_inc(s("tok_ready"), 1)
            token_rows(0, True)
            with dve.Fori(1, GROUPS) as i:
                token_rows(i, False)
            for a in range(BIG_TILES):
                dve.wait_ge(s(f"got{a}"), END["put"][a])

            def copy_y(j, u, early):
                for b in range(2):
                    dve.wait_ge(s("y_mm"), j * 2 + b + 1)
                    if not early and b == 0:
                        dve.wait_ge(s(f"y_out{u}"), 8 * (j - u))
                    dve.sem_inc(s("dve_turn"), 1)
                    tt(res[u][:, b, :], ps[5 + b][:, 0:D], mb2[u], ALU.add).then_inc(s("y_copied"), 1)
            copy_y(0, 0, True)
            copy_y(1, 1, True)
            with dve.Fori(1, MT // 2) as i:
                copy_y(i * 2, 0, False)
                copy_y(i * 2 + 1, 1, False)

            def take_pick(t, a):
                dve.tensor_copy(pick_tok[:, a, :], place[:, bass.ds(t, 1), :].rearrange("p a c -> p (a c)")).then_inc(s("take_ready"), 1)
            for a in range(BIG_TILES):
                take_pick(a, a)

            def mix_back(i, more):
                for a in range(BIG_TILES):
                    t = i * BIG_TILES + a
                    dve.wait_ge(s(f"got{a}"), START["take"][a] + 32 * i + 32)
                    xv = X[:, bass.ds(t, 1), :].rearrange("p a c -> p (a c)")
                    for c in range(2):
                        dve.scalar_tensor_tensor(out=xv, in0=got[:, 2 * a + c, 0:D], scalar=gate2[:, bass.ds(t, 1), c], in1=xv,
                                                 op0=ALU.mult, op1=ALU.add).then_inc(s("mixed"), 1)
                        dve.wait_ge(s("mixed"), t * 2 + c + 1)
                    if more:
                        take_pick(t + BIG_TILES, a)
            with dve.Fori(0, GROUPS - 1) as i:
                mix_back(i, True)
            mix_back(GROUPS - 1, False)


_INS = ['x', 'src', 'dst', 'edge_type_8', 'edge_weight', 'L0_gnn_weight', 'L0_gnn_attn_l', 'L0_gnn_attn_r', 'L0_ffn_W_gat',
        'L0_ffn_att_src', 'L0_ffn_att_dst', 'L0_ffn_b_gat', 'L0_ffn_ln_gamma', 'L0_ffn_ln_beta', 'L0_ffn_W1', 'L0_ffn_b1',
        'L0_ffn_W2', 'L0_ffn_b2', 'L0_ffn_edge_index', 'L1_gnn_weight', 'L1_ffn_Wg', 'L1_ffn_bg', 'L1_ffn_W1', 'L1_ffn_b1',
        'L1_ffn_W2', 'L1_ffn_b2']


def kernel(**inputs):
    import numpy as _np
    import concourse.bacc as _bacc
    from concourse import mybir as _mybir
    from concourse.bass_utils import run_bass_kernel_spmd as _run

    nc = _bacc.Bacc("TRN2", target_bir_lowering=False, num_devices=1)
    arrays, args = {}, []
    for name in _INS:
        a = _np.ascontiguousarray(inputs[name])
        arrays[f"in_{name}"] = a
        args.append(nc.dram_tensor(f"in_{name}", a.shape, _mybir.dt.from_np(a.dtype), kind="ExternalInput").ap())
    args.append(nc.dram_tensor("out_0", inputs['x'].shape, _mybir.dt.float32, kind="ExternalOutput").ap())
    graph_layers(nc, *args)
    r = _run(nc, [arrays], core_ids=[0])
    return r.results[0]["out_0"]
```
